# Optimizing a Trainium2 kernel written in Bass

```python
import numpy as np
import jax
import jax.numpy as jnp

def _softmax(x, axis=-1):
    return jax.nn.softmax(x, axis=axis)

def _gelu(x):
    return jax.nn.gelu(x, approximate=True)

def _silu(x):
    return jax.nn.silu(x)

def _sigmoid(x):
    return jax.nn.sigmoid(x)

def _layernorm(x, axis=-1, eps=1e-05):
    m = jnp.mean(x, axis=axis, keepdims=True)
    v = jnp.var(x, axis=axis, keepdims=True)
    return (x - m) / jnp.sqrt(v + eps)

def _scatter_add(tgt, idx, src, axis=0):
    return tgt.at[idx].add(src)

def _segment_sum(src, seg, n):
    return jax.ops.segment_sum(src, seg, n)
kernel_name = 'mk_sandwich_d2_jaxref_r8_b6bcf8'

def setup_inputs(seed: int=0):
    np.random.seed(seed)
    _w = jnp.asarray

    def _L0_attn_setup():
        import jax, jax.numpy as jnp
        import numpy as np
        D_MODEL, N_HEADS, D_HEAD, D_VALUE = (128, 16, 4, 64)
        B, T = (2, 256)
        SCALE = 1.0 / np.sqrt(D_HEAD)

        def _h4_simple_roots():
            c = np.cos(np.pi / 5)
            G = np.eye(4)
            G[0, 1] = G[1, 0] = -c
            G[1, 2] = G[2, 1] = -0.5
            G[2, 3] = G[3, 2] = -0.5
            return np.linalg.cholesky(G).astype(np.float32)

        def _normalize(v):
            return v / jnp.maximum(jnp.linalg.norm(v, axis=-1, keepdims=True), 1e-12)
        key = jax.random.key(seed)
        ks = jax.random.split(key, 8)
        x = jax.random.normal(ks[0], (B, T, D_MODEL), dtype=jnp.float32)
        W_q = jax.random.normal(ks[1], (D_HEAD * N_HEADS, D_MODEL), jnp.float32) / np.sqrt(D_MODEL)
        W_k = jax.random.normal(ks[2], (D_HEAD * N_HEADS, D_MODEL), jnp.float32) / np.sqrt(D_MODEL)
        W_v = jax.random.normal(ks[3], (D_VALUE * N_HEADS, D_MODEL), jnp.float32) / np.sqrt(D_MODEL)
        W_out = jax.random.normal(ks[4], (D_MODEL, D_VALUE * N_HEADS), jnp.float32) / np.sqrt(D_VALUE * N_HEADS)
        W_nudge = jnp.eye(4, dtype=jnp.float32)[None] + 0.01 * jax.random.normal(ks[5], (N_HEADS, 4, 4), jnp.float32)
        chamber_bonus = 0.02 * jax.random.normal(ks[6], (N_HEADS, 16), jnp.float32)
        simple_roots = jnp.asarray(_h4_simple_roots())
        return {'x': x, 'W_q': W_q, 'W_k': W_k, 'W_v': W_v, 'W_nudge': W_nudge, 'chamber_bonus': chamber_bonus, 'W_out': W_out, 'simple_roots': simple_roots}
    _L0_attn_in = _L0_attn_setup()

    def _L0_ffn_setup():
        import jax, jax.numpy as jnp
        import numpy as np
        D_IN, D_HID = (128, 512)

        def _ternary(key, shape):
            return jax.random.randint(key, shape, -1, 2).astype(jnp.float32)

        def _tlin(x, w, s):
            return jnp.einsum('bsi,oi->bso', x, w) * s
        key = jax.random.key(seed)
        ks = jax.random.split(key, 12)
        inv = lambda fan: 1.0 / np.sqrt(fan).astype(np.float32)
        return {'x': jax.random.normal(ks[0], (4, 256, D_IN), dtype=jnp.float32), 'w1_w': _ternary(ks[1], (D_HID, D_IN)), 'w1_s': jax.random.uniform(ks[2], (D_HID,), dtype=jnp.float32) * inv(D_IN), 'w2_w': _ternary(ks[3], (D_HID, D_IN)), 'w2_s': jax.random.uniform(ks[4], (D_HID,), dtype=jnp.float32) * inv(D_IN), 'h1_w': _ternary(ks[5], (D_HID, D_HID)), 'h1_s': jax.random.uniform(ks[6], (D_HID,), dtype=jnp.float32) * inv(D_HID), 'h2_w': _ternary(ks[7], (D_HID, D_HID)), 'h2_s': jax.random.uniform(ks[8], (D_HID,), dtype=jnp.float32) * inv(D_HID), 'w3_w': _ternary(ks[9], (D_IN, D_HID)), 'w3_s': jax.random.uniform(ks[10], (D_IN,), dtype=jnp.float32) * inv(D_HID)}
    _L0_ffn_in = _L0_ffn_setup()

    def _L1_attn_setup():
        import jax, jax.numpy as jnp
        import numpy as np
        B, T, D, H = (64, 64, 128, 128)
        key = jax.random.key(seed)
        k1, k2, k3 = jax.random.split(key, 3)
        scale = 0.02
        return {'x': jax.random.normal(k1, (B, T, D), dtype=jnp.float32), 'Wi': jax.random.normal(k2, (H, D), dtype=jnp.float32) * scale, 'bi': jnp.zeros((H,), dtype=jnp.float32), 'Wh': jax.random.normal(k3, (H, H), dtype=jnp.float32) * scale, 'bh': jnp.zeros((H,), dtype=jnp.float32)}
    _L1_attn_in = _L1_attn_setup()

    def _L1_ffn_setup():
        import jax, jax.numpy as jnp
        import numpy as np
        H = 128
        I = 256
        E = 32
        B, S = (4, 256)

        def _grouped_mm(a, w, group_sizes):
            return jax.lax.ragged_dot(a, w, group_sizes)

        def _swiglu(x, gw, uw, dw):
            return jax.nn.silu(x @ gw) * (x @ uw) @ dw
        key = jax.random.key(seed)
        ks = jax.random.split(key, 8)
        scale = 0.02
        inp = {'hidden_states': jax.random.normal(ks[0], (B, S, H), dtype=jnp.float32), 'gate_w': jax.random.normal(ks[1], (H, E), dtype=jnp.float32) * scale, 'shared_gate_w': jax.random.normal(ks[2], (H, I), dtype=jnp.float32) * scale, 'shared_up_w': jax.random.normal(ks[3], (H, I), dtype=jnp.float32) * scale, 'shared_down_w': jax.random.normal(ks[4], (I, H), dtype=jnp.float32) * scale, 'routed_gate_w': jax.random.normal(ks[5], (E, H, I), dtype=jnp.float32) * scale, 'routed_up_w': jax.random.normal(ks[6], (E, H, I), dtype=jnp.float32) * scale, 'routed_down_w': jax.random.normal(ks[7], (E, I, H), dtype=jnp.float32) * scale}
        return inp
    _L1_ffn_in = _L1_ffn_setup()
    _d = {'L0_attn_x': _L0_attn_in['x'], 'L0_attn_W_q': _L0_attn_in['W_q'], 'L0_attn_W_k': _L0_attn_in['W_k'], 'L0_attn_W_v': _L0_attn_in['W_v'], 'L0_attn_W_nudge': _L0_attn_in['W_nudge'], 'L0_attn_chamber_bonus': _L0_attn_in['chamber_bonus'], 'L0_attn_W_out': _L0_attn_in['W_out'], 'L0_attn_simple_roots': _L0_attn_in['simple_roots'], 'L0_ffn_w1_w': _L0_ffn_in['w1_w'], 'L0_ffn_w1_s': _L0_ffn_in['w1_s'], 'L0_ffn_w2_w': _L0_ffn_in['w2_w'], 'L0_ffn_w2_s': _L0_ffn_in['w2_s'], 'L0_ffn_h1_w': _L0_ffn_in['h1_w'], 'L0_ffn_h1_s': _L0_ffn_in['h1_s'], 'L0_ffn_h2_w': _L0_ffn_in['h2_w'], 'L0_ffn_h2_s': _L0_ffn_in['h2_s'], 'L0_ffn_w3_w': _L0_ffn_in['w3_w'], 'L0_ffn_w3_s': _L0_ffn_in['w3_s'], 'L1_attn_Wi': _L1_attn_in['Wi'], 'L1_attn_bi': _L1_attn_in['bi'], 'L1_attn_Wh': _L1_attn_in['Wh'], 'L1_attn_bh': _L1_attn_in['bh'], 'L1_ffn_gate_w': _L1_ffn_in['gate_w'], 'L1_ffn_shared_gate_w': _L1_ffn_in['shared_gate_w'], 'L1_ffn_shared_up_w': _L1_ffn_in['shared_up_w'], 'L1_ffn_shared_down_w': _L1_ffn_in['shared_down_w'], 'L1_ffn_routed_gate_w': _L1_ffn_in['routed_gate_w'], 'L1_ffn_routed_up_w': _L1_ffn_in['routed_up_w'], 'L1_ffn_routed_down_w': _L1_ffn_in['routed_down_w']}
    _x0 = _d['L0_attn_x']
    _d['L0_attn_x'] = jax.random.normal(jax.random.fold_in(jax.random.key(seed), 1), (32, 256, 128), dtype=_x0.dtype)
    del _x0
    return _d

def reference(L0_attn_x, L0_attn_W_q, L0_attn_W_k, L0_attn_W_v, L0_attn_W_nudge, L0_attn_chamber_bonus, L0_attn_W_out, L0_attn_simple_roots, L0_ffn_w1_w, L0_ffn_w1_s, L0_ffn_w2_w, L0_ffn_w2_s, L0_ffn_h1_w, L0_ffn_h1_s, L0_ffn_h2_w, L0_ffn_h2_s, L0_ffn_w3_w, L0_ffn_w3_s, L1_attn_Wi, L1_attn_bi, L1_attn_Wh, L1_attn_bh, L1_ffn_gate_w, L1_ffn_shared_gate_w, L1_ffn_shared_up_w, L1_ffn_shared_down_w, L1_ffn_routed_gate_w, L1_ffn_routed_up_w, L1_ffn_routed_down_w):

    def _L0_attn_ref(x, W_q, W_k, W_v, W_nudge, chamber_bonus, W_out, simple_roots):
        import jax, jax.numpy as jnp
        import numpy as np
        D_MODEL, N_HEADS, D_HEAD, D_VALUE = (128, 16, 4, 64)
        B, T = (2, 256)
        SCALE = 1.0 / np.sqrt(D_HEAD)

        def _h4_simple_roots():
            c = np.cos(np.pi / 5)
            G = np.eye(4)
            G[0, 1] = G[1, 0] = -c
            G[1, 2] = G[2, 1] = -0.5
            G[2, 3] = G[3, 2] = -0.5
            return np.linalg.cholesky(G).astype(np.float32)

        def _normalize(v):
            return v / jnp.maximum(jnp.linalg.norm(v, axis=-1, keepdims=True), 1e-12)
        b, t, _ = x.shape
        Q = _normalize((x @ W_q.T).reshape(b, t, N_HEADS, D_HEAD))
        K = _normalize((x @ W_k.T).reshape(b, t, N_HEADS, D_HEAD))
        V = (x @ W_v.T).reshape(b, t, N_HEADS, D_VALUE)
        Qn = _normalize(jnp.einsum('bthd,hde->bthe', Q, W_nudge))
        scores = jnp.einsum('bqhd,bkhd->bhqk', Qn, K) * SCALE
        k_dots = jnp.einsum('bthd,rd->bthr', K, simple_roots)
        s = jax.nn.sigmoid(3.0 * k_dots)
        bits = (jnp.arange(16)[:, None] >> jnp.arange(4)[None, :] & 1).astype(x.dtype)
        cw = jnp.prod(s[..., None, :] * bits + (1.0 - s[..., None, :]) * (1.0 - bits), axis=-1)
        k_bonus = jnp.einsum('bthc,hc->bth', cw, chamber_bonus)
        scores = scores + k_bonus.transpose(0, 2, 1)[:, :, None, :]
        causal = jnp.triu(jnp.ones((t, t), dtype=bool), k=1)
        scores = jnp.where(causal[None, None], -jnp.inf, scores)
        attn = jax.nn.softmax(scores, axis=-1)
        out = jnp.einsum('bhqk,bkhv->bqhv', attn, V).reshape(b, t, N_HEADS * D_VALUE)
        return out @ W_out.T

    def _L0_ffn_ref(x, w1_w, w1_s, w2_w, w2_s, h1_w, h1_s, h2_w, h2_s, w3_w, w3_s):
        import jax, jax.numpy as jnp
        import numpy as np
        D_IN, D_HID = (128, 512)

        def _ternary(key, shape):
            return jax.random.randint(key, shape, -1, 2).astype(jnp.float32)

        def _tlin(x, w, s):
            return jnp.einsum('bsi,oi->bso', x, w) * s
        h = jax.nn.silu(_tlin(x, w1_w, w1_s)) * _tlin(x, w2_w, w2_s)
        h = jax.nn.gelu(_tlin(h, h1_w, h1_s), approximate=False)
        h = jax.nn.gelu(_tlin(h, h2_w, h2_s), approximate=False)
        return _tlin(h, w3_w, w3_s)

    def _L1_attn_ref(x, Wi, bi, Wh, bh):
        import jax, jax.numpy as jnp
        import numpy as np
        B, T, D, H = (64, 64, 128, 128)
        xi = jnp.einsum('btd,hd->bth', x, Wi) + bi

        def step(h, xt):
            h_new = jnp.tanh(xt + h @ Wh.T + bh)
            return (h_new, h_new)
        h0 = jnp.zeros((x.shape[0], Wh.shape[0]), dtype=x.dtype)
        _, hs = jax.lax.scan(step, h0, jnp.swapaxes(xi, 0, 1))
        return jnp.swapaxes(hs, 0, 1)

    def _L1_ffn_ref(hidden_states, gate_w, shared_gate_w, shared_up_w, shared_down_w, routed_gate_w, routed_up_w, routed_down_w):
        import jax, jax.numpy as jnp
        import numpy as np
        H = 128
        I = 256
        E = 32
        B, S = (4, 256)

        def _grouped_mm(a, w, group_sizes):
            return jax.lax.ragged_dot(a, w, group_sizes)

        def _swiglu(x, gw, uw, dw):
            return jax.nn.silu(x @ gw) * (x @ uw) @ dw
        b, s, h = hidden_states.shape
        x = hidden_states.reshape(-1, h)
        shared_out = _swiglu(x, shared_gate_w, shared_up_w, shared_down_w)
        logits = x @ gate_w
        topk_ids = jnp.argmax(logits, axis=-1)
        topk_val = jnp.max(logits, axis=-1)
        scores = jax.nn.sigmoid(topk_val)[:, None]
        xs = x * scores
        tokens_per_expert = jnp.zeros((E,), jnp.int32).at[topk_ids].add(1)
        order = jnp.argsort(topk_ids)
        sorted_x = xs[order]
        g = _grouped_mm(sorted_x, routed_gate_w, tokens_per_expert)
        u = _grouped_mm(sorted_x, routed_up_w, tokens_per_expert)
        d = _grouped_mm(jax.nn.silu(g) * u, routed_down_w, tokens_per_expert)
        inv = jnp.argsort(order)
        routed_out = d[inv]
        return (shared_out + routed_out).reshape(b, s, h)
    x = L0_attn_x
    x = x + _layernorm(_L0_attn_ref(_layernorm(x, axis=-1), L0_attn_W_q, L0_attn_W_k, L0_attn_W_v, L0_attn_W_nudge, L0_attn_chamber_bonus, L0_attn_W_out, L0_attn_simple_roots), axis=-1)
    x = x + _layernorm(_L0_ffn_ref(_layernorm(x, axis=-1), L0_ffn_w1_w, L0_ffn_w1_s, L0_ffn_w2_w, L0_ffn_w2_s, L0_ffn_h1_w, L0_ffn_h1_s, L0_ffn_h2_w, L0_ffn_h2_s, L0_ffn_w3_w, L0_ffn_w3_s), axis=-1)
    x = x + _layernorm(_L1_attn_ref(_layernorm(x, axis=-1), L1_attn_Wi, L1_attn_bi, L1_attn_Wh, L1_attn_bh), axis=-1)
    x = x + _layernorm(_L1_ffn_ref(_layernorm(x, axis=-1), L1_ffn_gate_w, L1_ffn_shared_gate_w, L1_ffn_shared_up_w, L1_ffn_shared_down_w, L1_ffn_routed_gate_w, L1_ffn_routed_up_w, L1_ffn_routed_down_w), axis=-1)
    return x

_drawn_inputs = setup_inputs


def setup_inputs(seed=0):
    import zlib

    import numpy as np

    out = dict(_drawn_inputs(seed))
    spreads = {'L1_attn_bi': (0.0, 0.1), 'L1_attn_bh': (0.0, 0.1)}
    factors = {'L0_attn_chamber_bonus': 3.22, 'L0_attn_simple_roots': 3.258}
    for name, (base, spread) in spreads.items():
        noise = np.random.default_rng([zlib.crc32(name.encode()), seed]).standard_normal(out[name].shape)
        drawn = base * np.exp(spread * noise) if base else spread * noise
        out[name] = jnp.asarray(drawn.astype(out[name].dtype))
    for name, factor in factors.items():
        out[name] = (out[name] * factor).astype(out[name].dtype)
    return out
```

```python
from contextlib import ExitStack

import concourse.bass as bass
from concourse import mybir

F32 = mybir.dt.float32
F32R = mybir.dt.float32r
BF16 = mybir.dt.bfloat16
I32 = mybir.dt.int32
ALU = mybir.AluOpType
ACT = mybir.ActivationFunctionType
AX = mybir.AxisListType

P = 128
B, T, D = 32, 256, 128
HEADS, DH, DV = 16, 4, 64
TT = T // P
GH = 4
GROUPS = HEADS // GH
AUG = 32
VA = DV + 1
SC = 384
EPS = 1e-5
NORM_MIN2 = 1e-24


def wait(eng, sem, value):
    if isinstance(value, int) and value <= 0:
        return
    eng.wait_ge(sem, value)


def wait_apart(eng, sem, value, done):
    if not isinstance(value, int):
        value = eng.snap(eng.to_reg(value))
        eng.wait_ge(done, 1)
    wait(eng, sem, value)


def clear(nc, sems):
    with nc.Block() as block:
        @block.gpsimd
        def _(pool):
            for sem in sems:
                pool.sem_clear(sem)


def attention_layer(nc, x, w_qk, w_v, w_rot, w_out, bonus0, bonus_step, x1_d):
    with ExitStack() as ctx:
        def sb(name, shape, dt=F32):
            return ctx.enter_context(nc.sbuf_tensor(name, shape, dt))

        def ps(name, shape, dt=F32):
            return ctx.enter_context(nc.psum_tensor(name, shape, dt))

        def sem(name):
            return ctx.enter_context(nc.semaphore(name))

        ident = sb("ident", [P, P])
        ident_b = sb("ident_b", [P, P], BF16)
        wqk = sb("wqk", [P, 2 * HEADS * DH])
        wv = sb("wv", [P, HEADS * DV])
        wrot = sb("wrot", [P, P])
        wout = sb("wout", [P, HEADS * DV // P, D])
        bon0 = sb("bon0", [P, HEADS, 8])
        bond = sb("bond", [P, HEADS, 8])
        pow_half = sb("pow_half", [P, TT])
        xa = sb("xa", [P, TT, D])
        stat_a = sb("stat_a", [P, TT, 6])
        mv_a = sb("mv_a", [P, TT, 2])
        ve_a = sb("ve_a", [P, TT])
        rstd_a = sb("rstd_a", [P, TT])
        xn = sb("xn", [P, TT, D])
        xnT = sb("xnT", [P, T])
        sq1 = sb("sq1", [P, TT * 2 * HEADS, DH])
        ss1 = sb("ss1", [P, TT * 2 * HEADS])
        ssg1 = sb("ssg1", [P, TT * 2 * HEADS])
        ln1 = sb("ln1", [P, TT * 2 * HEADS])
        r01 = sb("r01", [P, TT * 2 * HEADS])
        nt1 = sb("nt1", [P, TT * 2 * HEADS])
        nu1 = sb("nu1", [P, TT * 2 * HEADS])
        r1 = sb("r1", [P, TT * 2 * HEADS])
        qkn = sb("qkn", [P, TT, 2 * HEADS, DH])
        qkT = sb("qkT", [P, T])
        sq2 = sb("sq2", [P, TT, HEADS, DH])
        ss2 = sb("ss2", [P, TT, HEADS])
        ssg2 = sb("ssg2", [P, TT, HEADS])
        ln2 = sb("ln2", [P, TT, HEADS])
        r02 = sb("r02", [P, TT, HEADS])
        nt2 = sb("nt2", [P, TT, HEADS])
        nu2 = sb("nu2", [P, TT, HEADS])
        r2 = sb("r2", [P, TT, HEADS])
        ek = sb("ek", [P, TT, HEADS, DH])
        ek1 = sb("ek1", [P, TT, HEADS, DH])
        sg = sb("sg", [P, TT, HEADS, DH])
        bt = [sb(f"bt{i}", [P, TT, HEADS, 8 >> i]) for i in range(4)]
        bv = [sb(f"bv{i}", [P, TT, HEADS, 8 >> i]) for i in range(3)]
        q5 = sb("q5", [P, TT, HEADS, DH + 1])
        k5 = sb("k5", [P, TT, HEADS, DH + 1])
        rest = [sb(f"rest{i}", [P, TT * HEADS * (DH + 1)]) for i in range(4)]
        q_part = sb("q_part", [P, 3, TT * HEADS, DH + 1], BF16)
        k_part = sb("k_part", [P, 3, TT * HEADS, DH + 1], BF16)
        q_aug = sb("q_aug", [P, TT * HEADS, AUG], BF16)
        k_aug = sb("k_aug", [P, TT * HEADS, AUG], BF16)
        q_augT = sb("q_augT", [P, GROUPS, T], BF16)
        k_augT = sb("k_augT", [P, GROUPS, T], BF16)
        bonT = sb("bonT", [HEADS, T])
        cmax = sb("cmax", [HEADS, T])
        vaug = [sb(f"vaug{i}", [P, TT, HEADS, VA]) for i in range(2)]
        prob = [sb(f"prob{i}", [P, GH, SC]) for i in range(2)]
        rsum = sb("rsum", [P, TT, GH])
        on = sb("on", [P, TT, HEADS * DV])
        onT = sb("onT", [P, HEADS * DV // P, T])
        xr = sb("xr", [P, TT, D])
        stat_y = sb("stat_y", [P, TT, 6])
        mv_y = sb("mv_y", [P, TT, 2])
        ve_y = sb("ve_y", [P, TT])
        rstd_y = sb("rstd_y", [P, TT])
        yn = sb("yn", [P, TT, D])
        x1 = sb("x1", [P, TT, D])

        score = [ps(f"score{j}", [P, 512]) for j in range(GH)]
        outp = ps("outp", [P, TT, 512])
        front = ps("front", [P, 512])
        front_b = front[:, :].bitcast(BF16)
        back = ps("back", [P, 512])
        back_b = back[:, :].bitcast(BF16)
        outh = outp[:, :, 0:GH * VA].rearrange("p i (h v) -> p i h v", h=GH)

        names = ("w", "const", "xa", "stat_a", "mv_a", "ve_a", "rstd_a", "xn", "p_xnT", "xnT", "p_qk", "sq1", "ss1",
                 "ssg1", "ln1", "r01", "nt1", "nu1", "r1", "qkn", "p_qkT", "qkT", "p_rot", "sq2", "ek", "ss2",
                 "ssg2", "ln2", "r02", "nt2", "nu2", "r2", "ek1", "sg", "q4", "kcopy", "bon", "p_bonT", "bonT", "cmax",
                 "p_cmax", "q5", "ksplit", "qsplit", "kaug", "qaug", "p_kaT", "p_qaT", "kaT", "qaT", "p_v",
                 "v_act", "v_dve", "p_score", "prob", "masked", "p_out", "rsum", "on", "p_onT", "onT", "p_y",
                 "stat_y", "mv_y", "ve_y", "rstd_y", "yn", "xr", "x1", "x1_out")
        s = {name: sem("a_" + name) for name in names}

        STEPS_K = 5
        BON = 11

        ctx.callback(clear, nc, list(s.values()))
        block = ctx.enter_context(nc.Block())

        def rounds(eng, step):
            step(None, 0, 0)
            step(0, 1, 1)
            with eng.Fori(0, (B - 2) // 2) as i:
                step(2 * i + 1, 2 * i + 2, 0)
                step(2 * i + 2, 2 * i + 3, 1)
            step(B - 1, None, 0)

        @block.sync
        def _(sp):
            for dst, src in ((wqk[:], w_qk), (wv[:], w_v), (wrot[:], w_rot),
                             (wout[:], w_out.rearrange("(c p) d -> p c d", p=P)),
                             (bon0[:], bonus0.to_broadcast([P, HEADS, 8])),
                             (bond[:], bonus_step.to_broadcast([P, HEADS, 8]))):
                sp.dma_start(dst, src).then_inc(s["w"], 16)

            def step(b, n, par):
                if n is not None:
                    wait(sp, s["xn"], n)
                    sp.dma_start(xa[:], x[n].rearrange("(i p) d -> p i d", p=P) if isinstance(n, int)
                                 else x[bass.ds(n, 1)].rearrange("o (i p) d -> p (o i) d", p=P)).then_inc(s["xa"], 16)
                if b is not None:
                    wait(sp, s["x1"], b)
                    sp.dma_start(xr[:], x[b].rearrange("(i p) d -> p i d", p=P) if isinstance(b, int)
                                 else x[bass.ds(b, 1)].rearrange("o (i p) d -> p (o i) d", p=P)).then_inc(s["xr"], 16)
                    wait(sp, s["x1"], b + 1)
                    sp.dma_start(x1_d[:, b, :].rearrange("(i p) d -> p i d", p=P) if isinstance(b, int)
                                 else x1_d[:, bass.ds(b, 1), :].rearrange("(i p) o d -> p (i o) d", p=P),
                                 x1[:]).then_inc(s["x1_out"], 16)

            rounds(sp, step)
            sp.wait_ge(s["x1_out"], 16 * B)

        @block.gpsimd
        def _(pool):
            def const(ins):
                const.n += 1
                ins.then_inc(s["const"], 1)
                pool.wait_ge(s["const"], const.n)
            const.n = 0
            const(pool.memset(ident[:], 0.0))
            const(pool.affine_select(out=ident[:], in_=ident[:], compare_op=ALU.not_equal, fill=1.0, base=0,
                                     pattern=[[-1, P]], channel_multiplier=1))
            const(pool.tensor_copy(ident_b[:], ident[:]))
            const(pool.memset(pow_half[:], -0.5))
            const(pool.memset(q_aug[:], 0.0))
            const(pool.memset(k_aug[:], 0.0))
            const(pool.memset(q_aug[:, :, 27:30], 1.0))
            const(pool.memset(k_aug[:, :, 24:27], 1.0))
            for i in range(2):
                const(pool.memset(vaug[i][:, :, :, DV:VA], 1.0))
            pool.wait_ge(s["w"], 96)
            const(pool.tensor_tensor(bond[:], bond[:], bon0[:], ALU.subtract))

            def split(value, part, name, n):
                v = value[:].rearrange("p i h c -> p (i h c)")
                parts = [part[:, k].rearrange("p r c -> p (r c)") for k in range(3)]
                c = 0
                for k in range(3):
                    pool.tensor_scalar(parts[k], v, 1.0, 0.0, ALU.mult, ALU.add).then_inc(s[name], 1)
                    c += 1
                    if k < 2:
                        wait_apart(pool, s[name], STEPS_K * n + c, s["const"])
                        pool.tensor_tensor(rest[k + (2 if name == "qsplit" else 0)][:], v, parts[k],
                                           ALU.subtract).then_inc(s[name], 1)
                        c += 1
                        wait_apart(pool, s[name], STEPS_K * n + c, s["const"])
                        v = rest[k + (2 if name == "qsplit" else 0)][:]

            def rstd(mv, ve, out, name, n):
                wait_apart(pool, s["mv_" + name], TT * (n + 1), s["const"])
                pool.tensor_scalar(ve[:], mv[:, :, 1], 1.0, EPS, ALU.mult, ALU.add).then_inc(s["ve_" + name], 1)
                wait_apart(pool, s["ve_" + name], n + 1, s["const"])
                pool.tensor_tensor(out[:], ve[:], pow_half[:], ALU.pow).then_inc(s["rstd_" + name], 1)

            def mask(b, g):
                for k in range(2):
                    wait_apart(pool, s["prob"], HEADS * b + GH * g + 2 * k + 2, s["const"])
                    for i in range(2):
                        v = prob[g % 2][:, 2 * k:2 * k + 2, 256 * i:256 * i + P]
                        m = pool.affine_select(out=v, in_=v, compare_op=ALU.is_ge, fill=0.0, base=0,
                                               pattern=[[0, 2], [1, P]], channel_multiplier=-1)
                    m.then_inc(s["masked"], 1)

            def bonus(n):
                wait_apart(pool, s["sg"], n + 1, s["const"])
                wait_apart(pool, s["p_bonT"], n, s["const"])
                c = 0
                def did(ins):
                    did.c += 1
                    ins.then_inc(s["bon"], 1)
                    wait_apart(pool, s["bon"], BON * n + did.c, s["const"])
                did.c = 0
                def sig(r, w):
                    return sg[:, :, :, r:r + 1].to_broadcast([P, TT, HEADS, w])
                step_b = bond[:].rearrange("p (o h) c -> p o h c", o=1).to_broadcast([P, TT, HEADS, 8])
                base_b = bon0[:].rearrange("p (o h) c -> p o h c", o=1).to_broadcast([P, TT, HEADS, 8])
                did(pool.tensor_tensor(bt[0][:], sig(0, 8), step_b, ALU.mult))
                did(pool.tensor_tensor(bv[0][:], bt[0][:], base_b, ALU.add))
                for r in range(1, 4):
                    pair = bv[r - 1][:].rearrange("p i h (c two) -> p (i h) c two", two=2)
                    w = 8 >> r
                    t = bt[r][:].rearrange("p i h c -> p (i h) c")
                    sr = sg[:].rearrange("p i h r -> p (i h) r")[:, :, r:r + 1].to_broadcast([P, TT * HEADS, w])
                    did(pool.tensor_tensor(t, pair[:, :, :, 1], pair[:, :, :, 0], ALU.subtract))
                    did(pool.tensor_tensor(t, t, sr, ALU.mult))
                    out = bv[r][:].rearrange("p i h c -> p (i h) c") if r < 3 \
                        else k5[:].rearrange("p i h c -> p (i h) c")[:, :, DH:DH + 1]
                    did(pool.tensor_tensor(out, t, pair[:, :, :, 0], ALU.add))

            def spread(aug, part, order_first, name, n):
                pass

            def step(b, n, par):
                if n is not None:
                    rstd(mv_a, ve_a, rstd_a, "a", n)
                if b is not None:
                    mask(b, 0)
                    mask(b, 1)
                if n is not None:
                    wait_apart(pool, s["qkn"], n + 1, s["const"])
                    pool.tensor_scalar(k5[:, :, :, 0:DH], qkn[:, :, HEADS:, :], 1.0, 0.0,
                                       ALU.mult, ALU.add).then_inc(s["kcopy"], 1)
                if b is not None:
                    mask(b, 2)
                    mask(b, 3)
                if n is not None:
                    bonus(n)
                    wait_apart(pool, s["kcopy"], n + 1, s["const"])
                    wait_apart(pool, s["p_kaT"], n, s["const"])
                    split(k5, k_part, "ksplit", n)
                    wait_apart(pool, s["ksplit"], STEPS_K * (n + 1), s["const"])
                    kp = k_part[:].rearrange("p k r c -> p r k c")
                    rows = k_aug[:].rearrange("p r (m c) -> p r m c", c=DH)
                    pool.tensor_scalar(rows[:, :, 0:3, :], kp[:, :, :, 0:DH], 1.0, 0.0, ALU.mult, ALU.add)
                    pool.tensor_scalar(rows[:, :, 3:5, :], kp[:, :, 0:2, 0:DH], 1.0, 0.0, ALU.mult, ALU.add)
                    pool.tensor_scalar(rows[:, :, 5, :], kp[:, :, 0, 0:DH], 1.0, 0.0, ALU.mult, ALU.add)
                    pool.tensor_scalar(k_aug[:, :, 27:30], kp[:, :, :, DH], 1.0, 0.0,
                                       ALU.mult, ALU.add).then_inc(s["kaug"], 1)
                    wait_apart(pool, s["q5"], n + 1, s["const"])
                    wait_apart(pool, s["p_qaT"], n, s["const"])
                    split(q5, q_part, "qsplit", n)
                    wait_apart(pool, s["qsplit"], STEPS_K * (n + 1), s["const"])
                    qp = q_part[:].rearrange("p k r c -> p r k c")
                    rows = q_aug[:].rearrange("p r (m c) -> p r m c", c=DH)
                    for lo, hi, k in ((0, 3, 0), (3, 5, 1), (5, 6, 2)):
                        pool.tensor_scalar(rows[:, :, lo:hi, :],
                                           qp[:, :, k:k + 1, 0:DH].to_broadcast([P, TT * HEADS, hi - lo, DH]),
                                           1.0, 0.0, ALU.mult, ALU.add)
                    pool.tensor_scalar(q_aug[:, :, 24:27], qp[:, :, :, DH], 1.0, 0.0,
                                       ALU.mult, ALU.add).then_inc(s["qaug"], 1)
                if b is not None:
                    rstd(mv_y, ve_y, rstd_y, "y", b)

            rounds(pool, step)

        @block.tensor
        def _(pe):
            def scores(b, g):
                if g == 0:
                    wait(pe, s["qaT"], b + 1)
                    wait(pe, s["kaT"], b + 1)
                for j in range(GH):
                    wait(pe, s["prob"], HEADS * b + GH * (g - 1) + j + 1)
                    r = slice(AUG * j, AUG * (j + 1))
                    pe.matmul(score[j][:, 0:T], k_augT[r, g, 0:P], q_augT[r, g, :], start=True, stop=True,
                              tile_position=(AUG * j, 0))
                    pe.matmul(score[j][:, T:SC], k_augT[r, g, P:T], q_augT[r, g, P:T], start=True, stop=True,
                              tile_position=(AUG * j, 0)).then_inc(s["p_score"], 1)

            def weighted(b, g, par):
                wait(pe, s["masked"], 2 * GROUPS * b + 2 * g + 2)
                wait(pe, s["on"], GROUPS * b + g)
                if g == 0:
                    wait(pe, s["v_act"], 2 * (b + 1))
                    wait(pe, s["v_dve"], 2 * (b + 1))
                w, v = prob[g % 2], vaug[par]
                for j in range(GH):
                    h = GH * g + j
                    c = slice(j * VA, (j + 1) * VA)
                    pe.matmul(outp[:, 0, c], w[:, j, 0:P], v[:, 0, h, :], start=True, stop=True)
                    pe.matmul(outp[:, 1, c], w[:, j, P:T], v[:, 0, h, :], start=True, stop=False)
                    m = pe.matmul(outp[:, 1, c], w[:, j, T:SC], v[:, 1, h, :], start=False, stop=True)
                m.then_inc(s["p_out"], 1)

            def turn_out(b, g):
                wait(pe, s["on"], GROUPS * b + g + 1)
                wait(pe, s["onT"], GROUPS * b)
                for c in range(2):
                    for i in range(TT):
                        o = (2 * c + i) * P
                        m = pe.transpose(back[:, o:o + P], on[:, i, (2 * g + c) * P:(2 * g + c + 1) * P], ident[:])
                m.then_inc(s["p_onT"], 1)

            def values(b, n, k):
                if b is not None:
                    wait(pe, s["yn"], b) if k == 0 else wait(pe, s["onT"], GROUPS * b + k)
                elif k:
                    pe.wait_ge(s["v_act" if k % 2 else "v_dve"], (k + 1) // 2)
                pe.matmul(back[:, :], xnT[:, (k // 2) * P:(k // 2 + 1) * P],
                          wv[:, (k % 2) * 512:(k % 2 + 1) * 512], start=True, stop=True).then_inc(s["p_v"], 1)

            pe.wait_ge(s["const"], 11)
            pe.wait_ge(s["w"], 96)

            def step(b, n, par):
                A, F = b is not None, n is not None
                opar = 1 - par
                if A:
                    scores(b, 0)
                    scores(b, 1)
                    weighted(b, 0, opar)
                if F:
                    wait(pe, s["xn"], n + 1)
                    wait(pe, s["qaT"], n)
                    for i in range(TT):
                        m = pe.transpose(front[:, i * P:(i + 1) * P], xn[:, i, :], ident[:])
                    m.then_inc(s["p_xnT"], 1)
                if A:
                    scores(b, 2)
                if F:
                    wait(pe, s["xnT"], n + 1)
                    for i in range(TT):
                        m = pe.matmul(front[:, i * P:(i + 1) * P], xnT[:, i * P:(i + 1) * P], wqk[:],
                                      start=True, stop=True)
                    m.then_inc(s["p_qk"], 1)
                    values(b, n, 0)
                if A:
                    weighted(b, 1, opar)
                if A:
                    if F:
                        wait(pe, s["v_act"], 2 * n + 1)
                    turn_out(b, 0)
                if F:
                    wait(pe, s["qkn"], n + 1)
                    for i in range(TT):
                        m = pe.transpose(front[:, i * P:(i + 1) * P],
                                         qkn[:, i].rearrange("p h c -> p (h c)"), ident[:])
                    m.then_inc(s["p_qkT"], 1)
                    values(b, n, 1)
                if A:
                    scores(b, 3)
                    weighted(b, 2, opar)
                if F:
                    wait(pe, s["qkT"], n + 1)
                    for i in range(TT):
                        m = pe.matmul(front[:, i * P:(i + 1) * P], qkT[:, i * P:(i + 1) * P], wrot[:],
                                      start=True, stop=True)
                    m.then_inc(s["p_rot"], 1)
                if A:
                    if F:
                        wait(pe, s["v_dve"], 2 * n + 1)
                    else:
                        wait(pe, s["onT"], GROUPS * b + 1)
                    turn_out(b, 1)
                if F:
                    values(b, n, 2)
                if A:
                    weighted(b, 3, opar)
                    if F:
                        wait(pe, s["v_act"], 2 * n + 2)
                    else:
                        wait(pe, s["onT"], GROUPS * b + 2)
                    turn_out(b, 2)
                if F:
                    values(b, n, 3)
                    wait(pe, s["bon"], BON * (n + 1))
                    wait(pe, s["q4"], n + 1)
                    for i in range(TT):
                        m = pe.matmul(front[0:HEADS, i * P:(i + 1) * P], k5[:, i, :, DH], ident[:],
                                      start=True, stop=True)
                    m.then_inc(s["p_bonT"], 1)
                if A:
                    if F:
                        wait(pe, s["v_dve"], 2 * n + 2)
                    else:
                        wait(pe, s["onT"], GROUPS * b + 3)
                    turn_out(b, 3)
                if F:
                    wait(pe, s["cmax"], n + 1)
                    for i in range(TT):
                        m = pe.matmul(front[:, i * HEADS:(i + 1) * HEADS], cmax[:, i * P:(i + 1) * P],
                                      ident[0:HEADS, 0:HEADS], start=True, stop=True)
                    m.then_inc(s["p_cmax"], 1)
                if A:
                    wait(pe, s["onT"], GROUPS * (b + 1))
                    for i in range(TT):
                        for c in range(HEADS * DV // P):
                            m = pe.matmul(back[:, i * P:(i + 1) * P], onT[:, c, i * P:(i + 1) * P], wout[:, c, :],
                                          start=(c == 0), stop=(c == HEADS * DV // P - 1))
                    m.then_inc(s["p_y"], 1)
                if F:
                    for aug, name, last in ((k_aug, "k", "q5"), (q_aug, "q", "kaT")):
                        wait(pe, s[name + "aug"], n + 1)
                        wait(pe, s[last], n + 1)
                        for g in range(GROUPS):
                            for i in range(TT):
                                o = (g * TT + i) * P
                                m = pe.transpose(
                                    front_b[:, o:o + P],
                                    aug[:, i * HEADS + GH * g:i * HEADS + GH * (g + 1), :]
                                    .rearrange("p h c -> p (h c)"), ident_b[:])
                        m.then_inc(s[f"p_{name}aT"], 1)

            rounds(pe, step)

        @block.scalar
        def _(act):
            def weights(b, g):
                if g >= 2:
                    wait(act, s["p_out"], GROUPS * b + g - 1)
                else:
                    wait(act, s["p_out"], GROUPS * b + g - 1)
                for j in range(GH):
                    wait(act, s["p_score"], HEADS * b + GH * g + j + 1)
                    act.activation(prob[g % 2][:, j, :], score[j][:, 0:SC], ACT.Exp).then_inc(s["prob"], 1)

            def copy_values(n, k, par):
                wait(act, s["p_v"], 4 * n + k + 1)
                act.activation(vaug[par][:, k // 2, (k % 2) * 8:(k % 2) * 8 + 8, 0:DV],
                               back[:, :].rearrange("p (h v) -> p h v", h=8), ACT.Copy).then_inc(s["v_act"], 1)

            def copy_out(b, g):
                wait(act, s["p_onT"], GROUPS * b + g + 1)
                wait(act, s["p_y"], b)
                act.activation(onT[:, 2 * g:2 * g + 2, :].rearrange("p c t -> p (c t)"), back[:, :],
                               ACT.Copy).then_inc(s["onT"], 1)

            act.wait_ge(s["const"], 11)

            def step(b, n, par):
                A, F = b is not None, n is not None
                if A:
                    weights(b, 0)
                    weights(b, 1)
                if F:
                    wait(act, s["p_xnT"], n + 1)
                    wait(act, s["p_v"], 4 * n)
                    act.activation(xnT[:], front[:, 0:T], ACT.Copy).then_inc(s["xnT"], 1)
                if A:
                    weights(b, 2)
                if F:
                    wait(act, s["p_qk"], n + 1)
                    wait(act, s["ss1"], n)
                    act.activation(sq1[:].rearrange("p r c -> p (r c)"), front[:, 0:T],
                                   ACT.Square).then_inc(s["sq1"], 1)
                    copy_values(n, 0, par)
                    wait(act, s["ssg1"], n + 1)
                    act.activation(ln1[:], ssg1[:], ACT.Ln).then_inc(s["ln1"], 1)
                    act.wait_ge(s["ln1"], n + 1)
                    wait(act, s["r1"], n)
                    act.activation(r01[:], ln1[:], ACT.Exp, scale=-0.5).then_inc(s["r01"], 1)
                if A:
                    copy_out(b, 0)
                if F:
                    wait(act, s["p_qkT"], n + 1)
                    act.activation(qkT[:], front[:, 0:T], ACT.Copy).then_inc(s["qkT"], 1)
                if A:
                    weights(b, 3)
                if F:
                    wait(act, s["p_rot"], n + 1)
                    fr = front[:, 0:T].rearrange("p (i k h c) -> p i k h c", i=TT, k=2, c=DH)
                    act.activation(sq2[:], fr[:, :, 0], ACT.Square).then_inc(s["sq2"], 1)
                    act.activation(ek[:], fr[:, :, 1], ACT.Exp, scale=-3.0).then_inc(s["ek"], 1)
                if A:
                    copy_out(b, 1)
                if F:
                    copy_values(n, 2, par)
                    wait(act, s["ssg2"], n + 1)
                    act.activation(ln2[:], ssg2[:], ACT.Ln).then_inc(s["ln2"], 1)
                    act.wait_ge(s["ln2"], n + 1)
                    act.activation(r02[:], ln2[:], ACT.Exp, scale=-0.5).then_inc(s["r02"], 1)
                if A:
                    copy_out(b, 2)
                    copy_out(b, 3)
                if F:
                    wait(act, s["p_qaT"], n + 1)
                    act.activation(q_augT[:].rearrange("p g t -> p (g t)"), front_b[:, :],
                                   ACT.Copy).then_inc(s["qaT"], 1)

            rounds(act, step)

        @block.vector
        def _(dve):
            def stats(src, stat, mv, name, n):
                for i in range(TT):
                    m = dve.bn_stats(stat[:, i, :], src[:, i * D:(i + 1) * D])
                m.then_inc(s["stat_" + name], 1)
                wait_apart(dve, s["stat_" + name], n + 1, s["const"])
                for i in range(TT):
                    dve.bn_aggr(mv[:, i, :], stat[:, i, :]).then_inc(s["mv_" + name], 1)

            def normalise(b, g):
                wait(dve, s["p_out"], GROUPS * b + g + 1)
                dve.reciprocal(rsum[:], outh[:, :, :, DV]).then_inc(s["rsum"], 1)
                dve.wait_ge(s["rsum"], GROUPS * b + g + 1)
                wait(dve, s["p_onT"], GROUPS * (b - 1) + g + 1)
                dve.tensor_tensor(
                    on[:, :, g * GH * DV:(g + 1) * GH * DV].rearrange("p i (h v) -> p i h v", h=GH),
                    outh[:, :, :, 0:DV], rsum[:].rearrange("p i (h o) -> p i h o", o=1)
                    .to_broadcast([P, TT, GH, DV]), ALU.mult).then_inc(s["on"], 1)

            def copy_values(n, k, par):
                wait(dve, s["p_v"], 4 * n + k + 1)
                dve.tensor_copy(vaug[par][:, k // 2, (k % 2) * 8:(k % 2) * 8 + 8, 0:DV],
                                back[:, :].rearrange("p (h v) -> p h v", h=8)).then_inc(s["v_dve"], 1)

            def newton(r0, ssg, nt, nu, out, name, n, half):
                wait(dve, s["r0" + name], n + 1)
                dve.tensor_tensor(nt[:], ssg[:], r0[:], ALU.mult).then_inc(s["nt" + name], 1)
                dve.wait_ge(s["nt" + name], n + 1)
                dve.scalar_tensor_tensor(out=nu[:], in0=nt[:], scalar=-half, in1=r0[:], op0=ALU.mult,
                                         op1=ALU.mult).then_inc(s["nu" + name], 1)
                dve.wait_ge(s["nu" + name], n + 1)
                dve.scalar_tensor_tensor(out=out[:], in0=nu[:], scalar=3 * half, in1=r0[:], op0=ALU.add,
                                         op1=ALU.mult).then_inc(s["r" + name], 1)
                dve.wait_ge(s["r" + name], n + 1)

            dve.wait_ge(s["const"], 11)

            def step(b, n, par):
                A, F = b is not None, n is not None
                if F:
                    wait(dve, s["xa"], 16 * (n + 1))
                    stats(xa[:].rearrange("p i d -> p (i d)"), stat_a, mv_a, "a", n)
                    wait(dve, s["rstd_a"], n + 1)
                    wait(dve, s["p_xnT"], n)
                    for i in range(TT):
                        m = dve.tensor_scalar(xn[:, i, :], xa[:, i, :], mv_a[:, i, 0:1], rstd_a[:, i:i + 1],
                                              ALU.subtract, ALU.mult)
                    m.then_inc(s["xn"], 1)
                if A:
                    normalise(b, 0)
                if F:
                    wait(dve, s["sq1"], n + 1)
                    dve.tensor_reduce(ss1[:], sq1[:], AX.X, ALU.add).then_inc(s["ss1"], 1)
                    dve.wait_ge(s["ss1"], n + 1)
                    dve.tensor_scalar(ssg1[:], ss1[:], NORM_MIN2, None, ALU.max).then_inc(s["ssg1"], 1)
                    newton(r01, ssg1, nt1, nu1, r1, "1", n, 0.5)
                    wait(dve, s["kcopy"], n)
                    dve.tensor_tensor(qkn[:].rearrange("p i h c -> p (i h) c"),
                                      front[:, 0:T].rearrange("p (r c) -> p r c", c=DH),
                                      r1[:].rearrange("p (r o) -> p r o", o=1).to_broadcast([P, TT * 2 * HEADS, DH]),
                                      ALU.mult).then_inc(s["qkn"], 1)
                if A:
                    normalise(b, 1)
                if F:
                    copy_values(n, 1, par)
                if A:
                    normalise(b, 2)
                if F:
                    wait(dve, s["ek"], n + 1)
                    wait(dve, s["bon"], BON * n)
                    dve.tensor_reduce(ss2[:], sq2[:], AX.X, ALU.add).then_inc(s["ss2"], 1)
                    dve.tensor_scalar(ek1[:], ek[:], 1.0, None, ALU.add).then_inc(s["ek1"], 1)
                    dve.wait_ge(s["ss2"], n + 1)
                    dve.tensor_scalar(ssg2[:], ss2[:], NORM_MIN2, None, ALU.max).then_inc(s["ssg2"], 1)
                    dve.wait_ge(s["ek1"], n + 1)
                    dve.reciprocal(sg[:], ek1[:]).then_inc(s["sg"], 1)
                    newton(r02, ssg2, nt2, nu2, r2, "2", n, 0.25)
                    wait(dve, s["qsplit"], STEPS_K * n)
                    fr = front[:, 0:T].rearrange("p (i k h c) -> p i k h c", i=TT, k=2, c=DH)
                    dve.tensor_tensor(q5[:, :, :, 0:DH], fr[:, :, 0],
                                      r2[:].rearrange("p i (h o) -> p i h o", o=1).to_broadcast([P, TT, HEADS, DH]),
                                      ALU.mult).then_inc(s["q4"], 1)
                if A:
                    normalise(b, 3)
                if F:
                    copy_values(n, 3, par)
                    wait(dve, s["p_bonT"], n + 1)
                    dve.tensor_copy(bonT[:], front[0:HEADS, 0:T]).then_inc(s["bonT"], 1)
                    dve.wait_ge(s["bonT"], n + 1)
                    wait(dve, s["p_cmax"], n)
                    dve.tensor_tensor_scan(out=cmax[:], data0=bonT[:], data1=bonT[:], initial=bonT[:, 0:1],
                                           op0=ALU.max, op1=ALU.max).then_inc(s["cmax"], 1)
                    wait(dve, s["p_cmax"], n + 1)
                    dve.tensor_scalar(q5[:, :, :, DH], front[:, 0:TT * HEADS].rearrange("p (i h) -> p i h", i=TT),
                                      -1.0, None, ALU.mult).then_inc(s["q5"], 1)
                    wait(dve, s["p_kaT"], n + 1)
                    if A:
                        wait(dve, s["p_score"], HEADS * (b + 1))
                    dve.tensor_copy(k_augT[:].rearrange("p g t -> p (g t)"), front_b[:, :]).then_inc(s["kaT"], 1)
                if A:
                    wait(dve, s["p_y"], b + 1)
                    stats(back[:, 0:TT * D], stat_y, mv_y, "y", b)
                    wait(dve, s["rstd_y"], b + 1)
                    for i in range(TT):
                        m = dve.tensor_scalar(yn[:, i, :], back[:, i * D:(i + 1) * D], mv_y[:, i, 0:1],
                                              rstd_y[:, i:i + 1], ALU.subtract, ALU.mult)
                    m.then_inc(s["yn"], 1)
                    dve.wait_ge(s["yn"], b + 1)
                    wait(dve, s["xr"], 16 * (b + 1))
                    wait(dve, s["x1_out"], 16 * b)
                    dve.tensor_tensor(x1[:], yn[:], xr[:], ALU.add).then_inc(s["x1"], 1)

            rounds(dve, step)


CHUNK = 512
CT = CHUNK // P
NC = B * T // CHUNK
STEPS = CHUNK // B
HID = 512
HC = HID // P
E = 32
NT = B * T // P


def part(t, i, n):
    return t[:, i * n:(i + 1) * n] if isinstance(i, int) else t[:, bass.ds(i * n, n)]


def mixing_layers(nc, x1_d, x3_d, w1, w2, h1, h2, w3, scales, w3_scale, wi, wh, rnn_bias, gate, sorted_d, keep):
    with ExitStack() as ctx:
        def sb(name, shape, dt=F32):
            return ctx.enter_context(nc.sbuf_tensor(name, shape, dt))

        def ps(name, shape, dt=F32):
            return ctx.enter_context(nc.psum_tensor(name, shape, dt))

        def sem(name):
            return ctx.enter_context(nc.semaphore(name))

        ident = sb("ident2", [P, P])
        before = sb("before", [P, P], BF16)
        ones = sb("ones", [P, P], BF16)
        pow_half = sb("pow_half2", [P, CT])
        rev = sb("rev", [P, E])
        zeros = sb("zeros", [P, 2048])
        w1_sb = sb("w1_sb", [P, HID])
        w2_sb = sb("w2_sb", [P, HID])
        h1_sb = sb("h1_sb", [P, HC, HID])
        h2_sb = sb("h2_sb", [P, HC, HID])
        w3_sb = sb("w3_sb", [P, HC, D])
        sc = sb("sc", [P, 4, HC])
        sc_half = sb("sc_half", [P, HC])
        sc_prod = sb("sc_prod", [P, HC])
        w3s = sb("w3s", [P, D])
        wi_sb = sb("wi_sb", [P, D])
        wh_sb = sb("wh_sb", [P, D])
        rb = sb("rb", [P, 2])
        bias = sb("bias", [P, 1])
        gate_sb = sb("gate_sb", [P, E])

        x1c = [sb(f"x1c{i}", [P, CT, D]) for i in range(2)]
        xn2 = sb("xn2", [P, CT, D])
        xn2T = sb("xn2T", [P, CHUNK])
        th = [sb(f"th{i}", [P, CHUNK]) for i in range(2)]
        ag = [sb(f"ag{i}", [P, CHUNK]) for i in range(2)]
        hT = [sb(f"hT{i}", [P, HC, CHUNK]) for i in range(3)]
        y = sb("y", [P, CT, D])
        yn = sb("yn2", [P, CT, D])
        x2 = [sb(f"x2{i}", [P, CT, D]) for i in range(2)]
        xn3 = sb("xn3", [P, CT, D])
        xn3T = sb("xn3T", [P, CHUNK])
        state = sb("state", [P, CHUNK])
        hn = sb("hn", [P, CT, D])
        x3 = sb("x3", [P, CT, D])
        xn4 = sb("xn4", [P, CT, D])
        stat = {n: sb("bstat_" + n, [P, CT, 6]) for n in "fyxhe"}
        mv = {n: sb("bmv_" + n, [P, CT, 2]) for n in "fyxhe"}
        ve = {n: sb("bve_" + n, [P, CT]) for n in "fyxhe"}
        rs = {n: sb("brs_" + n, [P, CT]) for n in "fyxhe"}
        top = sb("top", [P, CT])
        is_top = sb("is_top", [P, CT, E])
        rtop = sb("rtop", [P, CT, E])
        first = sb("first", [P, CT])
        tanh_top = sb("tanh_top", [P, CT])
        gate_val = sb("gate_val", [P, CT])
        pre = sb("pre", [P, CT, E])
        pre_oh = sb("pre_oh", [P, CT, E])
        xn4T = sb("xn4T", [P, CHUNK])
        onehot = sb("onehot", [P, CT, E], BF16)
        xn4T_all, xs_all, oh_all, rank_all, counts = keep

        main = [ps(f"main{i}", [P, CHUNK]) for i in range(4)]
        yp = ps("yp", [P, CHUNK])
        turn = ps("turn", [P, CHUNK])
        xi = ps("xi", [P, CHUNK])
        route = ps("route", [P, CHUNK])

        names = ("w", "const", "xc0", "xc1", "p_xn2T", "xn2", "xn2T", "p_a", "p_g", "tanh", "ag", "h1", "p_h1", "p_h2", "h2", "h3",
                 "p_y", "y", "yn", "x2", "xn3", "p_xn3T", "xn3T", "p_xi", "p_step", "step", "p_state", "hn", "x3",
                 "x3_out", "xn4", "p_xn4T", "xn4T", "p_logit", "top", "is_top", "rtop", "first", "onehot",
                 "tanh_top", "gate_val", "xs", "p_rank", "pre", "pre_oh", "rank", "counts", "zero", "kept")
        s = {name: sem("b_" + name) for name in names}
        for n in "fyxhe":
            for k in ("stat", "mv", "ve", "rs"):
                s[k + n] = sem(f"b_{k}_{n}")
        N_CONST = 12

        ctx.callback(clear, nc, list(s.values()))
        block = ctx.enter_context(nc.Block())

        def rounds(eng, step):
            def row(k, par):
                return [v if not isinstance(v, int) or 0 <= v < NC else None for v in (k, k - 1, k - 2, k - 3)] + [par]
            for k in range(4):
                step(*row(k, k % 2))
            with eng.Fori(0, (NC - 4) // 2) as i:
                for par in range(2):
                    k = 2 * i + (4 + par)
                    step(k, k - 1, k - 2, k - 3, par)
            for k in range(NC, NC + 3):
                step(*row(k, k % 2))

        x1_rows = x1_d.rearrange("(c k u) b d -> c (u b) k d", k=CT, u=P // B)
        x3_rows = x3_d.rearrange("(c k p) d -> c p k d", k=CT, p=P)

        def chunk_of(ap, c):
            return ap[c] if isinstance(c, int) else ap[bass.ds(c, 1)].rearrange("o p k d -> p (o k) d")

        @block.sync
        def _(sp):
            for dst, src in ((w1_sb[:], w1), (w2_sb[:], w2), (wi_sb[:], wi), (wh_sb[:], wh), (gate_sb[:], gate),
                             (sc[:], scales), (rb[:], rnn_bias), (w3s[:], w3_scale.to_broadcast([P, D])),
                             (h1_sb[:], h1.rearrange("(c p) n -> p c n", p=P)),
                             (h2_sb[:], h2.rearrange("(c p) n -> p c n", p=P)),
                             (w3_sb[:], w3.rearrange("(c p) n -> p c n", p=P))):
                sp.dma_start(dst, src).then_inc(s["w"], 16)

            def step(p, c, r, q, par):
                if p is not None:
                    wait(sp, s["x2"], p - 1)
                    sp.dma_start(x1c[par][:], chunk_of(x1_rows, p)).then_inc(s[f"xc{par}"], 16)
                if r is not None:
                    wait(sp, s["x3"], r + 1)
                    sp.dma_start(chunk_of(x3_rows, r), x3[:]).then_inc(s["x3_out"], 16)

            rounds(sp, step)
            sp.wait_ge(s["const"], N_CONST)
            slots = sorted_d.rearrange("(g p k) d -> g p (k d)", p=P, k=16)
            for g in range(slots.shape[0]):
                sp.dma_start(slots[g], zeros[:]).then_inc(s["zero"], 16)
            sp.wait_ge(s["zero"], 16 * slots.shape[0])
            sp.wait_ge(s["x3_out"], 16 * NC)

        @block.gpsimd
        def _(pool):
            def const(ins):
                const.n += 1
                ins.then_inc(s["const"], 1)
                pool.wait_ge(s["const"], const.n)
            const.n = 0
            const(pool.memset(ident[:], 0.0))
            const(pool.affine_select(out=ident[:], in_=ident[:], compare_op=ALU.not_equal, fill=1.0, base=0,
                                     pattern=[[-1, P]], channel_multiplier=1))
            const(pool.memset(ones[:], 1.0))
            const(pool.affine_select(out=before[:], in_=ones[:], compare_op=ALU.is_gt, fill=0.0, base=0,
                                     pattern=[[1, P]], channel_multiplier=-1))
            const(pool.memset(pow_half[:], -0.5))
            const(pool.iota(rev[:], pattern=[[-1, E]], base=E, channel_multiplier=0,
                            allow_small_or_imprecise_dtypes=True))
            const(pool.memset(zeros[:], 0.0))
            const(pool.memset(state[:], 0.0))
            const(pool.memset(counts[:], 0.0))
            pool.wait_ge(s["w"], 176)
            const(pool.tensor_scalar(sc_half[:], sc[:, 0, :], 0.5, 0.0, ALU.mult, ALU.add))
            const(pool.tensor_tensor(sc_prod[:], sc_half[:], sc[:, 1, :], ALU.mult))
            const(pool.tensor_tensor(bias[:], rb[:, 0:1], rb[:, 1:2], ALU.add))

            def rstd(n, c):
                wait_apart(pool, s["mv" + n], CT * (c + 1), s["const"])
                pool.tensor_scalar(ve[n][:], mv[n][:, :, 1], 1.0, EPS, ALU.mult, ALU.add).then_inc(s["ve" + n], 1)
                wait_apart(pool, s["ve" + n], c + 1, s["const"])
                pool.tensor_tensor(rs[n][:], ve[n][:], pow_half[:], ALU.pow).then_inc(s["rs" + n], 1)

            def step(p, c, r, q, par):
                if p is not None:
                    rstd("f", p)
                if r is not None:
                    rstd("h", r)
                    rstd("e", r)
                if c is not None:
                    rstd("y", c)
                    rstd("x", c)

            rounds(pool, step)

        @block.tensor
        def _(pe):
            def turn4(src, name):
                for k in range(CT):
                    m = pe.transpose(turn[:, k * P:(k + 1) * P], src[:, k], ident[:])
                m.then_inc(s[name], 1)

            def rnn_step(r, t):
                wait(pe, s["step"], STEPS * r + t)
                o = t * B
                prev = (t - 1) % STEPS * B
                pe.matmul(xi[:, o:o + B], wh_sb[:], state[:, prev:prev + B], start=False, stop=(t == STEPS - 1),
                          skip_group_check=True).then_inc(s["p_step"], 1)

            pe.wait_ge(s["w"], 176)
            pe.wait_ge(s["const"], N_CONST)

            def step(p, c, r, q, par):
                if c is not None:
                    wait(pe, s["xn2"], c + 1)
                    wait(pe, s["hn"], c - 1)
                    turn4(xn2[:], "p_xn2T")
                    wait(pe, s["xn2T"], c + 1)
                    for m in range(HC):
                        wait(pe, s["h3"], HC * c) if m < 2 else wait(pe, s["h1"], HC * c + m - 1)
                        pe.matmul(main[2 * m % 4][:, :], w1_sb[:, m * P:(m + 1) * P], xn2T[:],
                                  start=True, stop=True).then_inc(s["p_a"], 1)
                        pe.matmul(main[(2 * m + 1) % 4][:, :], w2_sb[:, m * P:(m + 1) * P], xn2T[:],
                                  start=True, stop=True).then_inc(s["p_g"], 1)
                if q is not None:
                    wait(pe, s["xn4"], q + 1)
                    if c is not None:
                        wait(pe, s["xn2T"], c + 1)
                    wait(pe, s["hn"], q + 1)
                    turn4(xn4[:], "p_xn4T")
                    wait(pe, s["rank"], q)
                    wait(pe, s["counts"], q)
                    wait(pe, s["xn4T"], q + 1)
                    for k in range(CT):
                        m_ = pe.matmul(route[:, k * E:(k + 1) * E], xn4T[:, k * P:(k + 1) * P], gate_sb[:],
                                       start=True, stop=True)
                    m_.then_inc(s["p_logit"], 1)
                if r is not None:
                    wait(pe, s["xn3"], r + 1)
                    if q is not None:
                        wait(pe, s["xn4T"], q + 1)
                    elif c is not None:
                        wait(pe, s["xn2T"], c + 1)
                    turn4(xn3[:], "p_xn3T")
                slots = iter(range(STEPS))

                def rnn(n=1):
                    if r is not None:
                        for _ in range(n):
                            t = next(slots, None)
                            if t is not None:
                                rnn_step(r, t)

                def recurrence_input():
                    if r is not None:
                        wait(pe, s["xn3T"], r + 1)
                        wait(pe, s["step"], STEPS * r)
                        pe.matmul(xi[:, :], wi_sb[:], xn3T[:], start=True, stop=False,
                                  skip_group_check=True).then_inc(s["p_xi"], 1)

                def ranks():
                    if q is not None:
                        wait(pe, s["onehot"], q + 1)
                        for k in range(CT):
                            for j in range(k):
                                pe.matmul(route[:, 128 + k * E:128 + (k + 1) * E], ones[:], onehot[:, j, :],
                                          start=(j == 0), stop=False)
                            pe.matmul(route[:, 128 + k * E:128 + (k + 1) * E], before[:], onehot[:, k, :],
                                      start=(k == 0), stop=True)
                        for j in range(CT):
                            m_ = pe.matmul(route[:, 256:256 + E], ones[:], onehot[:, j, :], start=(j == 0),
                                           stop=(j == CT - 1))
                        m_.then_inc(s["p_rank"], 1)

                if c is not None:
                    for layer, (w, src, done, out) in enumerate(((h1_sb, hT[0], "h1", "h2"), (h2_sb, hT[1], "h2", "h3"))):
                        for m in range(HC):
                            if m == 0:
                                wait(pe, s[done], HC * (c + 1))
                            for k in range(HC):
                                mm = pe.matmul(main[m][:, :], w[:, k, m * P:(m + 1) * P], src[:, k, :],
                                               start=(k == 0), stop=(k == HC - 1))
                                if k == HC - 1:
                                    mm.then_inc(s["p_h1" if layer == 0 else "p_h2"], 1)
                                if k % 2 == 1 and (layer, m) != (0, 0):
                                    rnn(2 if (layer, m) == (1, 3) else 1)
                            if layer == 0 and m == 0:
                                ranks()
                                recurrence_input()
                else:
                    ranks()
                    recurrence_input()
                rnn(STEPS)
                if r is not None:
                    wait(pe, s["step"], STEPS * (r + 1))
                    wait(pe, s["xn3T"], r + 1)
                    for k in range(CT):
                        m_ = pe.transpose(turn[:, k * P:(k + 1) * P], state[:, k * P:(k + 1) * P], ident[:])
                    m_.then_inc(s["p_state"], 1)
                if c is not None:
                    wait(pe, s["h3"], HC * (c + 1))
                    wait(pe, s["y"], c)
                    for k in range(CT):
                        for m in range(HC):
                            mm = pe.matmul(yp[:, k * P:(k + 1) * P], hT[2][:, m, k * P:(k + 1) * P],
                                           w3_sb[:, m, :], start=(m == 0), stop=(m == HC - 1))
                    mm.then_inc(s["p_y"], 1)

            rounds(pe, step)

        @block.scalar
        def _(act):
            act.wait_ge(s["const"], N_CONST)

            def step(p, c, r, q, par):
                slots = iter(range(STEPS))

                def rnn(n=1):
                    if r is not None:
                        for _ in range(n):
                            t = next(slots, None)
                            if t is not None:
                                wait(act, s["p_step"], STEPS * r + t + 1)
                                if t == 0:
                                    wait(act, s["p_state"], r)
                                act.activation(state[:, t * B:(t + 1) * B], xi[:, t * B:(t + 1) * B], ACT.Tanh,
                                               bias=bias[:]).then_inc(s["step"], 1)

                if c is not None:
                    wait(act, s["p_xn2T"], c + 1)
                    wait(act, s["p_g"], HC * c)
                    act.activation(xn2T[:], turn[:, :], ACT.Copy).then_inc(s["xn2T"], 1)
                    for m in range(HC):
                        wait(act, s["p_a"], HC * c + m + 1)
                        wait(act, s["ag"], HC * c + m - 1)
                        act.activation(th[m % 2][:], main[2 * m % 4][:, :], ACT.Tanh,
                                       scale=sc_half[:, m:m + 1]).then_inc(s["tanh"], 1)
                if q is not None:
                    wait(act, s["p_xn4T"], q + 1)
                    wait(act, s["p_logit"], q)
                    wait(act, s["kept"], q)
                    act.activation(xn4T[:], turn[:, :], ACT.Copy).then_inc(s["xn4T"], 1)
                    wait(act, s["top"], q + 1)
                    act.activation(tanh_top[:], top[:], ACT.Tanh, scale=0.5).then_inc(s["tanh_top"], 1)
                if r is not None:
                    wait(act, s["p_xn3T"], r + 1)
                    act.activation(xn3T[:], turn[:, :], ACT.Copy).then_inc(s["xn3T"], 1)
                if c is not None:
                    for layer, (pname, dst, done) in enumerate((("p_h1", hT[1], "h2"), ("p_h2", hT[2], "h3"))):
                        for m in range(HC):
                            wait(act, s[pname], HC * c + m + 1)
                            if layer == 1 and m == 0:
                                wait(act, s["p_y"], c)
                            act.activation(dst[:, m, :], main[m][:, :], ACT.Gelu,
                                           scale=sc[:, 2 + layer, m:m + 1]).then_inc(s[done], 1)
                            if (layer, m) == (1, 2):
                                rnn(2)
                                rnn(2)
                            elif (layer, m) == (1, 3):
                                pass
                            else:
                                rnn(2)
                rnn(STEPS)

            rounds(act, step)

        @block.vector
        def _(dve):
            dve.wait_ge(s["const"], N_CONST)

            def stats(n, tiles, c):
                for k in range(CT):
                    m = dve.bn_stats(stat[n][:, k, :], tiles(k))
                m.then_inc(s["stat" + n], 1)
                wait_apart(dve, s["stat" + n], c + 1, s["const"])
                for k in range(CT):
                    dve.bn_aggr(mv[n][:, k, :], stat[n][:, k, :]).then_inc(s["mv" + n], 1)

            def apply(n, out, tiles, done, c):
                wait(dve, s["rs" + n], c + 1)
                for k in range(CT):
                    m = dve.tensor_scalar(out[:, k, :], tiles(k), mv[n][:, k, 0:1], rs[n][:, k:k + 1],
                                          ALU.subtract, ALU.mult)
                m.then_inc(s[done], 1)
                dve.wait_ge(s[done], c + 1)

            def step(p, c, r, q, par):
                if c is not None:
                    for m in range(HC):
                        wait(dve, s["tanh"], HC * c + m + 1)
                        dve.scalar_tensor_tensor(out=ag[m % 2][:], in0=th[m % 2][:], scalar=1.0,
                                                 in1=main[2 * m % 4][:, :], op0=ALU.add,
                                                 op1=ALU.mult).then_inc(s["ag"], 1)
                        wait(dve, s["p_g"], HC * c + m + 1)
                        wait(dve, s["p_h1"], HC * c)
                        dve.wait_ge(s["ag"], HC * c + m + 1)
                        dve.scalar_tensor_tensor(out=hT[0][:, m, :], in0=main[(2 * m + 1) % 4][:, :],
                                                 scalar=sc_prod[:, m:m + 1], in1=ag[m % 2][:], op0=ALU.mult,
                                                 op1=ALU.mult).then_inc(s["h1"], 1)
                if q is not None:
                    lg = route[:, 0:CT * E].rearrange("p (k e) -> p k e", e=E)

                    def wide(col):
                        return col[:].rearrange("p (k o) -> p k o", o=1).to_broadcast([P, CT, E])
                    wait(dve, s["p_logit"], q + 1)
                    wait(dve, s["tanh_top"], q)
                    dve.tensor_reduce(top[:], lg, AX.X, ALU.max).then_inc(s["top"], 1)
                    dve.wait_ge(s["top"], q + 1)
                    dve.tensor_tensor(is_top[:], lg, wide(top), ALU.is_ge).then_inc(s["is_top"], 1)
                    dve.wait_ge(s["is_top"], q + 1)
                    dve.tensor_tensor(rtop[:], is_top[:], rev[:].rearrange("p (o e) -> p o e", o=1)
                                      .to_broadcast([P, CT, E]), ALU.mult).then_inc(s["rtop"], 1)
                    dve.wait_ge(s["rtop"], q + 1)
                    dve.tensor_reduce(first[:], rtop[:], AX.X, ALU.max).then_inc(s["first"], 1)
                    dve.wait_ge(s["first"], q + 1)
                    wait(dve, s["p_rank"], q)
                    wait(dve, s["pre_oh"], q)
                    dve.tensor_tensor(onehot[:], rtop[:], wide(first), ALU.is_equal).then_inc(s["onehot"], 1)
                    dve.wait_ge(s["onehot"], q + 1)
                    dve.tensor_copy(part(oh_all, q, CT), onehot[:])
                    dve.tensor_copy(part(xn4T_all, q, CHUNK), xn4T[:]).then_inc(s["kept"], 1)
                    dve.wait_ge(s["tanh_top"], q + 1)
                    dve.tensor_scalar(gate_val[:], tanh_top[:], 0.5, 0.5, ALU.mult, ALU.add)\
                       .then_inc(s["gate_val"], 1)
                    dve.wait_ge(s["gate_val"], q + 1)
                    dve.tensor_tensor(part(xs_all, q, CT), xn4[:], gate_val[:].rearrange("p (k o) -> p k o", o=1)
                                      .to_broadcast([P, CT, D]), ALU.mult).then_inc(s["xs"], 1)
                if p is not None:
                    wait(dve, s[f"xc{par}"], 8 * (p - par) + 16)
                    stats("f", lambda k: x1c[par][:, k, :], p)
                    wait(dve, s["p_xn2T"], p)
                    apply("f", xn2, lambda k: x1c[par][:, k, :], "xn2", p)
                if q is not None:
                    wait(dve, s["p_rank"], q + 1)
                    cnt = counts[:].rearrange("p (o e) -> p o e", o=1).to_broadcast([P, CT, E])
                    dve.wait_ge(s["onehot"], q + 1)
                    wait(dve, s["counts"], q)
                    dve.tensor_tensor(pre[:], route[:, 128:128 + CT * E].rearrange("p (k e) -> p k e", e=E), cnt,
                                      ALU.add).then_inc(s["pre"], 1)
                    dve.wait_ge(s["pre"], q + 1)
                    dve.tensor_tensor(counts[:], counts[:], route[:, 256:256 + E], ALU.add)\
                       .then_inc(s["counts"], 1)
                    dve.tensor_tensor(pre_oh[:], pre[:], onehot[:], ALU.mult).then_inc(s["pre_oh"], 1)
                    dve.wait_ge(s["pre_oh"], q + 1)
                    dve.tensor_reduce(part(rank_all, q, CT), pre_oh[:], AX.X, ALU.add).then_inc(s["rank"], 1)
                if r is not None:
                    wait(dve, s["p_state"], r + 1)
                    stats("h", lambda k: turn[:, k * P:(k + 1) * P], r)
                    apply("h", hn, lambda k: turn[:, k * P:(k + 1) * P], "hn", r)
                    wait(dve, s["x3_out"], 16 * r)
                    dve.tensor_tensor(x3[:], hn[:], x2[par][:], ALU.add).then_inc(s["x3"], 1)
                    dve.wait_ge(s["x3"], r + 1)
                    stats("e", lambda k: x3[:, k, :], r)
                    wait(dve, s["xs"], r)
                    wait(dve, s["p_xn4T"], r)
                    apply("e", xn4, lambda k: x3[:, k, :], "xn4", r)
                if c is not None:
                    wait(dve, s["p_y"], c + 1)
                    dve.tensor_tensor(y[:], yp[:, :].rearrange("p (k d) -> p k d", d=D),
                                      w3s[:].rearrange("p (o d) -> p o d", o=1).to_broadcast([P, CT, D]),
                                      ALU.mult).then_inc(s["y"], 1)
                    dve.wait_ge(s["y"], c + 1)
                    stats("y", lambda k: y[:, k, :], c)
                    apply("y", yn, lambda k: y[:, k, :], "yn", c)
                    wait(dve, s["x3"], c - 1)
                    dve.tensor_tensor(x2[1 - par][:], yn[:], x1c[1 - par][:], ALU.add).then_inc(s["x2"], 1)
                    dve.wait_ge(s["x2"], c + 1)
                    stats("x", lambda k: x2[1 - par][:, k, :], c)
                    wait(dve, s["p_xn3T"], c)
                    apply("x", xn3, lambda k: x2[1 - par][:, k, :], "xn3", c)

            rounds(dve, step)


I = 256
IC = I // P
SLOTS = NT + E
OFF = P.bit_length() - 1


def experts_layer(nc, x3_d, sorted_d, routed_d, shared_d, gate_up, down, sh_gate_up, sh_down, out, keep):
    with ExitStack() as ctx:
        def sb(name, shape, dt=F32):
            return ctx.enter_context(nc.sbuf_tensor(name, shape, dt))

        def ps(name, shape, dt=F32):
            return ctx.enter_context(nc.psum_tensor(name, shape, dt))

        def sem(name):
            return ctx.enter_context(nc.semaphore(name))

        xn4T_all, xs_all, oh_all, rank_all, counts = keep
        position = sb("position", [P, NT], I32)
        ident = sb("ident3", [P, P])
        pow_half = sb("pow_half3", [P, CT])
        col = sb("col", [P, 1])
        expert = sb("expert", [1, SLOTS], I32)
        wgu = sb("wgu", [P, E, 2 * I])
        wd = sb("wd", [P, E, IC, D])
        sgu = sb("sgu", [P, 2 * I])
        sd = sb("sd", [P, IC, D])
        full = sb("full", [P, E])
        full_i = sb("full_i", [P, E], I32)
        tiles_i = sb("tiles_i", [P, E], I32)
        tiles = sb("tiles", [P, E])
        upto = sb("upto", [P, E])
        start0 = sb("start0", [P, E])
        start = sb("start", [P, E])
        own = sb("own", [P, 16, E])
        own_start = sb("own_start", [P, NT])
        behind = sb("behind", [P, E])
        owner0 = sb("owner0", [P, 1])
        ones_e = sb("ones_e", [P, E])
        owner = sb("owner", [P, 1])
        silu = [sb(f"silu{i}", [P, CHUNK]) for i in range(2)]
        hid = sb("hid", [P, IC, CHUNK])
        sh = sb("sh", [P, CT, D])
        xg = [sb(f"xg{i}", [P, D]) for i in range(2)]
        xgT = [sb(f"xgT{i}", [P, P]) for i in range(2)]
        act_g = [sb(f"act_g{i}", [P, I]) for i in range(2)]
        hid_g = [sb(f"hid_g{i}", [P, I]) for i in range(2)]
        hid_gT = [sb(f"hid_gT{i}", [P, I]) for i in range(2)]
        yg = [sb(f"yg{i}", [P, D]) for i in range(2)]
        rt = sb("rt", [P, CT, D])
        shl = sb("shl", [P, CT, D])
        x3l = sb("x3l", [P, CT, D])
        ysum = sb("ysum", [P, CT, D])
        stat = sb("cstat", [P, CT, 6])
        mv = sb("cmv", [P, CT, 2])
        ve = sb("cve", [P, CT])
        rs = sb("crs", [P, CT])
        yn = sb("yn4", [P, CT, D])
        res = sb("res", [P, CT, D])

        bank = [ps(f"bank{i}", [P, 512]) for i in range(8)]

        names = ("wsh", "wex", "const", "full", "full_i", "tiles_i", "tiles", "upto", "start0", "start", "own", "own_start",
                 "position", "behind", "owner0", "owner", "p_owner", "expert", "p_g", "p_u", "silu", "hid", "p_sh",
                 "sh", "sh_out", "placed", "xg0", "xg1", "p_xgT", "xgT", "p_gu", "act_g", "hid_g", "p_hT",
                 "hid_gT", "p_yg", "yg", "yg_out0", "yg_out1", "rt", "shl", "x3l", "ysum", "stat", "mv", "ve", "rs", "yn",
                 "res", "out")
        s = {name: sem("c_" + name) for name in names}
        N_CONST = 5
        ctx.callback(clear, nc, list(s.values()))
        block = ctx.enter_context(nc.Block())

        sorted_t = sorted_d.rearrange("(j p) d -> j p d", p=P)
        routed_t = routed_d.rearrange("(j p) d -> j p d", p=P)
        shared_c = shared_d.rearrange("(c k p) d -> c p k d", k=CT, p=P)
        x3_c = x3_d.rearrange("(c k p) d -> c p k d", k=CT, p=P)
        out_v = out.rearrange("b (c k u) d -> c k u b d", k=CT, u=P // B)

        def tile_of(ap, j):
            return ap[j] if isinstance(j, int) else ap[bass.ds(j, 1)].rearrange("o p d -> (o p) d")

        def chunk_of(ap, c):
            return ap[c] if isinstance(c, int) else ap[bass.ds(c, 1)].rearrange("o p k d -> p (o k) d")

        def slot_rounds(eng, step):
            step(0, None, None, 0)
            step(1, 0, None, 1)
            step(2, 1, 0, 0)
            step(3, 2, 1, 1)
            with eng.Fori(0, (SLOTS - 4) // 2) as i:
                for par in range(2):
                    j = 2 * i + (4 + par)
                    step(j, j - 1, j - 2, par)
            step(None, SLOTS - 1, SLOTS - 2, 0)
            step(None, None, SLOTS - 1, 1)

        @block.sync
        def _(sp):
            sp.dma_start(sgu[:], sh_gate_up).then_inc(s["wsh"], 16)
            sp.dma_start(sd[:], sh_down.rearrange("(c p) d -> p c d", p=P)).then_inc(s["wsh"], 16)
            for e in range(0, E, 8):
                sp.dma_start(wgu[:, e:e + 8, :], gate_up[e:e + 8].rearrange("e d i -> d e i")).then_inc(s["wex"], 16)
                sp.dma_start(wd[:, e:e + 8], down[e:e + 8].rearrange("e (c p) d -> p e c d", p=P))\
                  .then_inc(s["wex"], 16)
            with sp.Fori(0, NC) as c:
                sp.wait_ge(s["sh"], c + 1)
                sp.dma_start(chunk_of(shared_c, c), sh[:]).then_inc(s["sh_out"], 16)
            sp.wait_ge(s["placed"], 16 * NT)

            def step(a, g, d, par):
                if a is not None:
                    wait(sp, s["p_xgT"], a - 1)
                    sp.dma_start(xg[par][:], tile_of(sorted_t, a)).then_inc(s[f"xg{par}"], 16)
                if d is not None:
                    wait(sp, s["yg"], d + 1)
                    sp.dma_start(tile_of(routed_t, d), yg[par][:])\
                      .then_inc(s[f"yg_out{par}"], 16)

            slot_rounds(sp, step)
            sp.wait_ge(s["sh_out"], 16 * NC)

            def last(c):
                wait(sp, s["ysum"], c)
                sp.dma_start(shl[:], chunk_of(shared_c, c)).then_inc(s["shl"], 16)
                wait(sp, s["res"], c)
                sp.dma_start(x3l[:], chunk_of(x3_c, c)).then_inc(s["x3l"], 16)
                wait(sp, s["res"], c + 1)
                for k in range(CT):
                    for u in range(P // B):
                        dst = out_v[c, k, u] if isinstance(c, int) else out_v[bass.ds(c, 1), k, u]\
                            .rearrange("o b d -> (o b) d")
                        sp.dma_start(dst, res[u * B:(u + 1) * B, k, :]).then_inc(s["out"], 16)
            last(0)
            with sp.Fori(0, NC - 1) as c:
                last(c + 1)
            sp.wait_ge(s["out"], 16 * NC * CT * (P // B))

        @block.gpsimd
        def _(pool):
            def const(ins):
                const.n += 1
                ins.then_inc(s["const"], 1)
                pool.wait_ge(s["const"], const.n)
            const.n = 0
            const(pool.memset(ident[:], 0.0))
            const(pool.affine_select(out=ident[:], in_=ident[:], compare_op=ALU.not_equal, fill=1.0, base=0,
                                     pattern=[[-1, P]], channel_multiplier=1))
            const(pool.memset(pow_half[:], -0.5))
            const(pool.memset(ones_e[:], 1.0))
            const(pool.iota(col[:], pattern=[[0, 1]], base=0, channel_multiplier=1,
                            allow_small_or_imprecise_dtypes=True))
            pool.wait_ge(s["position"], 1)
            for k in range(NT):
                pool.indirect_dma_start(out=sorted_d[:, :], out_offset=bass.IndirectOffsetOnAxis(
                    ap=position[:, k:k + 1], axis=0), in_=xs_all[:, k, :], in_offset=None)\
                    .then_inc(s["placed"], 16)
            pool.wait_ge(s["placed"], 16 * NT)
            for par in range(2):
                pool.wait_ge(s[f"yg_out{par}"], 8 * SLOTS)

            def last(c):
                for k in range(CT):
                    if k == 0:
                        wait(pool, s["ysum"], c)
                    pool.indirect_dma_start(out=rt[:, k, :], out_offset=None, in_=routed_d[:, :],
                                            in_offset=bass.IndirectOffsetOnAxis(
                                                ap=position[:, c * CT + k:c * CT + k + 1], axis=0))\
                        .then_inc(s["rt"], 16)
                wait_apart(pool, s["mv"], CT * (c + 1), s["const"])
                pool.tensor_scalar(ve[:], mv[:, :, 1], 1.0, EPS, ALU.mult, ALU.add).then_inc(s["ve"], 1)
                wait_apart(pool, s["ve"], c + 1, s["const"])
                pool.tensor_tensor(rs[:], ve[:], pow_half[:], ALU.pow).then_inc(s["rs"], 1)
            for c in range(NC):
                last(c)

        @block.tensor
        def _(pe):
            pe.wait_ge(s["wsh"], 32)
            pe.wait_ge(s["const"], N_CONST)
            pe.wait_ge(s["owner"], 1)
            pe.matmul(bank[7][0:1, 0:SLOTS], owner[:], ident[:, 0:SLOTS], start=True, stop=True)\
              .then_inc(s["p_owner"], 1)

            def shared(c):
                for m in range(IC):
                    wait(pe, s["hid"], IC * c + m - 1)
                    pe.matmul(bank[2 * m][:, :], sgu[:, m * P:(m + 1) * P], part(xn4T_all, c, CHUNK),
                              start=True, stop=True).then_inc(s["p_g"], 1)
                    pe.matmul(bank[2 * m + 1][:, :], sgu[:, I + m * P:I + (m + 1) * P], part(xn4T_all, c, CHUNK),
                              start=True, stop=True).then_inc(s["p_u"], 1)
                wait(pe, s["hid"], IC * (c + 1))
                wait(pe, s["sh"], c)
                for k in range(CT):
                    for m in range(IC):
                        mm = pe.matmul(bank[4][:, k * P:(k + 1) * P], hid[:, m, k * P:(k + 1) * P], sd[:, m, :],
                                       start=(m == 0), stop=(m == IC - 1))
                mm.then_inc(s["p_sh"], 1)
            shared(0)
            with pe.Fori(0, NC - 1) as c:
                shared(c + 1)

            pe.wait_ge(s["wex"], 16 * (E // 4))
            pe.wait_ge(s["expert"], 1)
            pe.wait_ge(s["sh"], NC)

            def step(a, g, d, par):
                if d is not None:
                    wait(pe, s["hid_g"], d + 1)
                    wait(pe, s["hid_gT"], d)
                    for m in range(IC):
                        mm = pe.transpose(bank[2][:, m * P:(m + 1) * P], hid_g[par][:, m * P:(m + 1) * P], ident[:])
                    mm.then_inc(s["p_hT"], 1)
                if a is not None:
                    wait(pe, s[f"xg{par}"], 8 * (a - par) + 16)
                    wait(pe, s["xgT"], a)
                    pe.transpose(bank[3][:, 0:P], xg[par][:], ident[:]).then_inc(s["p_xgT"], 1)
                if g is not None:
                    e = pe.value_load(expert[0:1, g:g + 1] if isinstance(g, int)
                                      else expert[0:1, bass.ds(g, 1)], min_val=0, max_val=E - 1)
                    wait(pe, s["xgT"], g + 1)
                    wait(pe, s["hid_g"], g - 1)
                    pe.matmul(bank[1 - par][:, :], xgT[1 - par][:],
                              wgu[:, bass.ds(e, 1), :].rearrange("p o i -> p (o i)"),
                              start=True, stop=True).then_inc(s["p_gu"], 1)
                if d is not None:
                    e = pe.value_load(expert[0:1, d:d + 1] if isinstance(d, int)
                                      else expert[0:1, bass.ds(d, 1)], min_val=0, max_val=E - 1)
                    wait(pe, s["hid_gT"], d + 1)
                    wait(pe, s["yg"], d - 1)
                    for m in range(IC):
                        mm = pe.matmul(bank[5 + par][:, 0:D], hid_gT[par][:, m * P:(m + 1) * P],
                                       wd[:, bass.ds(e, 1), m, :].rearrange("p o d -> p (o d)"),
                                       start=(m == 0), stop=(m == IC - 1))
                    mm.then_inc(s["p_yg"], 1)

            slot_rounds(pe, step)

        @block.scalar
        def _(act):
            def shared(c):
                for m in range(IC):
                    wait(act, s["p_g"], IC * c + m + 1)
                    wait(act, s["hid"], IC * c + m - 1)
                    act.activation(silu[m][:], bank[2 * m][:, :], ACT.Silu).then_inc(s["silu"], 1)
                wait(act, s["p_sh"], c + 1)
                wait(act, s["sh_out"], 16 * c)
                act.activation(sh[:].rearrange("p k d -> p (k d)"), bank[4][:, :], ACT.Copy).then_inc(s["sh"], 1)
            shared(0)
            with act.Fori(0, NC - 1) as c:
                shared(c + 1)

            def step(a, g, d, par):
                if d is not None:
                    wait(act, s["p_hT"], d + 1)
                    wait(act, s["p_yg"], d - 1)
                    act.activation(hid_gT[par][:], bank[2][:, 0:I], ACT.Copy).then_inc(s["hid_gT"], 1)
                if g is not None:
                    wait(act, s["p_gu"], g + 1)
                    wait(act, s["hid_g"], g - 1)
                    act.activation(act_g[1 - par][:], bank[1 - par][:, 0:I], ACT.Silu).then_inc(s["act_g"], 1)

            slot_rounds(act, step)

        @block.vector
        def _(dve):
            dve.wait_ge(s["const"], N_CONST)

            def did(ins, name):
                ins.then_inc(s[name], 1)
                dve.wait_ge(s[name], 1)
            did(dve.tensor_scalar(full[:], counts[:], float(P - 1), None, ALU.add), "full")
            did(dve.tensor_copy(full_i[:], full[:]), "full_i")
            did(dve.tensor_single_scalar(tiles_i[:], full_i[:], OFF, ALU.arith_shift_right), "tiles_i")
            did(dve.tensor_copy(tiles[:], tiles_i[:]), "tiles")
            did(dve.tensor_tensor_scan(out=upto[:], data0=ones_e[:], data1=tiles[:], initial=0.0, op0=ALU.mult,
                                       op1=ALU.add), "upto")
            did(dve.tensor_tensor(start0[:], upto[:], tiles[:], ALU.subtract), "start0")
            did(dve.tensor_scalar(start[:], start0[:], float(P), None, ALU.mult), "start")
            did(dve.tensor_scalar(behind[:], upto[:], col[:, 0:1], None, ALU.is_le), "behind")
            did(dve.tensor_reduce(owner0[:], behind[:], AX.X, ALU.add), "owner0")
            did(dve.tensor_scalar(owner[:], owner0[:], float(E - 1), None, ALU.min), "owner")
            for k in range(0, NT, 16):
                dve.tensor_tensor(own[:], oh_all[:, k:k + 16, :], start[:].rearrange("p (o e) -> p o e", o=1)
                                  .to_broadcast([P, 16, E]), ALU.mult).then_inc(s["own"], 1)
                dve.wait_ge(s["own"], k // 16 + 1)
                dve.tensor_reduce(own_start[:, k:k + 16], own[:], AX.X, ALU.add).then_inc(s["own_start"], 1)
                dve.wait_ge(s["own_start"], k // 16 + 1)
            did(dve.tensor_tensor(position[:], own_start[:], rank_all[:], ALU.add), "position")
            dve.wait_ge(s["p_owner"], 1)
            did(dve.tensor_copy(expert[:], bank[7][0:1, 0:SLOTS]), "expert")

            def shared(c):
                for m in range(IC):
                    wait(dve, s["silu"], IC * c + m + 1)
                    wait(dve, s["p_u"], IC * c + m + 1)
                    wait(dve, s["p_sh"], c)
                    dve.tensor_tensor(hid[:, m, :], bank[2 * m + 1][:, :], silu[m][:], ALU.mult)\
                       .then_inc(s["hid"], 1)
            shared(0)
            with dve.Fori(0, NC - 1) as c:
                shared(c + 1)

            def step(a, g, d, par):
                if a is not None:
                    wait(dve, s["p_xgT"], a + 1)
                    wait(dve, s["p_gu"], a - 1)
                    dve.tensor_copy(xgT[par][:], bank[3][:, 0:P]).then_inc(s["xgT"], 1)
                if g is not None:
                    wait(dve, s["act_g"], g + 1)
                    wait(dve, s["p_hT"], g - 1)
                    dve.tensor_tensor(hid_g[1 - par][:], bank[1 - par][:, I:2 * I], act_g[1 - par][:], ALU.mult)\
                       .then_inc(s["hid_g"], 1)
                if d is not None:
                    wait(dve, s["p_yg"], d + 1)
                    wait(dve, s[f"yg_out{par}"], 8 * (d - par))
                    dve.tensor_copy(yg[par][:], bank[5 + par][:, 0:D]).then_inc(s["yg"], 1)

            slot_rounds(dve, step)

            def last(c):
                wait(dve, s["rt"], 16 * CT * (c + 1))
                wait(dve, s["shl"], 16 * (c + 1))
                dve.tensor_tensor(ysum[:], rt[:], shl[:], ALU.add).then_inc(s["ysum"], 1)
                dve.wait_ge(s["ysum"], c + 1)
                for k in range(CT):
                    m = dve.bn_stats(stat[:, k, :], ysum[:, k, :])
                m.then_inc(s["stat"], 1)
                wait_apart(dve, s["stat"], c + 1, s["const"])
                for k in range(CT):
                    dve.bn_aggr(mv[:, k, :], stat[:, k, :]).then_inc(s["mv"], 1)
                wait(dve, s["rs"], c + 1)
                for k in range(CT):
                    m = dve.tensor_scalar(yn[:, k, :], ysum[:, k, :], mv[:, k, 0:1], rs[:, k:k + 1],
                                          ALU.subtract, ALU.mult)
                m.then_inc(s["yn"], 1)
                dve.wait_ge(s["yn"], c + 1)
                wait(dve, s["x3l"], 16 * (c + 1))
                wait(dve, s["out"], 16 * CT * (P // B) * c)
                dve.tensor_tensor(res[:], yn[:], x3l[:], ALU.add).then_inc(s["res"], 1)
            last(0)
            with dve.Fori(0, NC - 1) as c:
                last(c + 1)


def build(nc, t, out):
    def dram(name, shape):
        return nc.dram_tensor(name, shape, F32).ap()

    x1_d = dram("x1_d", (T, B, D))
    x3_d = dram("x3_d", (T * B, D))
    sorted_d = dram("sorted_d", (SLOTS * P, D))
    routed_d = dram("routed_d", (SLOTS * P, D))
    shared_d = dram("shared_d", (T * B, D))
    attention_layer(nc, t["x"], t["w_qk"], t["w_v"], t["w_rot"], t["w_out"], t["bonus0"], t["bonus1"], x1_d)
    with ExitStack() as ctx:
        def sb(name, shape, dt=F32):
            return ctx.enter_context(nc.sbuf_tensor(name, shape, dt))
        keep = (sb("xn4T_all", [P, NT * P]), sb("xs_all", [P, NT, D]), sb("oh_all", [P, NT, E], BF16),
                sb("rank_all", [P, NT]), sb("counts", [P, E]))
        mixing_layers(nc, x1_d, x3_d, t["w1"], t["w2"], t["h1"], t["h2"], t["w3"], t["scales"], t["w3_s"],
                      t["wi"], t["wh"], t["rnn_bias"], t["gate"], sorted_d, keep)
        experts_layer(nc, x3_d, sorted_d, routed_d, shared_d, t["gate_up"], t["down"], t["sh_gate_up"],
                      t["sh_down"], out, keep)


def host_layout(np, i):
    w_rot = np.zeros((P, P), np.float32)
    for h in range(HEADS):
        q = slice(DH * h, DH * (h + 1))
        k = slice(DH * (HEADS + h), DH * (HEADS + h + 1))
        w_rot[q, q] = i["L0_attn_W_nudge"][h]
        w_rot[k, k] = i["L0_attn_simple_roots"].T
    bonus = i["L0_attn_chamber_bonus"].reshape(1, HEADS, 8, 2)
    return {
        "x": i["L0_attn_x"],
        "w_qk": np.concatenate([i["L0_attn_W_q"].T, i["L0_attn_W_k"].T], 1),
        "w_v": i["L0_attn_W_v"].T,
        "w_rot": w_rot,
        "w_out": i["L0_attn_W_out"].T,
        "bonus0": bonus[..., 0],
        "bonus1": bonus[..., 1],
        "w1": i["L0_ffn_w1_w"].T,
        "w2": i["L0_ffn_w2_w"].T,
        "h1": i["L0_ffn_h1_w"].T,
        "h2": i["L0_ffn_h2_w"].T,
        "w3": i["L0_ffn_w3_w"].T,
        "scales": np.stack([i[f"L0_ffn_{k}_s"].reshape(HC, P) for k in ("w1", "w2", "h1", "h2")]).transpose(2, 0, 1),
        "w3_s": i["L0_ffn_w3_s"].reshape(1, D),
        "wi": i["L1_attn_Wi"].T,
        "wh": i["L1_attn_Wh"].T,
        "rnn_bias": np.stack([i["L1_attn_bi"], i["L1_attn_bh"]], 1),
        "gate": i["L1_ffn_gate_w"],
        "sh_gate_up": np.concatenate([i["L1_ffn_shared_gate_w"], i["L1_ffn_shared_up_w"]], 1),
        "sh_down": i["L1_ffn_shared_down_w"],
        "gate_up": np.concatenate([i["L1_ffn_routed_gate_w"], i["L1_ffn_routed_up_w"]], 2),
        "down": i["L1_ffn_routed_down_w"],
    }


def kernel(**inputs):
    import numpy as np
    import concourse.bacc as bacc
    from concourse.bass_utils import run_bass_kernel_spmd

    nc = bacc.Bacc("TRN2", target_bir_lowering=False, num_devices=1)
    arrays, tensors = {}, {}
    for name, a in host_layout(np, {k: np.asarray(v) for k, v in inputs.items()}).items():
        a = np.ascontiguousarray(a)
        arrays[f"in_{name}"] = a
        tensors[name] = nc.dram_tensor(f"in_{name}", a.shape, mybir.dt.from_np(a.dtype), kind="ExternalInput").ap()
    out = nc.dram_tensor("out_0", (B, T, D), F32, kind="ExternalOutput").ap()
    build(nc, tensors, out)
    r = run_bass_kernel_spmd(nc, [arrays], core_ids=[0])
    return r.results[0]["out_0"]
```

```python
from contextlib import ExitStack

import concourse.bass as bass
from concourse import mybir

F32 = mybir.dt.float32
F32R = mybir.dt.float32r
BF16 = mybir.dt.bfloat16
I32 = mybir.dt.int32
ALU = mybir.AluOpType
ACT = mybir.ActivationFunctionType
AX = mybir.AxisListType

P = 128
B, T, D = 32, 256, 128
HEADS, DH, DV = 16, 4, 64
TT = T // P
GH = 4
GROUPS = HEADS // GH
AUG = 32
SC = 384
EPS = 1e-5
NORM_MIN2 = 1e-24
MASKED = -1e38
MAGIC = 0x5f3759df
RING = 8
PAIRS_A = HEADS // 2
BANKS = 2


def wait(eng, sem, value):
    if isinstance(value, int) and value <= 0:
        return
    eng.wait_ge(sem, value)


def wait_apart(eng, sem, value, done):
    if not isinstance(value, int):
        value = eng.snap(eng.to_reg(value))
        eng.wait_ge(done, 1)
    wait(eng, sem, value)


def clear(nc, sems):
    with nc.Block() as block:
        @block.gpsimd
        def _(pool):
            for sem in sems:
                pool.sem_clear(sem)


def attention_layer(nc, x, w_qk, w_v, w_rot, w_out, bonus0, bonus_step, x1_d):
    with ExitStack() as ctx:
        def sb(name, shape, dt=F32):
            return ctx.enter_context(nc.sbuf_tensor(name, shape, dt))

        def ps(name, shape, dt=F32):
            return ctx.enter_context(nc.psum_tensor(name, shape, dt))

        def sem(name):
            return ctx.enter_context(nc.semaphore(name))

        ident = sb("ident", [P, P])
        ident_b = sb("ident_b", [P, P], BF16)
        wqk = sb("wqk", [P, 2 * HEADS * DH])
        wv = sb("wv", [P, HEADS * DV])
        wrot = sb("wrot", [P, P])
        wout = sb("wout", [P, HEADS * DV // P, D])
        bon0 = sb("bon0", [P, HEADS, 8])
        bond = sb("bond", [P, HEADS, 8])
        pick = sb("pick", [P, GROUPS, AUG])
        back_to = sb("back_to", [P, PAIRS_A, 2, DV])
        mask_b = sb("mask_b", [P, P], BF16)
        mask_f = sb("mask_f", [P, P])
        pow_half = sb("pow_half", [P, TT])
        xa = sb("xa", [P, TT, D])
        stat_a = sb("stat_a", [P, TT, 6])
        mv_a = sb("mv_a", [P, TT, 2])
        ve_a = sb("ve_a", [P, TT])
        rstd_a = sb("rstd_a", [P, TT])
        xn = sb("xn", [P, TT, D])
        xnT = [sb(f"xnT{i}", [P, T]) for i in range(2)]
        sq1 = sb("sq1", [P, TT * 2 * HEADS, DH])
        ss1 = sb("ss1", [P, TT * 2 * HEADS])
        ssg1 = sb("ssg1", [P, TT * 2 * HEADS])
        r1 = [sb(f"r1_{i}", [P, TT * 2 * HEADS]) for i in range(4)]
        nt1 = sb("nt1", [P, TT * 2 * HEADS])
        nu1 = sb("nu1", [P, TT * 2 * HEADS])
        qkn = sb("qkn", [P, TT, 2 * HEADS, DH])
        qkT = sb("qkT", [P, T])
        sq2 = sb("sq2", [P, TT, HEADS, DH])
        ss2 = sb("ss2", [P, TT, HEADS])
        ssg2 = sb("ssg2", [P, TT, HEADS])
        r2 = [sb(f"r2_{i}", [P, TT, HEADS]) for i in range(4)]
        nt2 = sb("nt2", [P, TT, HEADS])
        nu2 = sb("nu2", [P, TT, HEADS])
        qraw = sb("qraw", [P, TT, HEADS, DH])
        ek = sb("ek", [P, TT, HEADS, DH])
        ek1 = sb("ek1", [P, TT, HEADS, DH])
        sg = sb("sg", [P, TT, HEADS, DH])
        bt = [sb(f"bt{i}", [P, TT, HEADS, 8 >> i]) for i in range(4)]
        bv = [sb(f"bv{i}", [P, TT, HEADS, 8 >> i]) for i in range(3)]
        q5 = sb("q5", [P, TT, HEADS, DH + 1])
        k5 = sb("k5", [P, TT, HEADS, DH + 1])
        rest = [sb(f"rest{i}", [P, TT * HEADS * (DH + 1)]) for i in range(4)]
        q_part = sb("q_part", [P, 3, TT * HEADS, DH + 1], BF16)
        k_part = sb("k_part", [P, 3, TT * HEADS, DH + 1], BF16)
        q_aug = sb("q_aug", [P, TT * HEADS, AUG], BF16)
        k_aug = sb("k_aug", [P, TT * HEADS, AUG], BF16)
        q_augT = [sb(f"q_augT{i}", [P, GROUPS, T], BF16) for i in range(2)]
        k_augT = [sb(f"k_augT{i}", [P, GROUPS, T], BF16) for i in range(2)]
        bonT = sb("bonT", [HEADS, T])
        cmax = sb("cmax", [HEADS, T])
        val = [sb(f"val{i}", [P, TT, HEADS, DV]) for i in range(2)]
        prob = sb("prob", [P, RING, SC])
        onT = [sb(f"onT{i}", [P, PAIRS_A, T]) for i in range(2)]
        rec = sb("rec", [P, T])
        y_sb = sb("y_sb", [P, TT * D])
        xr = sb("xr", [P, TT, D])
        stat_y = sb("stat_y", [P, TT, 6])
        mv_y = sb("mv_y", [P, TT, 2])
        ve_y = sb("ve_y", [P, TT])
        rstd_y = sb("rstd_y", [P, TT])
        yn = sb("yn", [P, TT, D])
        x1 = sb("x1", [P, TT, D])

        score = [ps(f"score{j}", [P, 512]) for j in range(BANKS)]
        outp = ps("outp", [P, 2, T])
        total = ps("total", [P, 512])
        spread = ps("spread", [P, 2, T])
        front = ps("front", [P, 512])
        turned = ps("turned", [P, 512])
        turned_b = turned[:, :].bitcast(BF16)
        back = ps("back", [P, 512])

        names = ("w", "const", "xa", "stat_a", "mv_a", "ve_a", "rstd_a", "xn", "p_xnT", "xnT", "p_qk", "sq1", "ss1",
                 "ssg1", "rsq1", "qkn", "p_qkT", "qkT", "p_rot", "sq2", "ek", "qraw", "ss2", "ssg2", "rsq2", "ek1",
                 "sg", "q4", "kcopy", "bon", "p_bonT", "bonT", "cmax", "p_cmax", "q5", "ksplit", "qsplit", "kaug",
                 "qaug", "p_kaT", "p_qaT", "kaT", "qaT", "p_v", "val", "p_score", "prob", "p_out", "raw", "p_sum", "rec", "p_bc", "onT", "p_y",
                 "y", "stat_y", "mv_y", "ve_y", "rstd_y", "yn", "xr", "x1", "x1_out")
        s = {name: sem("a_" + name) for name in names}

        STEPS_K = 5
        BON = 11
        RSQ = 10
        N_CONST = 27

        ctx.callback(clear, nc, list(s.values()))
        block = ctx.enter_context(nc.Block())

        def rounds(eng, step):
            def row(b):
                return [v if 0 <= v < B else None for v in (b, b + 1, b + 2, b + 3, b - 1, b - 2)] + [b % 2]
            for b in range(-3, 3):
                step(*row(b))
            with eng.Fori(0, (B - 6) // 2) as i:
                for k in range(2):
                    b = 2 * i + (3 + k)
                    step(b, b + 1, b + 2, b + 3, b - 1, b - 2, 1 - k)
            for b in range(B - 3, B + 2):
                step(*row(b))

        @block.sync
        def _(sp):
            for dst, src in ((wqk[:], w_qk), (wv[:], w_v), (wrot[:], w_rot),
                             (wout[:], w_out.rearrange("(c p) d -> p c d", p=P)),
                             (bon0[:], bonus0.to_broadcast([P, HEADS, 8])),
                             (bond[:], bonus_step.to_broadcast([P, HEADS, 8]))):
                sp.dma_start(dst, src).then_inc(s["w"], 16)

            def step(b, f, n, m, z, y, par):
                if m is not None:
                    wait(sp, s["xn"], m)
                    sp.dma_start(xa[:], x[m].rearrange("(i p) d -> p i d", p=P) if isinstance(m, int)
                                 else x[bass.ds(m, 1)].rearrange("o (i p) d -> p (o i) d", p=P)).then_inc(s["xa"], 16)
                if y is not None:
                    wait(sp, s["x1"], y)
                    sp.dma_start(xr[:], x[y].rearrange("(i p) d -> p i d", p=P) if isinstance(y, int)
                                 else x[bass.ds(y, 1)].rearrange("o (i p) d -> p (o i) d", p=P)).then_inc(s["xr"], 16)
                    wait(sp, s["x1"], y + 1)
                    sp.dma_start(x1_d[:, y, :].rearrange("(i p) d -> p i d", p=P) if isinstance(y, int)
                                 else x1_d[:, bass.ds(y, 1), :].rearrange("(i p) o d -> p (i o) d", p=P),
                                 x1[:]).then_inc(s["x1_out"], 16)

            rounds(sp, step)
            sp.wait_ge(s["x1_out"], 16 * B)

        @block.gpsimd
        def _(pool):
            def const(ins):
                const.n += 1
                ins.then_inc(s["const"], 1)
                pool.wait_ge(s["const"], const.n)
            const.n = 0
            const(pool.memset(ident[:], 0.0))
            const(pool.affine_select(out=ident[:], in_=ident[:], compare_op=ALU.not_equal, fill=1.0, base=0,
                                     pattern=[[-1, P]], channel_multiplier=1))
            const(pool.tensor_copy(ident_b[:], ident[:]))
            const(pool.memset(pow_half[:], -0.5))
            const(pool.memset(q_aug[:], 0.0))
            const(pool.memset(k_aug[:], 0.0))
            const(pool.memset(q_aug[:, :, 27:30], 1.0))
            const(pool.memset(k_aug[:, :, 24:27], 1.0))
            const(pool.memset(pick[:], 0.0))
            const(pool.memset(pick[:, :, GROUPS:], 1.0))
            for g in range(GROUPS):
                const(pool.memset(pick[:, g, g:g + 1], 1.0))
            const(pool.memset(back_to[:], 0.0))
            for q in range(PAIRS_A):
                const(pool.affine_select(out=back_to[:, q], in_=back_to[:, q], compare_op=ALU.not_equal, fill=1.0,
                                         base=-(2 * AUG * (q % 2) + q // 2), pattern=[[-AUG, 2], [0, DV]],
                                         channel_multiplier=1))
            const(pool.memset(mask_f[:], 0.0))
            const(pool.affine_select(out=mask_f[:], in_=mask_f[:], compare_op=ALU.is_ge, fill=MASKED, base=0,
                                     pattern=[[1, P]], channel_multiplier=-1))
            const(pool.tensor_copy(mask_b[:], mask_f[:]))
            pool.wait_ge(s["w"], 96)
            const(pool.tensor_tensor(bond[:], bond[:], bon0[:], ALU.subtract))

            def split(value, part, name, n):
                v = value[:].rearrange("p i h c -> p (i h c)")
                parts = [part[:, k].rearrange("p r c -> p (r c)") for k in range(3)]
                c = 0
                for k in range(3):
                    pool.tensor_scalar(parts[k], v, 1.0, 0.0, ALU.mult, ALU.add).then_inc(s[name], 1)
                    c += 1
                    if k < 2:
                        wait_apart(pool, s[name], STEPS_K * n + c, s["const"])
                        pool.tensor_tensor(rest[k + (2 if name == "qsplit" else 0)][:], v, parts[k],
                                           ALU.subtract).then_inc(s[name], 1)
                        c += 1
                        wait_apart(pool, s[name], STEPS_K * n + c, s["const"])
                        v = rest[k + (2 if name == "qsplit" else 0)][:]

            def rstd(mv, ve, out, name, n):
                wait_apart(pool, s["mv_" + name], TT * (n + 1), s["const"])
                pool.tensor_scalar(ve[:], mv[:, :, 1], 1.0, EPS, ALU.mult, ALU.add).then_inc(s["ve_" + name], 1)
                wait_apart(pool, s["ve_" + name], n + 1, s["const"])
                pool.tensor_tensor(out[:], ve[:], pow_half[:], ALU.pow).then_inc(s["rstd_" + name], 1)

            def bonus(n):
                wait_apart(pool, s["sg"], n + 1, s["const"])
                wait_apart(pool, s["p_bonT"], n, s["const"])
                def did(ins):
                    did.c += 1
                    ins.then_inc(s["bon"], 1)
                    wait_apart(pool, s["bon"], BON * n + did.c, s["const"])
                did.c = 0
                def sig(r, w):
                    return sg[:, :, :, r:r + 1].to_broadcast([P, TT, HEADS, w])
                step_b = bond[:].rearrange("p (o h) c -> p o h c", o=1).to_broadcast([P, TT, HEADS, 8])
                base_b = bon0[:].rearrange("p (o h) c -> p o h c", o=1).to_broadcast([P, TT, HEADS, 8])
                did(pool.tensor_tensor(bt[0][:], sig(0, 8), step_b, ALU.mult))
                did(pool.tensor_tensor(bv[0][:], bt[0][:], base_b, ALU.add))
                for r in range(1, 4):
                    pair = bv[r - 1][:].rearrange("p i h (c two) -> p (i h) c two", two=2)
                    w = 8 >> r
                    t = bt[r][:].rearrange("p i h c -> p (i h) c")
                    sr = sg[:].rearrange("p i h r -> p (i h) r")[:, :, r:r + 1].to_broadcast([P, TT * HEADS, w])
                    did(pool.tensor_tensor(t, pair[:, :, :, 1], pair[:, :, :, 0], ALU.subtract))
                    did(pool.tensor_tensor(t, t, sr, ALU.mult))
                    out = bv[r][:].rearrange("p i h c -> p (i h) c") if r < 3 \
                        else k5[:].rearrange("p i h c -> p (i h) c")[:, :, DH:DH + 1]
                    did(pool.tensor_tensor(out, t, pair[:, :, :, 0], ALU.add))

            def step(b, f, n, m, z, y, par):
                if f is not None:
                    wait_apart(pool, s["qkn"], f + 1, s["const"])
                    pool.tensor_scalar(k5[:, :, :, 0:DH], qkn[:, :, HEADS:, :], 1.0, 0.0,
                                       ALU.mult, ALU.add).then_inc(s["kcopy"], 1)
                    bonus(f)
                    wait_apart(pool, s["kcopy"], f + 1, s["const"])
                    wait_apart(pool, s["p_kaT"], f, s["const"])
                    split(k5, k_part, "ksplit", f)
                    wait_apart(pool, s["ksplit"], STEPS_K * (f + 1), s["const"])
                    kp = k_part[:].rearrange("p k r c -> p r k c")
                    rows = k_aug[:].rearrange("p r (m c) -> p r m c", c=DH)
                    pool.tensor_scalar(rows[:, :, 0:3, :], kp[:, :, :, 0:DH], 1.0, 0.0, ALU.mult, ALU.add)
                    pool.tensor_scalar(rows[:, :, 3:5, :], kp[:, :, 0:2, 0:DH], 1.0, 0.0, ALU.mult, ALU.add)
                    pool.tensor_scalar(rows[:, :, 5, :], kp[:, :, 0, 0:DH], 1.0, 0.0, ALU.mult, ALU.add)
                    pool.tensor_scalar(k_aug[:, :, 27:30], kp[:, :, :, DH], 1.0, 0.0,
                                       ALU.mult, ALU.add).then_inc(s["kaug"], 1)
                if y is not None:
                    rstd(mv_y, ve_y, rstd_y, "y", y)
                if m is not None:
                    rstd(mv_a, ve_a, rstd_a, "a", m)
                if f is not None:
                    wait_apart(pool, s["q5"], f + 1, s["const"])
                    wait_apart(pool, s["p_qaT"], f, s["const"])
                    split(q5, q_part, "qsplit", f)
                    wait_apart(pool, s["qsplit"], STEPS_K * (f + 1), s["const"])
                    qp = q_part[:].rearrange("p k r c -> p r k c")
                    rows = q_aug[:].rearrange("p r (m c) -> p r m c", c=DH)
                    for lo, hi, k in ((0, 3, 0), (3, 5, 1), (5, 6, 2)):
                        pool.tensor_scalar(rows[:, :, lo:hi, :],
                                           qp[:, :, k:k + 1, 0:DH].to_broadcast([P, TT * HEADS, hi - lo, DH]),
                                           1.0, 0.0, ALU.mult, ALU.add)
                    pool.tensor_scalar(q_aug[:, :, 24:27], qp[:, :, :, DH], 1.0, 0.0,
                                       ALU.mult, ALU.add).then_inc(s["qaug"], 1)

            rounds(pool, step)

        @block.tensor
        def _(pe):
            pe.wait_ge(s["const"], N_CONST)
            pe.wait_ge(s["w"], 96)

            def scores(b, par, *heads):
                if b is None:
                    return
                for h in heads:
                    g, j = h // GH, h % GH
                    if h == 0:
                        wait(pe, s["qaT"], b + 1)
                        wait(pe, s["kaT"], b + 1)
                    wait(pe, s["prob"], HEADS * b + max(h - BANKS + 1, 0))
                    bank = score[h % BANKS]
                    r = slice(AUG * j, AUG * (j + 1))
                    pe.matmul(bank[:, 0:T], k_augT[par][r, g, 0:P], q_augT[par][r, g, :], start=True, stop=True,
                              tile_position=(AUG * j, 0))
                    pe.matmul(bank[:, T:SC], k_augT[par][r, g, P:T], q_augT[par][r, g, P:T], start=False,
                              stop=True, tile_position=(AUG * j, 0), skip_group_check=True)
                    for o in (0, T):
                        m = pe.matmul(bank[:, o:o + P], ident_b[:], mask_b[:], start=False, stop=True,
                                      skip_group_check=True)
                    m.then_inc(s["p_score"], 1)

            def weighted(b, par, p):
                if b is None:
                    return
                if p == 0:
                    wait(pe, s["val"], 4 * (b + 1))
                wait(pe, s["prob"], HEADS * b + 2 * p + 2)
                wait(pe, s["raw"], GROUPS * b + p // 2)
                for k, (q, w) in enumerate(((slice(0, T), slice(0, T)), (slice(P, T), slice(T, SC)))):
                    for i in range(2):
                        h = 2 * p + i
                        m = pe.matmul(outp[DV * i:DV * (i + 1), p % 2, q], val[par][:, k, h, :],
                                      prob[:, h % RING, w], start=(k == 0), stop=(k == 1),
                                      tile_position=(0, DV * i), skip_group_check=True)
                m.then_inc(s["p_out"], 1)

            def sums(b, g):
                if b is None:
                    return
                if g == 0:
                    wait(pe, s["rec"], b)
                for k, (q, w) in enumerate(((slice(0, T), slice(0, T)), (slice(P, T), slice(T, SC)))):
                    for j in range(GH):
                        m = pe.matmul(total[AUG * j:AUG * (j + 1), q], pick[:, g, :],
                                      prob[:, (GH * g + j) % RING, w], start=(g == 0 and k == 0),
                                      stop=(g == GROUPS - 1 and k == 1), tile_position=(0, AUG * j),
                                      skip_group_check=True)
                m.then_inc(s["p_sum"], 1)

            def spread_out(z, g):
                if z is None:
                    return
                if g == 0:
                    wait(pe, s["rec"], z + 1)
                    wait(pe, s["q5"], min(z + 2, B) if isinstance(z, int) else z + 2)
                if g == 2:
                    wait(pe, s["q5"], min(z + 3, B) if isinstance(z, int) else z + 3)
                wait(pe, s["onT"], GROUPS * z + g)
                for i in range(2):
                    m = pe.matmul(spread[:, i, :], back_to[:, 2 * g + i].rearrange("p i d -> p (i d)"), rec[:],
                                  start=True, stop=True)
                m.then_inc(s["p_bc"], 1)

            def output(z, par, pieces):
                if z is None:
                    return
                for c in pieces:
                    if c == 0:
                        wait(pe, s["y"], z)
                        wait(pe, s["val"], 4 * min(z + 3, B) if isinstance(z, int) else 4 * (z + 3))
                    wait(pe, s["onT"], GROUPS * z + c // 2 + 1)
                    for i in range(TT):
                        m = pe.matmul(back[:, i * P:(i + 1) * P], onT[1 - par][:, c, i * P:(i + 1) * P],
                                      wout[:, c, :], start=(c == 0 and i == 0), stop=(c == PAIRS_A - 1),
                                      skip_group_check=True)
                if c == PAIRS_A - 1:
                    m.then_inc(s["p_y"], 1)

            def values(f, par, k):
                if f is None:
                    return
                if k == 0:
                    wait(pe, s["y"], f - 2)
                wait(pe, s["val"], 4 * f + k)
                wait(pe, s["xnT"], f + 1)
                pe.matmul(back[:, :], xnT[1 - par][:, (k // 2) * P:(k // 2 + 1) * P],
                          wv[:, (k % 2) * 512:(k % 2 + 1) * 512], start=True, stop=True).then_inc(s["p_v"], 1)

            def step(b, f, n, m, z, y, par):
                values(f, par, 0)
                scores(b, par, 0, 1)
                if n is not None:
                    wait(pe, s["xn"], n + 1)
                    wait(pe, s["qraw"], n)
                    for i in range(TT):
                        mm = pe.transpose(front[:, i * P:(i + 1) * P], xn[:, i, :], ident[:])
                    mm.then_inc(s["p_xnT"], 1)
                values(f, par, 1)
                scores(b, par, 2, 3)
                if n is not None:
                    wait(pe, s["xnT"], n + 1)
                    for i in range(TT):
                        mm = pe.matmul(front[:, T + i * P:T + (i + 1) * P], xnT[par][:, i * P:(i + 1) * P], wqk[:],
                                       start=True, stop=True)
                    mm.then_inc(s["p_qk"], 1)
                spread_out(z, 0)
                weighted(b, par, 0)
                scores(b, par, 4, 5)
                weighted(b, par, 1)
                sums(b, 0)
                values(f, par, 2)
                scores(b, par, 6, 7)
                spread_out(z, 1)
                scores(b, par, 8, 9)
                weighted(b, par, 2)
                values(f, par, 3)
                weighted(b, par, 3)
                sums(b, 1)
                if f is not None:
                    wait(pe, s["bon"], BON * (f + 1))
                    wait(pe, s["q5"], f)
                    if z is not None:
                        wait(pe, s["onT"], GROUPS * z + 2)
                    for i in range(TT):
                        mm = pe.matmul(spread[0:HEADS, 0, i * P:(i + 1) * P], k5[:, i, :, DH], ident[:],
                                       start=True, stop=True)
                    mm.then_inc(s["p_bonT"], 1)
                scores(b, par, 10, 11)
                if n is not None:
                    wait(pe, s["qkn"], n + 1)
                    for i in range(TT):
                        mm = pe.transpose(front[:, i * P:(i + 1) * P], qkn[:, i].rearrange("p h c -> p (h c)"),
                                          ident[:])
                    mm.then_inc(s["p_qkT"], 1)
                weighted(b, par, 4)
                output(z, par, range(0, 4))
                if f is not None:
                    wait(pe, s["cmax"], f + 1)
                    for i in range(TT):
                        mm = pe.matmul(spread[:, 1, i * HEADS:(i + 1) * HEADS], cmax[:, i * P:(i + 1) * P],
                                       ident[0:HEADS, 0:HEADS], start=True, stop=True)
                    mm.then_inc(s["p_cmax"], 1)
                weighted(b, par, 5)
                sums(b, 2)
                spread_out(z, 2)
                scores(b, par, 12, 13)
                if n is not None:
                    wait(pe, s["qkT"], n + 1)
                    for i in range(TT):
                        mm = pe.matmul(front[:, T + i * P:T + (i + 1) * P], qkT[:, i * P:(i + 1) * P], wrot[:],
                                       start=True, stop=True)
                    mm.then_inc(s["p_rot"], 1)

                def turn_operands(aug, name, last, count):
                    wait(pe, s[name + "aug"], f + 1)
                    wait(pe, s[last], count)
                    for g in range(GROUPS):
                        for i in range(TT):
                            o = (g * TT + i) * P
                            mm = pe.transpose(turned_b[:, o:o + P],
                                              aug[:, i * HEADS + GH * g:i * HEADS + GH * (g + 1), :]
                                              .rearrange("p h c -> p (h c)"), ident_b[:])
                    mm.then_inc(s[f"p_{name}aT"], 1)
                if f is not None:
                    turn_operands(k_aug, "k", "qaT", f)
                spread_out(z, 3)
                weighted(b, par, 6)
                scores(b, par, 14, 15)
                output(z, par, range(4, 6))
                weighted(b, par, 7)
                sums(b, 3)
                output(z, par, range(6, 8))
                if f is not None:
                    turn_operands(q_aug, "q", "kaT", f + 1)

            rounds(pe, step)

        @block.scalar
        def _(act):
            act.wait_ge(s["const"], N_CONST)

            def weights(b, *heads):
                if b is None:
                    return
                for h in heads:
                    wait(act, s["p_sum"], GROUPS * b + (h - RING) // GH + 1)
                    wait(act, s["p_score"], HEADS * b + h + 1)
                    act.activation(prob[:, h % RING, :], score[h % BANKS][:, 0:SC], ACT.Exp).then_inc(s["prob"], 1)

            def copy_out(b, par, g):
                if b is None:
                    return
                wait(act, s["p_out"], PAIRS_A * b + 2 * g + 2)
                if g == 0:
                    wait(act, s["p_y"], b - 1)
                act.activation(onT[par][:, 2 * g:2 * g + 2, :], outp[:], ACT.Copy).then_inc(s["raw"], 1)

            def copy_values(f, par, k):
                if f is None:
                    return
                if k == 0:
                    wait(act, s["p_out"], PAIRS_A * (f - 1))
                wait(act, s["p_v"], 4 * f + k + 1)
                act.activation(val[1 - par][:, k // 2, (k % 2) * 8:(k % 2) * 8 + 8, :],
                               back[:, :].rearrange("p (h v) -> p h v", h=8), ACT.Copy).then_inc(s["val"], 1)

            def step(b, f, n, m, z, y, par):
                copy_values(f, par, 0)
                weights(b, 0, 1)
                if n is not None:
                    wait(act, s["p_xnT"], n + 1)
                    wait(act, s["p_v"], 4 * (n - 1))
                    act.activation(xnT[par][:], front[:, 0:T], ACT.Copy).then_inc(s["xnT"], 1)
                copy_values(f, par, 1)
                weights(b, 2, 3)
                if n is not None:
                    wait(act, s["p_qk"], n + 1)
                    wait(act, s["ss1"], n)
                    act.activation(sq1[:].rearrange("p r c -> p (r c)"), front[:, T:2 * T],
                                   ACT.Square).then_inc(s["sq1"], 1)
                weights(b, 4, 5)
                copy_out(b, par, 0)
                copy_values(f, par, 2)
                weights(b, 6, 7)
                weights(b, 8, 9)
                copy_values(f, par, 3)
                copy_out(b, par, 1)
                weights(b, 10, 11)
                if n is not None:
                    wait(act, s["p_qkT"], n + 1)
                    act.activation(qkT[:], front[:, 0:T], ACT.Copy).then_inc(s["qkT"], 1)
                copy_out(b, par, 2)
                weights(b, 12, 13)
                if n is not None:
                    wait(act, s["p_rot"], n + 1)
                    wait(act, s["q4"], n)
                    fr = front[:, T:2 * T].rearrange("p (i k h c) -> p i k h c", i=TT, k=2, c=DH)
                    act.activation(ek[:], fr[:, :, 1], ACT.Exp, scale=-3.0).then_inc(s["ek"], 1)
                    act.activation(sq2[:], fr[:, :, 0], ACT.Square).then_inc(s["sq2"], 1)
                    act.activation(qraw[:], fr[:, :, 0], ACT.Copy).then_inc(s["qraw"], 1)
                weights(b, 14, 15)
                copy_out(b, par, 3)
                if z is not None:
                    wait(act, s["p_y"], z + 1)
                    wait(act, s["yn"], z)
                    act.activation(y_sb[:], back[:, 0:TT * D], ACT.Copy).then_inc(s["y"], 1)
                if f is not None:
                    wait(act, s["p_qaT"], f + 1)
                    wait(act, s["p_score"], HEADS * (f - 1))
                    act.activation(q_augT[1 - par][:].rearrange("p g t -> p (g t)"), turned_b[:, :],
                                   ACT.Copy).then_inc(s["qaT"], 1)

            rounds(act, step)

        @block.vector
        def _(dve):
            def stats(src, stat, mv, name, n):
                for i in range(TT):
                    m = dve.bn_stats(stat[:, i, :], src[:, i * D:(i + 1) * D])
                m.then_inc(s["stat_" + name], 1)
                wait_apart(dve, s["stat_" + name], n + 1, s["const"])
                for i in range(TT):
                    dve.bn_aggr(mv[:, i, :], stat[:, i, :]).then_inc(s["mv_" + name], 1)

            def rsqrt(ssg, r, nt, nu, name, n, half):
                def did(ins):
                    did.c += 1
                    ins.then_inc(s[name], 1)
                    dve.wait_ge(s[name], RSQ * n + did.c)
                did.c = 0
                did(dve.tensor_scalar(r[0][:].bitcast(I32), ssg[:].bitcast(I32), -0.5, float(MAGIC),
                                      ALU.mult, ALU.add))
                for k in range(3):
                    w = half if k == 2 else 0.5
                    did(dve.tensor_tensor(nt[:], ssg[:], r[k][:], ALU.mult))
                    did(dve.scalar_tensor_tensor(out=nu[:], in0=nt[:], scalar=-w, in1=r[k][:], op0=ALU.mult,
                                                 op1=ALU.mult))
                    did(dve.scalar_tensor_tensor(out=r[k + 1][:], in0=nu[:], scalar=3 * w, in1=r[k][:],
                                                 op0=ALU.add, op1=ALU.mult))

            dve.wait_ge(s["const"], N_CONST)

            def reciprocal(z):
                if z is None:
                    return
                wait(dve, s["p_sum"], GROUPS * (z + 1))
                wait(dve, s["p_bc"], GROUPS * z)
                dve.reciprocal(rec[:], total[:, 0:T]).then_inc(s["rec"], 1)

            def normalise(z, par, g):
                if z is None:
                    return
                wait(dve, s["p_bc"], GROUPS * z + g + 1)
                wait(dve, s["raw"], GROUPS * z + g + 1)
                o = onT[1 - par][:, 2 * g:2 * g + 2, :]
                dve.tensor_tensor(o, spread[:], o, ALU.mult).then_inc(s["onT"], 1)

            def step(b, f, n, m, z, y, par):
                if f is not None:
                    wait(dve, s["ek"], f + 1)
                    wait(dve, s["bon"], BON * f)
                    dve.tensor_scalar(ek1[:], ek[:], 1.0, None, ALU.add).then_inc(s["ek1"], 1)
                    wait(dve, s["sq2"], f + 1)
                    dve.tensor_reduce(ss2[:], sq2[:], AX.X, ALU.add).then_inc(s["ss2"], 1)
                    dve.wait_ge(s["ek1"], f + 1)
                    dve.reciprocal(sg[:], ek1[:]).then_inc(s["sg"], 1)
                    dve.wait_ge(s["ss2"], f + 1)
                    dve.tensor_scalar(ssg2[:], ss2[:], NORM_MIN2, None, ALU.max).then_inc(s["ssg2"], 1)
                    dve.wait_ge(s["ssg2"], f + 1)
                reciprocal(z)
                if f is not None:
                    rsqrt(ssg2, r2, nt2, nu2, "rsq2", f, 0.25)
                    wait(dve, s["qsplit"], STEPS_K * f)
                    wait(dve, s["qraw"], f + 1)
                    dve.tensor_tensor(q5[:, :, :, 0:DH], qraw[:],
                                      r2[3][:].rearrange("p i (h o) -> p i h o", o=1)
                                      .to_broadcast([P, TT, HEADS, DH]), ALU.mult).then_inc(s["q4"], 1)
                if n is not None:
                    wait(dve, s["sq1"], n + 1)
                    dve.tensor_reduce(ss1[:], sq1[:], AX.X, ALU.add).then_inc(s["ss1"], 1)
                    dve.wait_ge(s["ss1"], n + 1)
                    dve.tensor_scalar(ssg1[:], ss1[:], NORM_MIN2, None, ALU.max).then_inc(s["ssg1"], 1)
                    dve.wait_ge(s["ssg1"], n + 1)
                normalise(z, par, 0)
                if n is not None:
                    rsqrt(ssg1, r1, nt1, nu1, "rsq1", n, 0.5)
                    wait(dve, s["kcopy"], n)
                    dve.tensor_tensor(qkn[:].rearrange("p i h c -> p (i h) c"),
                                      front[:, T:2 * T].rearrange("p (r c) -> p r c", c=DH),
                                      r1[3][:].rearrange("p (r o) -> p r o", o=1)
                                      .to_broadcast([P, TT * 2 * HEADS, DH]), ALU.mult).then_inc(s["qkn"], 1)
                normalise(z, par, 1)
                if f is not None:
                    wait(dve, s["p_bonT"], f + 1)
                    dve.tensor_copy(bonT[:], spread[0:HEADS, 0, :]).then_inc(s["bonT"], 1)
                    dve.wait_ge(s["bonT"], f + 1)
                    wait(dve, s["p_cmax"], f)
                    dve.tensor_tensor_scan(out=cmax[:], data0=bonT[:], data1=bonT[:], initial=bonT[:, 0:1],
                                           op0=ALU.max, op1=ALU.max).then_inc(s["cmax"], 1)
                if f is not None:
                    wait(dve, s["p_cmax"], f + 1)
                    dve.tensor_scalar(q5[:, :, :, DH], spread[:, 1, 0:TT * HEADS].rearrange("p (i h) -> p i h", i=TT),
                                      -1.0, None, ALU.mult).then_inc(s["q5"], 1)
                normalise(z, par, 2)
                if y is not None:
                    wait(dve, s["y"], y + 1)
                    stats(y_sb, stat_y, mv_y, "y", y)
                if m is not None:
                    wait(dve, s["xa"], 16 * (m + 1))
                    stats(xa[:].rearrange("p i d -> p (i d)"), stat_a, mv_a, "a", m)
                normalise(z, par, 3)
                if y is not None:
                    wait(dve, s["rstd_y"], y + 1)
                    for i in range(TT):
                        mm = dve.tensor_scalar(yn[:, i, :], y_sb[:, i * D:(i + 1) * D], mv_y[:, i, 0:1],
                                               rstd_y[:, i:i + 1], ALU.subtract, ALU.mult)
                    mm.then_inc(s["yn"], 1)
                    dve.wait_ge(s["yn"], y + 1)
                    wait(dve, s["xr"], 16 * (y + 1))
                    wait(dve, s["x1_out"], 16 * y)
                    dve.tensor_tensor(x1[:], yn[:], xr[:], ALU.add).then_inc(s["x1"], 1)
                if m is not None:
                    wait(dve, s["rstd_a"], m + 1)
                    wait(dve, s["p_xnT"], m)
                    for i in range(TT):
                        mm = dve.tensor_scalar(xn[:, i, :], xa[:, i, :], mv_a[:, i, 0:1], rstd_a[:, i:i + 1],
                                               ALU.subtract, ALU.mult)
                    mm.then_inc(s["xn"], 1)
                if f is not None:
                    wait(dve, s["p_kaT"], f + 1)
                    wait(dve, s["p_score"], HEADS * (f - 1))
                    dve.tensor_copy(k_augT[1 - par][:].rearrange("p g t -> p (g t)"), turned_b[:, :])\
                       .then_inc(s["kaT"], 1)

            rounds(dve, step)


CHUNK = 512
CT = CHUNK // P
NC = B * T // CHUNK
STEPS = CHUNK // B
HID = 512
HC = HID // P
E = 32
NT = B * T // P


def part(t, i, n):
    return t[:, i * n:(i + 1) * n] if isinstance(i, int) else t[:, bass.ds(i * n, n)]


def mixing_layers(nc, x1_d, x3_d, w1, w2, h1, h2, w3, scales, w3_scale, wi, wh, rnn_bias, gate, sorted_d, keep):
    with ExitStack() as ctx:
        def sb(name, shape, dt=F32):
            return ctx.enter_context(nc.sbuf_tensor(name, shape, dt))

        def ps(name, shape, dt=F32):
            return ctx.enter_context(nc.psum_tensor(name, shape, dt))

        def sem(name):
            return ctx.enter_context(nc.semaphore(name))

        ident = sb("ident2", [P, P])
        before = sb("before", [P, P], BF16)
        ones = sb("ones", [P, P], BF16)
        pow_half = sb("pow_half2", [P, CT])
        rev = sb("rev", [P, E])
        zeros = sb("zeros", [P, 2048])
        w1_sb = sb("w1_sb", [P, HID])
        w2_sb = sb("w2_sb", [P, HID])
        h1_sb = sb("h1_sb", [P, HC, HID])
        h2_sb = sb("h2_sb", [P, HC, HID])
        w3_sb = sb("w3_sb", [P, HC, D])
        sc = sb("sc", [P, 4, HC])
        sc_half = sb("sc_half", [P, HC])
        sc_prod = sb("sc_prod", [P, HC])
        w3s = sb("w3s", [P, D])
        wi_sb = sb("wi_sb", [P, D])
        wh_sb = sb("wh_sb", [P, D])
        rb = sb("rb", [P, 2])
        bias = sb("bias", [P, 1])
        gate_sb = sb("gate_sb", [P, E])

        x1c = [sb(f"x1c{i}", [P, CT, D]) for i in range(2)]
        xn2 = sb("xn2", [P, CT, D])
        xn2T = sb("xn2T", [P, CHUNK])
        th = [sb(f"th{i}", [P, CHUNK]) for i in range(2)]
        ag = [sb(f"ag{i}", [P, CHUNK]) for i in range(2)]
        hT = [sb(f"hT{i}", [P, HC, CHUNK]) for i in range(3)]
        x1v = sb("x1v", [P, CT, D])
        hs = sb("hs", [P, CHUNK])
        y = sb("y", [P, CT, D])
        yn = sb("yn2", [P, CT, D])
        x2 = [sb(f"x2{i}", [P, CT, D]) for i in range(2)]
        xn3 = sb("xn3", [P, CT, D])
        xn3T = sb("xn3T", [P, CHUNK])
        state = sb("state", [P, CHUNK])
        hn = sb("hn", [P, CT, D])
        x3 = sb("x3", [P, CT, D])
        xn4 = sb("xn4", [P, CT, D])
        stat = {n: sb("bstat_" + n, [P, CT, 6]) for n in "fyxhe"}
        mv = {n: sb("bmv_" + n, [P, CT, 2]) for n in "fyxhe"}
        ve = {n: sb("bve_" + n, [P, CT]) for n in "fyxhe"}
        rs = {n: sb("brs_" + n, [P, CT]) for n in "fyxhe"}
        top = sb("top", [P, CT])
        is_top = sb("is_top", [P, CT, E])
        rtop = sb("rtop", [P, CT, E])
        first = sb("first", [P, CT])
        tanh_top = sb("tanh_top", [P, CT])
        gate_val = sb("gate_val", [P, CT])
        pre = sb("pre", [P, CT, E])
        pre_oh = sb("pre_oh", [P, CT, E])
        xn4T = sb("xn4T", [P, CHUNK])
        onehot = sb("onehot", [P, CT, E], BF16)
        xn4T_all, xs_all, oh_all, rank_all, counts = keep

        main = [ps(f"main{i}", [P, CHUNK]) for i in range(4)]
        yp = ps("yp", [P, CHUNK])
        turn = ps("turn", [P, CHUNK])
        xi = ps("xi", [P, CHUNK])
        route = ps("route", [P, CHUNK])

        names = ("w", "const", "xc0", "xc1", "p_xn2T", "xn2", "xn2T", "p_a", "p_g", "tanh", "ag", "h1", "p_h1", "p_h2", "h2", "h3",
                 "p_y", "y", "yn", "x2", "xn3", "p_xn3T", "xn3T", "p_xi", "p_step", "step", "p_state", "hs", "xv", "hn", "x3",
                 "x3_out", "xn4", "p_xn4T", "xn4T", "p_logit", "top", "is_top", "rtop", "first", "onehot",
                 "tanh_top", "gate_val", "xs", "p_rank", "pre", "pre_oh", "rank", "counts", "zero", "kept")
        s = {name: sem("b_" + name) for name in names}
        for n in "fyxhe":
            for k in ("stat", "mv", "ve", "rs"):
                s[k + n] = sem(f"b_{k}_{n}")
        N_CONST = 12

        ctx.callback(clear, nc, list(s.values()))
        block = ctx.enter_context(nc.Block())

        def rounds(eng, step):
            def row(k, par):
                return [v if not isinstance(v, int) or 0 <= v < NC else None for v in
                        (k, k - 1, k - 2, k - 3, k - 4, k - 5)] + [par]
            for k in range(6):
                step(*row(k, k % 2))
            with eng.Fori(0, (NC - 6) // 2) as i:
                for par in range(2):
                    step(*row(2 * i + (6 + par), par))
            for k in range(NC, NC + 5):
                step(*row(k, k % 2))

        x1_rows = x1_d.rearrange("(c k u) b d -> c (u b) k d", k=CT, u=P // B)
        x3_rows = x3_d.rearrange("(c k p) d -> c p k d", k=CT, p=P)

        def chunk_of(ap, c):
            return ap[c] if isinstance(c, int) else ap[bass.ds(c, 1)].rearrange("o p k d -> p (o k) d")

        @block.sync
        def _(sp):
            for dst, src in ((w1_sb[:], w1), (w2_sb[:], w2), (wi_sb[:], wi), (wh_sb[:], wh), (gate_sb[:], gate),
                             (sc[:], scales), (rb[:], rnn_bias), (w3s[:], w3_scale.to_broadcast([P, D])),
                             (h1_sb[:], h1.rearrange("(c p) n -> p c n", p=P)),
                             (h2_sb[:], h2.rearrange("(c p) n -> p c n", p=P)),
                             (w3_sb[:], w3.rearrange("(c p) n -> p c n", p=P))):
                sp.dma_start(dst, src).then_inc(s["w"], 16)

            def step(p, c, v, r, h, q, par):
                if p is not None:
                    wait(sp, s["xn2"], p - 1)
                    sp.dma_start(x1c[par][:], chunk_of(x1_rows, p)).then_inc(s[f"xc{par}"], 16)
                if v is not None:
                    wait(sp, s["x2"], v)
                    sp.dma_start(x1v[:], chunk_of(x1_rows, v)).then_inc(s["xv"], 16)
                if h is not None:
                    wait(sp, s["x3"], h + 1)
                    sp.dma_start(chunk_of(x3_rows, h), x3[:]).then_inc(s["x3_out"], 16)

            rounds(sp, step)
            sp.wait_ge(s["const"], N_CONST)
            slots = sorted_d.rearrange("(g p k) d -> g p (k d)", p=P, k=16)
            for g in range(slots.shape[0]):
                sp.dma_start(slots[g], zeros[:]).then_inc(s["zero"], 16)
            sp.wait_ge(s["zero"], 16 * slots.shape[0])
            sp.wait_ge(s["x3_out"], 16 * NC)

        @block.gpsimd
        def _(pool):
            def const(ins):
                const.n += 1
                ins.then_inc(s["const"], 1)
                pool.wait_ge(s["const"], const.n)
            const.n = 0
            const(pool.memset(ident[:], 0.0))
            const(pool.affine_select(out=ident[:], in_=ident[:], compare_op=ALU.not_equal, fill=1.0, base=0,
                                     pattern=[[-1, P]], channel_multiplier=1))
            const(pool.memset(ones[:], 1.0))
            const(pool.affine_select(out=before[:], in_=ones[:], compare_op=ALU.is_gt, fill=0.0, base=0,
                                     pattern=[[1, P]], channel_multiplier=-1))
            const(pool.memset(pow_half[:], -0.5))
            const(pool.iota(rev[:], pattern=[[-1, E]], base=E, channel_multiplier=0,
                            allow_small_or_imprecise_dtypes=True))
            const(pool.memset(zeros[:], 0.0))
            const(pool.memset(state[:], 0.0))
            const(pool.memset(counts[:], 0.0))
            pool.wait_ge(s["w"], 176)
            const(pool.tensor_scalar(sc_half[:], sc[:, 0, :], 0.5, 0.0, ALU.mult, ALU.add))
            const(pool.tensor_tensor(sc_prod[:], sc_half[:], sc[:, 1, :], ALU.mult))
            const(pool.tensor_tensor(bias[:], rb[:, 0:1], rb[:, 1:2], ALU.add))

            def rstd(n, c):
                wait_apart(pool, s["mv" + n], CT * (c + 1), s["const"])
                pool.tensor_scalar(ve[n][:], mv[n][:, :, 1], 1.0, EPS, ALU.mult, ALU.add).then_inc(s["ve" + n], 1)
                wait_apart(pool, s["ve" + n], c + 1, s["const"])
                pool.tensor_tensor(rs[n][:], ve[n][:], pow_half[:], ALU.pow).then_inc(s["rs" + n], 1)

            def step(p, c, v, r, h, q, par):
                if h is not None:
                    rstd("h", h)
                    rstd("e", h)
                if v is not None:
                    rstd("y", v)
                    rstd("x", v)
                if p is not None:
                    rstd("f", p)

            rounds(pool, step)

        @block.tensor
        def _(pe):
            def turn4(src, name):
                for k in range(CT):
                    m = pe.transpose(turn[:, k * P:(k + 1) * P], src[:, k], ident[:])
                m.then_inc(s[name], 1)

            def rnn_step(r, t):
                wait(pe, s["step"], STEPS * r + t)
                o = t * B
                prev = (t - 1) % STEPS * B
                pe.matmul(xi[:, o:o + B], wh_sb[:], state[:, prev:prev + B], start=False, stop=(t == STEPS - 1),
                          skip_group_check=True).then_inc(s["p_step"], 1)

            pe.wait_ge(s["w"], 176)
            pe.wait_ge(s["const"], N_CONST)

            def step(p, c, v, r, h, q, par):
                if c is not None:
                    wait(pe, s["xn2"], c + 1)
                    wait(pe, s["hs"], c - 2)
                    turn4(xn2[:], "p_xn2T")
                    wait(pe, s["xn2T"], c + 1)
                    for m in range(HC):
                        wait(pe, s["h3"], HC * c) if m < 2 else wait(pe, s["h1"], HC * c + m - 1)
                        pe.matmul(main[2 * m % 4][:, :], w1_sb[:, m * P:(m + 1) * P], xn2T[:],
                                  start=True, stop=True).then_inc(s["p_a"], 1)
                        pe.matmul(main[(2 * m + 1) % 4][:, :], w2_sb[:, m * P:(m + 1) * P], xn2T[:],
                                  start=True, stop=True).then_inc(s["p_g"], 1)
                if q is not None:
                    wait(pe, s["xn4"], q + 1)
                    if c is not None:
                        wait(pe, s["xn2T"], c + 1)
                    else:
                        wait(pe, s["hs"], min(q + 2, NC))
                    turn4(xn4[:], "p_xn4T")
                    wait(pe, s["rank"], q)
                    wait(pe, s["counts"], q)
                    wait(pe, s["xn4T"], q + 1)
                    for k in range(CT):
                        m_ = pe.matmul(route[:, k * E:(k + 1) * E], xn4T[:, k * P:(k + 1) * P], gate_sb[:],
                                       start=True, stop=True)
                    m_.then_inc(s["p_logit"], 1)
                if r is not None:
                    wait(pe, s["xn3"], r + 1)
                    if q is not None:
                        wait(pe, s["xn4T"], q + 1)
                    elif c is not None:
                        wait(pe, s["xn2T"], c + 1)
                    turn4(xn3[:], "p_xn3T")
                slots = iter(range(STEPS))

                def rnn(n=1):
                    if r is not None:
                        for _ in range(n):
                            t = next(slots, None)
                            if t is not None:
                                rnn_step(r, t)

                def recurrence_input():
                    if r is not None:
                        wait(pe, s["xn3T"], r + 1)
                        wait(pe, s["step"], STEPS * r)
                        pe.matmul(xi[:, :], wi_sb[:], xn3T[:], start=True, stop=False,
                                  skip_group_check=True).then_inc(s["p_xi"], 1)

                def ranks():
                    if q is not None:
                        wait(pe, s["onehot"], q + 1)
                        for k in range(CT):
                            for j in range(k):
                                pe.matmul(route[:, 128 + k * E:128 + (k + 1) * E], ones[:], onehot[:, j, :],
                                          start=(j == 0), stop=False)
                            pe.matmul(route[:, 128 + k * E:128 + (k + 1) * E], before[:], onehot[:, k, :],
                                      start=(k == 0), stop=True)
                        for j in range(CT):
                            m_ = pe.matmul(route[:, 256:256 + E], ones[:], onehot[:, j, :], start=(j == 0),
                                           stop=(j == CT - 1))
                        m_.then_inc(s["p_rank"], 1)

                if c is not None:
                    for layer, (w, src, done, out) in enumerate(((h1_sb, hT[0], "h1", "h2"), (h2_sb, hT[1], "h2", "h3"))):
                        for m in range(HC):
                            if m == 0:
                                wait(pe, s[done], HC * (c + 1))
                            for k in range(HC):
                                mm = pe.matmul(main[m][:, :], w[:, k, m * P:(m + 1) * P], src[:, k, :],
                                               start=(k == 0), stop=(k == HC - 1))
                                if k == HC - 1:
                                    mm.then_inc(s["p_h1" if layer == 0 else "p_h2"], 1)
                                if k % 2 == 1 and (layer, m) != (0, 0):
                                    rnn(2 if (layer, m) == (1, 3) else 1)
                            if layer == 0 and m == 0:
                                ranks()
                                recurrence_input()
                else:
                    ranks()
                    recurrence_input()
                rnn(STEPS)
                if r is not None:
                    wait(pe, s["step"], STEPS * (r + 1))
                    wait(pe, s["xn3T"], r + 1)
                    for k in range(CT):
                        m_ = pe.transpose(turn[:, k * P:(k + 1) * P], state[:, k * P:(k + 1) * P], ident[:])
                    m_.then_inc(s["p_state"], 1)
                if c is not None:
                    wait(pe, s["h3"], HC * (c + 1))
                    wait(pe, s["y"], c)
                    for k in range(CT):
                        for m in range(HC):
                            mm = pe.matmul(yp[:, k * P:(k + 1) * P], hT[2][:, m, k * P:(k + 1) * P],
                                           w3_sb[:, m, :], start=(m == 0), stop=(m == HC - 1))
                    mm.then_inc(s["p_y"], 1)

            rounds(pe, step)

        @block.scalar
        def _(act):
            act.wait_ge(s["const"], N_CONST)

            def step(p, c, v, r, h, q, par):
                slots = iter(range(STEPS))

                def rnn(n=1):
                    if r is not None:
                        for _ in range(n):
                            t = next(slots, None)
                            if t is not None:
                                wait(act, s["p_step"], STEPS * r + t + 1)
                                if t == 0:
                                    wait(act, s["p_state"], r)
                                act.activation(state[:, t * B:(t + 1) * B], xi[:, t * B:(t + 1) * B], ACT.Tanh,
                                               bias=bias[:]).then_inc(s["step"], 1)

                if c is not None:
                    wait(act, s["p_xn2T"], c + 1)
                    wait(act, s["p_g"], HC * c)
                    act.activation(xn2T[:], turn[:, :], ACT.Copy).then_inc(s["xn2T"], 1)
                    for m in range(HC):
                        wait(act, s["p_a"], HC * c + m + 1)
                        wait(act, s["ag"], HC * c + m - 1)
                        act.activation(th[m % 2][:], main[2 * m % 4][:, :], ACT.Tanh,
                                       scale=sc_half[:, m:m + 1]).then_inc(s["tanh"], 1)
                if q is not None:
                    wait(act, s["p_xn4T"], q + 1)
                    wait(act, s["p_logit"], q)
                    wait(act, s["kept"], q)
                    act.activation(xn4T[:], turn[:, :], ACT.Copy).then_inc(s["xn4T"], 1)
                if r is not None:
                    wait(act, s["p_xn3T"], r + 1)
                    act.activation(xn3T[:], turn[:, :], ACT.Copy).then_inc(s["xn3T"], 1)
                if q is not None:
                    wait(act, s["top"], q + 1)
                    act.activation(tanh_top[:], top[:], ACT.Tanh, scale=0.5).then_inc(s["tanh_top"], 1)
                if c is not None:
                    for layer, (pname, dst, done) in enumerate((("p_h1", hT[1], "h2"), ("p_h2", hT[2], "h3"))):
                        for m in range(HC):
                            wait(act, s[pname], HC * c + m + 1)
                            if layer == 1 and m == 0:
                                wait(act, s["p_y"], c)
                            act.activation(dst[:, m, :], main[m][:, :], ACT.Gelu,
                                           scale=sc[:, 2 + layer, m:m + 1]).then_inc(s[done], 1)
                            if (layer, m) == (1, 2):
                                rnn(2)
                                rnn(2)
                            elif (layer, m) == (1, 3):
                                pass
                            else:
                                rnn(2)
                rnn(STEPS)
                if r is not None:
                    wait(act, s["p_state"], r + 1)
                    wait(act, s["hn"], r)
                    act.activation(hs[:], turn[:, :], ACT.Copy).then_inc(s["hs"], 1)

            rounds(act, step)

        @block.vector
        def _(dve):
            dve.wait_ge(s["const"], N_CONST)

            def stats(n, tiles, c):
                for k in range(CT):
                    m = dve.bn_stats(stat[n][:, k, :], tiles(k))
                m.then_inc(s["stat" + n], 1)
                wait_apart(dve, s["stat" + n], c + 1, s["const"])
                for k in range(CT):
                    dve.bn_aggr(mv[n][:, k, :], stat[n][:, k, :]).then_inc(s["mv" + n], 1)

            def apply(n, out, tiles, done, c):
                wait(dve, s["rs" + n], c + 1)
                for k in range(CT):
                    m = dve.tensor_scalar(out[:, k, :], tiles(k), mv[n][:, k, 0:1], rs[n][:, k:k + 1],
                                          ALU.subtract, ALU.mult)
                m.then_inc(s[done], 1)
                dve.wait_ge(s[done], c + 1)

            def step(p, c, v, r, h, q, par):
                if c is not None:
                    for m in range(HC):
                        wait(dve, s["tanh"], HC * c + m + 1)
                        dve.scalar_tensor_tensor(out=ag[m % 2][:], in0=th[m % 2][:], scalar=1.0,
                                                 in1=main[2 * m % 4][:, :], op0=ALU.add,
                                                 op1=ALU.mult).then_inc(s["ag"], 1)
                        wait(dve, s["p_g"], HC * c + m + 1)
                        wait(dve, s["p_h1"], HC * c)
                        dve.wait_ge(s["ag"], HC * c + m + 1)
                        dve.scalar_tensor_tensor(out=hT[0][:, m, :], in0=main[(2 * m + 1) % 4][:, :],
                                                 scalar=sc_prod[:, m:m + 1], in1=ag[m % 2][:], op0=ALU.mult,
                                                 op1=ALU.mult).then_inc(s["h1"], 1)
                if q is not None:
                    lg = route[:, 0:CT * E].rearrange("p (k e) -> p k e", e=E)

                    def wide(col):
                        return col[:].rearrange("p (k o) -> p k o", o=1).to_broadcast([P, CT, E])
                    wait(dve, s["p_logit"], q + 1)
                    wait(dve, s["tanh_top"], q)
                    dve.tensor_reduce(top[:], lg, AX.X, ALU.max).then_inc(s["top"], 1)
                    dve.wait_ge(s["top"], q + 1)
                    dve.tensor_tensor(is_top[:], lg, wide(top), ALU.is_ge).then_inc(s["is_top"], 1)
                    dve.wait_ge(s["is_top"], q + 1)
                    dve.tensor_tensor(rtop[:], is_top[:], rev[:].rearrange("p (o e) -> p o e", o=1)
                                      .to_broadcast([P, CT, E]), ALU.mult).then_inc(s["rtop"], 1)
                    dve.wait_ge(s["rtop"], q + 1)
                    dve.tensor_reduce(first[:], rtop[:], AX.X, ALU.max).then_inc(s["first"], 1)
                    dve.wait_ge(s["first"], q + 1)
                    wait(dve, s["p_rank"], q)
                    wait(dve, s["pre_oh"], q)
                    dve.tensor_tensor(onehot[:], rtop[:], wide(first), ALU.is_equal).then_inc(s["onehot"], 1)
                    dve.wait_ge(s["onehot"], q + 1)
                    dve.tensor_copy(part(oh_all, q, CT), onehot[:])
                    dve.tensor_copy(part(xn4T_all, q, CHUNK), xn4T[:]).then_inc(s["kept"], 1)
                    dve.wait_ge(s["tanh_top"], q + 1)
                    dve.tensor_scalar(gate_val[:], tanh_top[:], 0.5, 0.5, ALU.mult, ALU.add)\
                       .then_inc(s["gate_val"], 1)
                    dve.wait_ge(s["gate_val"], q + 1)
                    dve.tensor_tensor(part(xs_all, q, CT), xn4[:], gate_val[:].rearrange("p (k o) -> p k o", o=1)
                                      .to_broadcast([P, CT, D]), ALU.mult).then_inc(s["xs"], 1)
                if h is not None:
                    wait(dve, s["hs"], h + 1)
                    stats("h", lambda k: hs[:, k * P:(k + 1) * P], h)
                    apply("h", hn, lambda k: hs[:, k * P:(k + 1) * P], "hn", h)
                    wait(dve, s["x3_out"], 16 * h)
                    dve.tensor_tensor(x3[:], hn[:], x2[par][:], ALU.add).then_inc(s["x3"], 1)
                    dve.wait_ge(s["x3"], h + 1)
                    stats("e", lambda k: x3[:, k, :], h)
                    wait(dve, s["xs"], h)
                    wait(dve, s["p_xn4T"], h)
                    apply("e", xn4, lambda k: x3[:, k, :], "xn4", h)
                if q is not None:
                    wait(dve, s["p_rank"], q + 1)
                    cnt = counts[:].rearrange("p (o e) -> p o e", o=1).to_broadcast([P, CT, E])
                    dve.wait_ge(s["onehot"], q + 1)
                    wait(dve, s["counts"], q)
                    dve.tensor_tensor(pre[:], route[:, 128:128 + CT * E].rearrange("p (k e) -> p k e", e=E), cnt,
                                      ALU.add).then_inc(s["pre"], 1)
                    dve.wait_ge(s["pre"], q + 1)
                    dve.tensor_tensor(counts[:], counts[:], route[:, 256:256 + E], ALU.add)\
                       .then_inc(s["counts"], 1)
                    dve.tensor_tensor(pre_oh[:], pre[:], onehot[:], ALU.mult).then_inc(s["pre_oh"], 1)
                    dve.wait_ge(s["pre_oh"], q + 1)
                    dve.tensor_reduce(part(rank_all, q, CT), pre_oh[:], AX.X, ALU.add).then_inc(s["rank"], 1)
                if v is not None:
                    wait(dve, s["p_y"], v + 1)
                    dve.tensor_tensor(y[:], yp[:, :].rearrange("p (k d) -> p k d", d=D),
                                      w3s[:].rearrange("p (o d) -> p o d", o=1).to_broadcast([P, CT, D]),
                                      ALU.mult).then_inc(s["y"], 1)
                    dve.wait_ge(s["y"], v + 1)
                    stats("y", lambda k: y[:, k, :], v)
                    apply("y", yn, lambda k: y[:, k, :], "yn", v)
                    wait(dve, s["xv"], 16 * (v + 1))
                    wait(dve, s["x3"], v - 1)
                    dve.tensor_tensor(x2[par][:], yn[:], x1v[:], ALU.add).then_inc(s["x2"], 1)
                    dve.wait_ge(s["x2"], v + 1)
                    stats("x", lambda k: x2[par][:, k, :], v)
                    wait(dve, s["p_xn3T"], v)
                    apply("x", xn3, lambda k: x2[par][:, k, :], "xn3", v)
                if p is not None:
                    wait(dve, s[f"xc{par}"], 8 * (p - par) + 16)
                    stats("f", lambda k: x1c[par][:, k, :], p)
                    wait(dve, s["p_xn2T"], p)
                    apply("f", xn2, lambda k: x1c[par][:, k, :], "xn2", p)

            rounds(dve, step)


I = 256
IC = I // P
SLOTS = NT + E
OFF = P.bit_length() - 1


def experts_layer(nc, x3_d, sorted_d, routed_d, gate_up, down, sh_gate_up, sh_down, out, keep):
    with ExitStack() as ctx:
        def sb(name, shape, dt=F32):
            return ctx.enter_context(nc.sbuf_tensor(name, shape, dt))

        def ps(name, shape, dt=F32):
            return ctx.enter_context(nc.psum_tensor(name, shape, dt))

        def sem(name):
            return ctx.enter_context(nc.semaphore(name))

        xn4T_all, xs_all, oh_all, rank_all, counts = keep
        position = sb("position", [P, NT], I32)
        ident = sb("ident3", [P, P])
        col = sb("col", [P, 1])
        expert = sb("expert", [1, SLOTS], I32)
        wgu = sb("wgu", [P, E, 2 * I])
        wd = sb("wd", [P, E, IC, D])
        sgu = sb("sgu", [P, 2 * I])
        sd = sb("sd", [P, IC, D])
        full = sb("full", [P, E])
        full_i = sb("full_i", [P, E], I32)
        tiles_i = sb("tiles_i", [P, E], I32)
        tiles = sb("tiles", [P, E])
        upto = sb("upto", [P, E])
        start0 = sb("start0", [P, E])
        start = sb("start", [P, E])
        own = sb("own", [P, 16, E])
        own_start = sb("own_start", [P, NT])
        behind = sb("behind", [P, E])
        owner0 = sb("owner0", [P, 1])
        ones_e = sb("ones_e", [P, E])
        owner = sb("owner", [P, 1])
        silu = [sb(f"silu{i}", [P, CHUNK]) for i in range(2)]
        hid = [sb(f"hid{i}", [P, IC, CHUNK]) for i in range(2)]
        xg = [sb(f"xg{i}", [P, 2, D]) for i in range(2)]
        xgT = [sb(f"xgT{i}", [P, 2 * P]) for i in range(2)]
        act_g = [sb(f"act_g{i}", [P, I]) for i in range(2)]
        hid_g = [sb(f"hid_g{i}", [P, I]) for i in range(2)]
        hid_gT = [sb(f"hid_gT{i}", [P, I]) for i in range(2)]
        yg = [sb(f"yg{i}", [P, 2, D]) for i in range(2)]
        stat = sb("cstat", [P, CT, 6])
        mv = sb("cmv", [P, CT, 2])
        eps = sb("eps", [P, 1])
        sd_y = sb("sd_y", [P, CT])
        rs = sb("crs", [P, CT])
        shared_all = xn4T_all
        x3_all = xs_all
        rows = wgu[:].rearrange("p e i -> p (e i)")
        rt_all = rows[:, 0:NT * D]
        res_all = rows[:, NT * D:2 * NT * D]

        bank = [ps(f"bank{i}", [P, 512]) for i in range(8)]

        names = ("wsh", "wex", "const", "full", "full_i", "tiles_i", "tiles", "upto", "start0", "start", "own", "own_start",
                 "position", "behind", "owner0", "owner", "p_owner", "expert", "p_g", "p_u", "silu", "hid", "p_sh",
                 "sh", "placed", "x3l", "xg0", "xg1", "p_xgT", "xgT", "p_gu", "act_g", "hid_g", "p_hT",
                 "hid_gT", "p_yg", "yg", "yg_out0", "yg_out1", "rt0", "rt1", "rt2", "rt3", "ysum", "stat",
                 "mv", "sd_y", "rs", "yn", "res", "out")
        s = {name: sem("c_" + name) for name in names}
        N_CONST = 5
        ctx.callback(clear, nc, list(s.values()))
        block = ctx.enter_context(nc.Block())

        sorted_t = sorted_d.rearrange("(j k p) d -> j p k d", k=2, p=P)
        routed_t = routed_d.rearrange("(j k p) d -> j p k d", k=2, p=P)
        out_v = out.rearrange("b (c k u) d -> c u b k d", k=CT, u=P // B)
        PAIRS = SLOTS // 2

        def chunk_of(ap, c):
            return ap[c] if isinstance(c, int) else ap[bass.ds(c, 1)].rearrange("o p k d -> p (o k) d")

        def chunk_rounds(eng, step):
            step(0, None, 0)
            step(1, 0, 1)
            with eng.Fori(0, (NC - 2) // 2) as i:
                for par in range(2):
                    step(2 * i + (2 + par), 2 * i + (1 + par), par)
            step(None, NC - 1, 0)

        def slot_rounds(eng, step):
            step(-1, 0, 1)
            step(0, 1, 0)
            step(1, 2, 1)
            with eng.Fori(0, (PAIRS - 4) // 2) as i:
                for par in range(2):
                    step(2 * i + (2 + par), 2 * i + (3 + par), par)
            step(PAIRS - 2, PAIRS - 1, 0)
            step(PAIRS - 1, None, 1)
            step(PAIRS, None, 0)

        def tiles_of(m):
            for i in range(2):
                t = 2 * m + i
                if isinstance(t, int):
                    yield t, i, 0 <= t < SLOTS, 1 <= t <= SLOTS, 2 <= t <= SLOTS + 1
                else:
                    yield t, i, True, True, True

        @block.sync
        def _(sp):
            sp.dma_start(sgu[:], sh_gate_up).then_inc(s["wsh"], 16)
            sp.dma_start(sd[:], sh_down.rearrange("(c p) d -> p c d", p=P)).then_inc(s["wsh"], 16)
            for e in range(0, E, 8):
                sp.dma_start(wgu[:, e:e + 8, :], gate_up[e:e + 8].rearrange("e d i -> d e i")).then_inc(s["wex"], 16)
                sp.dma_start(wd[:, e:e + 8], down[e:e + 8].rearrange("e (c p) d -> p e c d", p=P))\
                  .then_inc(s["wex"], 16)
            sp.wait_ge(s["placed"], 16 * NT)
            sp.dma_start(xg[0][:], sorted_t[0]).then_inc(s["xg0"], 16)
            sp.dma_start(xg[1][:], sorted_t[1]).then_inc(s["xg1"], 16)
            sp.dma_start(x3_all[:], x3_d.rearrange("(j p) d -> p j d", p=P)).then_inc(s["x3l"], 16)

            def step(m, a, par):
                if not isinstance(m, int) or 0 <= m < PAIRS - 2:
                    wait(sp, s["p_xgT"], m + 1)
                    sp.dma_start(xg[par][:], chunk_of(sorted_t, m + 2)).then_inc(s[f"xg{par}"], 16)
                if not isinstance(m, int) or m >= 2:
                    wait(sp, s["yg"], 2 * (m - 1))
                    sp.dma_start(chunk_of(routed_t, m - 2), yg[par][:]).then_inc(s[f"yg_out{par}"], 16)

            slot_rounds(sp, step)
            sp.wait_ge(s["yg"], SLOTS)
            sp.dma_start(routed_t[PAIRS - 1], yg[1][:]).then_inc(s["yg_out1"], 16)

            def last(c):
                wait(sp, s["res"], c + 1)
                for u in range(P // B):
                    dst = out_v[c, u] if isinstance(c, int) else out_v[bass.ds(c, 1), u]\
                        .rearrange("o b k d -> (o b) k d")
                    sp.dma_start(dst, part(res_all, c, CHUNK)[u * B:(u + 1) * B]
                                 .rearrange("b (k d) -> b k d", d=D)).then_inc(s["out"], 16)
            last(0)
            with sp.Fori(0, NC - 1) as c:
                last(c + 1)
            sp.wait_ge(s["out"], 16 * NC * (P // B))

        @block.gpsimd
        def _(pool):
            def const(ins):
                const.n += 1
                ins.then_inc(s["const"], 1)
                pool.wait_ge(s["const"], const.n)
            const.n = 0
            const(pool.memset(ident[:], 0.0))
            const(pool.affine_select(out=ident[:], in_=ident[:], compare_op=ALU.not_equal, fill=1.0, base=0,
                                     pattern=[[-1, P]], channel_multiplier=1))
            const(pool.memset(eps[:], EPS))
            const(pool.memset(ones_e[:], 1.0))
            const(pool.iota(col[:], pattern=[[0, 1]], base=0, channel_multiplier=1,
                            allow_small_or_imprecise_dtypes=True))
            pool.wait_ge(s["position"], 1)
            for k in range(NT):
                pool.indirect_dma_start(out=sorted_d[:, :], out_offset=bass.IndirectOffsetOnAxis(
                    ap=position[:, k:k + 1], axis=0), in_=xs_all[:, k, :], in_offset=None)\
                    .then_inc(s["placed"], 16)
            pool.wait_ge(s["placed"], 16 * NT)
            for par in range(2):
                pool.wait_ge(s[f"yg_out{par}"], 8 * PAIRS)

            for c in range(NC):
                wait(pool, s["ysum"], c - 3)
                for k in range(c * CT, (c + 1) * CT):
                    pool.indirect_dma_start(out=rt_all[:, k * D:(k + 1) * D], out_offset=None, in_=routed_d[:, :],
                                            in_offset=bass.IndirectOffsetOnAxis(ap=position[:, k:k + 1], axis=0))\
                        .then_inc(s[f"rt{c % 4}"], 16)

        @block.tensor
        def _(pe):
            pe.wait_ge(s["wsh"], 32)
            pe.wait_ge(s["const"], N_CONST)
            pe.wait_ge(s["owner"], 1)
            pe.matmul(bank[7][0:1, 0:SLOTS], owner[:], ident[:, 0:SLOTS], start=True, stop=True)\
              .then_inc(s["p_owner"], 1)

            def shared(c, d, par):
                if c is not None:
                    for m in range(IC):
                        wait(pe, s["hid"], IC * (c - 1) + m + 1)
                        pe.matmul(bank[2 * m][:, :], sgu[:, m * P:(m + 1) * P], part(xn4T_all, c, CHUNK),
                                  start=True, stop=True).then_inc(s["p_g"], 1)
                        pe.matmul(bank[2 * m + 1][:, :], sgu[:, I + m * P:I + (m + 1) * P],
                                  part(xn4T_all, c, CHUNK), start=True, stop=True).then_inc(s["p_u"], 1)
                if d is not None:
                    wait(pe, s["hid"], IC * (d + 1))
                    wait(pe, s["sh"], d)
                    for k in range(CT):
                        for m in range(IC):
                            mm = pe.matmul(bank[4][:, k * P:(k + 1) * P], hid[1 - par][:, m, k * P:(k + 1) * P],
                                           sd[:, m, :], start=(m == 0), stop=(m == IC - 1))
                    mm.then_inc(s["p_sh"], 1)
            chunk_rounds(pe, shared)

            pe.wait_ge(s["wex"], 16 * (E // 4))
            pe.wait_ge(s["expert"], 1)
            pe.wait_ge(s["sh"], NC)

            def owner_of(t):
                return pe.value_load(expert[0:1, t:t + 1] if isinstance(t, int) else expert[0:1, bass.ds(t, 1)],
                                     min_val=0, max_val=E - 1)

            def step(m, a, par):
                if a is not None:
                    wait(pe, s[f"xg{1 - par}"], 8 * (m + par) + 16)
                    wait(pe, s["xgT"], m + 1)
                    for k in range(2):
                        mm = pe.transpose(bank[5][:, k * P:(k + 1) * P], xg[1 - par][:, k, :], ident[:])
                    mm.then_inc(s["p_xgT"], 1)
                for t, i, now, one, two in tiles_of(m):
                    if now:
                        e = owner_of(t)
                        wait(pe, s["xgT"], m + 1)
                        wait(pe, s["hid_g"], t - 3)
                        pe.matmul(bank[2 * par + i][:, :], xgT[par][:, i * P:(i + 1) * P],
                                  wgu[:, bass.ds(e, 1), :].rearrange("p o i -> p (o i)"),
                                  start=True, stop=True).then_inc(s["p_gu"], 1)
                    if two:
                        e = owner_of(t - 2)
                        wait(pe, s["hid_gT"], t - 1)
                        wait(pe, s["yg"], t - 3)
                        for k in range(IC):
                            mm = pe.matmul(bank[6 + i][:, 0:D], hid_gT[i][:, k * P:(k + 1) * P],
                                           wd[:, bass.ds(e, 1), k, :].rearrange("p o d -> p (o d)"),
                                           start=(k == 0), stop=(k == IC - 1))
                        mm.then_inc(s["p_yg"], 1)
                    if one:
                        wait(pe, s["hid_g"], t)
                        wait(pe, s["hid_gT"], t - 1)
                        for k in range(IC):
                            mm = pe.transpose(bank[4][:, k * P:(k + 1) * P], hid_g[1 - i][:, k * P:(k + 1) * P],
                                              ident[:])
                        mm.then_inc(s["p_hT"], 1)

            slot_rounds(pe, step)

        @block.scalar
        def _(act):
            def shared(c, d, par):
                if d is not None:
                    wait(act, s["p_sh"], d + 1)
                    wait(act, s["p_u"], IC * (d + 1))
                    act.activation(part(shared_all, d, CHUNK), bank[4][:, :], ACT.Copy).then_inc(s["sh"], 1)
                if c is not None:
                    for m in range(IC):
                        wait(act, s["p_g"], IC * c + m + 1)
                        wait(act, s["hid"], IC * (c - 1) + m + 1)
                        act.activation(silu[m][:], bank[2 * m][:, :], ACT.Silu).then_inc(s["silu"], 1)
            chunk_rounds(act, shared)

            def step(m, a, par):
                for t, i, now, one, two in tiles_of(m):
                    if now:
                        wait(act, s["p_gu"], t + 1)
                        wait(act, s["hid_g"], t - 1)
                        act.activation(act_g[i][:], bank[2 * par + i][:, 0:I], ACT.Silu).then_inc(s["act_g"], 1)
                    if one:
                        wait(act, s["p_hT"], t)
                        wait(act, s["p_yg"], t - 2)
                        act.activation(hid_gT[1 - i][:], bank[4][:, 0:I], ACT.Copy).then_inc(s["hid_gT"], 1)

            slot_rounds(act, step)

            def last(c):
                wait(act, s["mv"], CT * (c + 1))
                wait(act, s["rs"], c)
                act.activation(sd_y[:], mv[:, :, 1], ACT.Sqrt, bias=eps[:]).then_inc(s["sd_y"], 1)
            last(0)
            with act.Fori(0, NC - 1) as c:
                last(c + 1)

        @block.vector
        def _(dve):
            dve.wait_ge(s["const"], N_CONST)

            def did(ins, name):
                ins.then_inc(s[name], 1)
                dve.wait_ge(s[name], 1)
            did(dve.tensor_scalar(full[:], counts[:], float(P - 1), None, ALU.add), "full")
            did(dve.tensor_copy(full_i[:], full[:]), "full_i")
            did(dve.tensor_single_scalar(tiles_i[:], full_i[:], OFF, ALU.arith_shift_right), "tiles_i")
            did(dve.tensor_copy(tiles[:], tiles_i[:]), "tiles")
            did(dve.tensor_tensor_scan(out=upto[:], data0=ones_e[:], data1=tiles[:], initial=0.0, op0=ALU.mult,
                                       op1=ALU.add), "upto")
            did(dve.tensor_tensor(start0[:], upto[:], tiles[:], ALU.subtract), "start0")
            did(dve.tensor_scalar(start[:], start0[:], float(P), None, ALU.mult), "start")
            did(dve.tensor_scalar(behind[:], upto[:], col[:, 0:1], None, ALU.is_le), "behind")
            did(dve.tensor_reduce(owner0[:], behind[:], AX.X, ALU.add), "owner0")
            did(dve.tensor_scalar(owner[:], owner0[:], float(E - 1), None, ALU.min), "owner")
            for k in range(0, NT, 16):
                dve.tensor_tensor(own[:], oh_all[:, k:k + 16, :], start[:].rearrange("p (o e) -> p o e", o=1)
                                  .to_broadcast([P, 16, E]), ALU.mult).then_inc(s["own"], 1)
                dve.wait_ge(s["own"], k // 16 + 1)
                dve.tensor_reduce(own_start[:, k:k + 16], own[:], AX.X, ALU.add).then_inc(s["own_start"], 1)
                dve.wait_ge(s["own_start"], k // 16 + 1)
            did(dve.tensor_tensor(position[:], own_start[:], rank_all[:], ALU.add), "position")
            dve.wait_ge(s["p_owner"], 1)
            did(dve.tensor_copy(expert[:], bank[7][0:1, 0:SLOTS]), "expert")

            def shared(c, d, par):
                if c is not None:
                    for m in range(IC):
                        wait(dve, s["silu"], IC * c + m + 1)
                        wait(dve, s["p_u"], IC * c + m + 1)
                        wait(dve, s["p_sh"], c - 1)
                        dve.tensor_tensor(hid[par][:, m, :], bank[2 * m + 1][:, :], silu[m][:], ALU.mult)\
                           .then_inc(s["hid"], 1)
            chunk_rounds(dve, shared)

            def step(m, a, par):
                if a is not None:
                    wait(dve, s["p_xgT"], m + 2)
                    wait(dve, s["p_gu"], 2 * m)
                    dve.tensor_copy(xgT[1 - par][:], bank[5][:, 0:2 * P]).then_inc(s["xgT"], 1)
                for t, i, now, one, two in tiles_of(m):
                    if two:
                        wait(dve, s["p_yg"], t - 1)
                        if i == 0:
                            wait(dve, s[f"yg_out{1 - par}"], 8 * (m - 1 - (1 - par)))
                        dve.tensor_copy(yg[1 - par][:, i, :], bank[6 + i][:, 0:D]).then_inc(s["yg"], 1)
                    if now:
                        wait(dve, s["act_g"], t + 1)
                        wait(dve, s["p_hT"], t - 1)
                        dve.tensor_tensor(hid_g[i][:], bank[2 * par + i][:, I:2 * I], act_g[i][:], ALU.mult)\
                           .then_inc(s["hid_g"], 1)

            slot_rounds(dve, step)

            dve.wait_ge(s["x3l"], 16)
            dve.wait_ge(s["sh"], NC)

            def last(c, i, turn):
                def tile(ap, k):
                    return part(ap, c * CT + k, D)
                wait(dve, s[f"rt{i}"], 16 * CT * (turn + 1))
                dve.tensor_tensor(part(rt_all, c, CHUNK), part(rt_all, c, CHUNK), part(shared_all, c, CHUNK),
                                  ALU.add).then_inc(s["ysum"], 1)
                dve.wait_ge(s["ysum"], c + 1)
                for k in range(CT):
                    m = dve.bn_stats(stat[:, k, :], tile(rt_all, k))
                m.then_inc(s["stat"], 1)
                wait_apart(dve, s["stat"], c + 1, s["const"])
                for k in range(CT):
                    dve.bn_aggr(mv[:, k, :], stat[:, k, :]).then_inc(s["mv"], 1)
                wait(dve, s["sd_y"], c + 1)
                dve.reciprocal(rs[:], sd_y[:]).then_inc(s["rs"], 1)
                dve.wait_ge(s["rs"], c + 1)
                for k in range(CT):
                    m = dve.tensor_scalar(tile(res_all, k), tile(rt_all, k), mv[:, k, 0:1], rs[:, k:k + 1],
                                          ALU.subtract, ALU.mult)
                m.then_inc(s["yn"], 1)
                dve.wait_ge(s["yn"], c + 1)
                dve.tensor_tensor(part(res_all, c, CHUNK), part(res_all, c, CHUNK),
                                  part(x3_all[:].rearrange("p k d -> p (k d)"), c, CHUNK),
                                  ALU.add).then_inc(s["res"], 1)
            for c in range(4):
                last(c, c, 0)
            with dve.Fori(0, NC // 4 - 1) as j:
                for i in range(4):
                    last(4 * j + (4 + i), i, j + 1)


def build(nc, t, out):
    def dram(name, shape):
        return nc.dram_tensor(name, shape, F32).ap()

    x1_d = dram("x1_d", (T, B, D))
    x3_d = dram("x3_d", (T * B, D))
    sorted_d = dram("sorted_d", (SLOTS * P, D))
    routed_d = dram("routed_d", (SLOTS * P, D))
    attention_layer(nc, t["x"], t["w_qk"], t["w_v"], t["w_rot"], t["w_out"], t["bonus0"], t["bonus1"], x1_d)
    with ExitStack() as ctx:
        def sb(name, shape, dt=F32):
            return ctx.enter_context(nc.sbuf_tensor(name, shape, dt))
        keep = (sb("xn4T_all", [P, NT * P]), sb("xs_all", [P, NT, D]), sb("oh_all", [P, NT, E], BF16),
                sb("rank_all", [P, NT]), sb("counts", [P, E]))
        mixing_layers(nc, x1_d, x3_d, t["w1"], t["w2"], t["h1"], t["h2"], t["w3"], t["scales"], t["w3_s"],
                      t["wi"], t["wh"], t["rnn_bias"], t["gate"], sorted_d, keep)
        experts_layer(nc, x3_d, sorted_d, routed_d, t["gate_up"], t["down"], t["sh_gate_up"],
                      t["sh_down"], out, keep)


def host_layout(np, i):
    w_rot = np.zeros((P, P), np.float32)
    for h in range(HEADS):
        q = slice(DH * h, DH * (h + 1))
        k = slice(DH * (HEADS + h), DH * (HEADS + h + 1))
        w_rot[q, q] = i["L0_attn_W_nudge"][h]
        w_rot[k, k] = i["L0_attn_simple_roots"].T
    bonus = i["L0_attn_chamber_bonus"].reshape(1, HEADS, 8, 2)
    return {
        "x": i["L0_attn_x"],
        "w_qk": np.concatenate([i["L0_attn_W_q"].T, i["L0_attn_W_k"].T], 1),
        "w_v": i["L0_attn_W_v"].T,
        "w_rot": w_rot,
        "w_out": i["L0_attn_W_out"].T,
        "bonus0": bonus[..., 0],
        "bonus1": bonus[..., 1],
        "w1": i["L0_ffn_w1_w"].T,
        "w2": i["L0_ffn_w2_w"].T,
        "h1": i["L0_ffn_h1_w"].T,
        "h2": i["L0_ffn_h2_w"].T,
        "w3": i["L0_ffn_w3_w"].T,
        "scales": np.stack([i[f"L0_ffn_{k}_s"].reshape(HC, P) for k in ("w1", "w2", "h1", "h2")]).transpose(2, 0, 1),
        "w3_s": i["L0_ffn_w3_s"].reshape(1, D),
        "wi": i["L1_attn_Wi"].T,
        "wh": i["L1_attn_Wh"].T,
        "rnn_bias": np.stack([i["L1_attn_bi"], i["L1_attn_bh"]], 1),
        "gate": i["L1_ffn_gate_w"],
        "sh_gate_up": np.concatenate([i["L1_ffn_shared_gate_w"], i["L1_ffn_shared_up_w"]], 1),
        "sh_down": i["L1_ffn_shared_down_w"],
        "gate_up": np.concatenate([i["L1_ffn_routed_gate_w"], i["L1_ffn_routed_up_w"]], 2),
        "down": i["L1_ffn_routed_down_w"],
    }


def kernel(**inputs):
    import numpy as np
    import concourse.bacc as bacc
    from concourse.bass_utils import run_bass_kernel_spmd

    nc = bacc.Bacc("TRN2", target_bir_lowering=False, num_devices=1)
    arrays, tensors = {}, {}
    for name, a in host_layout(np, {k: np.asarray(v) for k, v in inputs.items()}).items():
        a = np.ascontiguousarray(a)
        arrays[f"in_{name}"] = a
        tensors[name] = nc.dram_tensor(f"in_{name}", a.shape, mybir.dt.from_np(a.dtype), kind="ExternalInput").ap()
    out = nc.dram_tensor("out_0", (B, T, D), F32, kind="ExternalOutput").ap()
    build(nc, tensors, out)
    r = run_bass_kernel_spmd(nc, [arrays], core_ids=[0])
    return r.results[0]["out_0"]
```

```python
from contextlib import ExitStack

import concourse.bass as bass
from concourse import mybir

F32 = mybir.dt.float32
F32R = mybir.dt.float32r
BF16 = mybir.dt.bfloat16
I32 = mybir.dt.int32
ALU = mybir.AluOpType
ACT = mybir.ActivationFunctionType
AX = mybir.AxisListType

P = 128
B, T, D = 32, 256, 128
HEADS, DH, DV = 16, 4, 64
TT = T // P
GH = 4
GROUPS = HEADS // GH
AUG = 32
SC = 384
EPS = 1e-5
NORM_MIN2 = 1e-24
MASKED = -1e38
MAGIC = 0x5f3759df
RING = 8
PAIRS_A = HEADS // 2
BANKS = 2


def wait(eng, sem, value):
    if isinstance(value, int) and value <= 0:
        return
    eng.wait_ge(sem, value)


def wait_apart(eng, sem, value, done):
    if not isinstance(value, int):
        value = eng.snap(eng.to_reg(value))
        eng.wait_ge(done, 1)
    wait(eng, sem, value)


def clear(nc, sems):
    with nc.Block() as block:
        @block.gpsimd
        def _(pool):
            for sem in sems:
                pool.sem_clear(sem)


def attention_layer(nc, x, w_qk, w_v, w_rot, w_out, bonus0, bonus_step, x1_d):
    with ExitStack() as ctx:
        def sb(name, shape, dt=F32):
            return ctx.enter_context(nc.sbuf_tensor(name, shape, dt))

        def ps(name, shape, dt=F32):
            return ctx.enter_context(nc.psum_tensor(name, shape, dt))

        def sem(name):
            return ctx.enter_context(nc.semaphore(name))

        ident = sb("ident", [P, P])
        ident_b = sb("ident_b", [P, P], BF16)
        wqk = sb("wqk", [P, 2 * HEADS * DH])
        wv = sb("wv", [P, HEADS * DV])
        wrot = sb("wrot", [P, P])
        wout = sb("wout", [P, HEADS * DV // P, D])
        bon0 = sb("bon0", [P, HEADS, 8])
        bond = sb("bond", [P, HEADS, 8])
        pick = sb("pick", [P, GROUPS, AUG])
        back_to = sb("back_to", [P, PAIRS_A, 2, DV])
        mask_b = sb("mask_b", [P, P], BF16)
        mask_f = sb("mask_f", [P, P])
        pow_half = sb("pow_half", [P, TT])
        xa = sb("xa", [P, TT, D])
        stat_a = sb("stat_a", [P, TT, 6])
        mv_a = sb("mv_a", [P, TT, 2])
        ve_a = sb("ve_a", [P, TT])
        rstd_a = sb("rstd_a", [P, TT])
        xn = sb("xn", [P, TT, D])
        xnT = [sb(f"xnT{i}", [P, T]) for i in range(2)]
        sq1 = sb("sq1", [P, TT * 2 * HEADS, DH])
        ss1 = sb("ss1", [P, TT * 2 * HEADS])
        ssg1 = sb("ssg1", [P, TT * 2 * HEADS])
        r1 = [sb(f"r1_{i}", [P, TT * 2 * HEADS]) for i in range(4)]
        nt1 = sb("nt1", [P, TT * 2 * HEADS])
        nu1 = sb("nu1", [P, TT * 2 * HEADS])
        qkn = sb("qkn", [P, TT, 2 * HEADS, DH])
        qkT = sb("qkT", [P, T])
        sq2 = sb("sq2", [P, TT, HEADS, DH])
        ss2 = sb("ss2", [P, TT, HEADS])
        ssg2 = sb("ssg2", [P, TT, HEADS])
        r2 = [sb(f"r2_{i}", [P, TT, HEADS]) for i in range(4)]
        nt2 = sb("nt2", [P, TT, HEADS])
        nu2 = sb("nu2", [P, TT, HEADS])
        qraw = sb("qraw", [P, TT, HEADS, DH])
        ek = sb("ek", [P, TT, HEADS, DH])
        ek1 = sb("ek1", [P, TT, HEADS, DH])
        sg = sb("sg", [P, TT, HEADS, DH])
        bt = [sb(f"bt{i}", [P, TT, HEADS, 8 >> i]) for i in range(4)]
        bv = [sb(f"bv{i}", [P, TT, HEADS, 8 >> i]) for i in range(3)]
        q5 = sb("q5", [P, TT, HEADS, DH + 1])
        k5 = sb("k5", [P, TT, HEADS, DH + 1])
        rest = [sb(f"rest{i}", [P, TT * HEADS * (DH + 1)]) for i in range(4)]
        q_part = sb("q_part", [P, 3, TT * HEADS, DH + 1], BF16)
        k_part = sb("k_part", [P, 3, TT * HEADS, DH + 1], BF16)
        q_aug = sb("q_aug", [P, TT * HEADS, AUG], BF16)
        k_aug = sb("k_aug", [P, TT * HEADS, AUG], BF16)
        q_augT = [sb(f"q_augT{i}", [P, GROUPS, T], BF16) for i in range(2)]
        k_augT = [sb(f"k_augT{i}", [P, GROUPS, T], BF16) for i in range(2)]
        bonT = sb("bonT", [HEADS, T])
        cmax = sb("cmax", [HEADS, T])
        val = [sb(f"val{i}", [P, TT, HEADS, DV]) for i in range(2)]
        prob = sb("prob", [P, RING, SC])
        onT = [sb(f"onT{i}", [P, PAIRS_A, T]) for i in range(2)]
        rec = sb("rec", [P, T])
        rec_part = [sb(f"rec_{i}", [P, T], F32R) for i in ("high", "low")]
        back_to_r = sb("back_to_r", [P, PAIRS_A, 2, DV], F32R)
        wv_part = [sb(f"wv_{i}", [P, HEADS * DV], F32R) for i in ("high", "low")]
        xnT_part = [[sb(f"xnT{k}_{i}", [P, T], F32R) for i in ("high", "low")] for k in range(2)]
        y_sb = sb("y_sb", [P, TT * D])
        xr = sb("xr", [P, TT, D])
        stat_y = sb("stat_y", [P, TT, 6])
        mv_y = sb("mv_y", [P, TT, 2])
        ve_y = sb("ve_y", [P, TT])
        rstd_y = sb("rstd_y", [P, TT])
        yn = sb("yn", [P, TT, D])
        x1 = sb("x1", [P, TT, D])

        score = [ps(f"score{j}", [P, 512]) for j in range(BANKS)]
        outp = ps("outp", [P, 2, T])
        total = ps("total", [P, 512])
        spread = ps("spread", [P, 2, T])
        front = ps("front", [P, 512])
        turned = ps("turned", [P, 512])
        turned_b = turned[:, :].bitcast(BF16)
        back = ps("back", [P, 512])

        names = ("w", "const", "xa", "stat_a", "mv_a", "ve_a", "rstd_a", "xn", "p_xnT", "xnT", "p_qk", "sq1", "ss1",
                 "ssg1", "rsq1", "qkn", "p_qkT", "qkT", "p_rot", "sq2", "ek", "qraw", "ss2", "ssg2", "rsq2", "ek1",
                 "sg", "q4", "kcopy", "bon", "p_bonT", "bonT", "cmax", "p_cmax", "q5", "ksplit", "qsplit", "kaug",
                 "qaug", "p_kaT", "p_qaT", "kaT", "qaT", "p_v", "val", "p_score", "prob", "p_out", "raw", "p_sum", "rec",
                 "rec_high", "rec_low", "xnT_high", "xnT_low", "p_bc", "onT", "p_y",
                 "y", "stat_y", "mv_y", "ve_y", "rstd_y", "yn", "xr", "x1", "x1_out")
        s = {name: sem("a_" + name) for name in names}

        STEPS_K = 5
        BON = 11
        RSQ = 10
        N_CONST = 30

        ctx.callback(clear, nc, list(s.values()))
        block = ctx.enter_context(nc.Block())

        def rounds(eng, step):
            def row(b):
                return [v if 0 <= v < B else None for v in (b, b + 1, b + 2, b + 3, b - 1, b - 2)] + [b % 2]
            for b in range(-3, 3):
                step(*row(b))
            with eng.Fori(0, (B - 6) // 2) as i:
                for k in range(2):
                    b = 2 * i + (3 + k)
                    step(b, b + 1, b + 2, b + 3, b - 1, b - 2, 1 - k)
            for b in range(B - 3, B + 2):
                step(*row(b))

        @block.sync
        def _(sp):
            for dst, src in ((wqk[:], w_qk), (wv[:], w_v), (wrot[:], w_rot),
                             (wout[:], w_out.rearrange("(c p) d -> p c d", p=P)),
                             (bon0[:], bonus0.to_broadcast([P, HEADS, 8])),
                             (bond[:], bonus_step.to_broadcast([P, HEADS, 8]))):
                sp.dma_start(dst, src).then_inc(s["w"], 16)

            def step(b, f, n, m, z, y, par):
                if m is not None:
                    wait(sp, s["xn"], m)
                    sp.dma_start(xa[:], x[m].rearrange("(i p) d -> p i d", p=P) if isinstance(m, int)
                                 else x[bass.ds(m, 1)].rearrange("o (i p) d -> p (o i) d", p=P)).then_inc(s["xa"], 16)
                if y is not None:
                    wait(sp, s["x1"], y)
                    sp.dma_start(xr[:], x[y].rearrange("(i p) d -> p i d", p=P) if isinstance(y, int)
                                 else x[bass.ds(y, 1)].rearrange("o (i p) d -> p (o i) d", p=P)).then_inc(s["xr"], 16)
                    wait(sp, s["x1"], y + 1)
                    sp.dma_start(x1_d[:, y, :].rearrange("(i p) d -> p i d", p=P) if isinstance(y, int)
                                 else x1_d[:, bass.ds(y, 1), :].rearrange("(i p) o d -> p (i o) d", p=P),
                                 x1[:]).then_inc(s["x1_out"], 16)

            rounds(sp, step)
            sp.wait_ge(s["x1_out"], 16 * B)

        @block.gpsimd
        def _(pool):
            def const(ins):
                const.n += 1
                ins.then_inc(s["const"], 1)
                pool.wait_ge(s["const"], const.n)
            const.n = 0
            const(pool.memset(ident[:], 0.0))
            const(pool.affine_select(out=ident[:], in_=ident[:], compare_op=ALU.not_equal, fill=1.0, base=0,
                                     pattern=[[-1, P]], channel_multiplier=1))
            const(pool.tensor_copy(ident_b[:], ident[:]))
            const(pool.memset(pow_half[:], -0.5))
            const(pool.memset(q_aug[:], 0.0))
            const(pool.memset(k_aug[:], 0.0))
            const(pool.memset(q_aug[:, :, 27:30], 1.0))
            const(pool.memset(k_aug[:, :, 24:27], 1.0))
            const(pool.memset(pick[:], 0.0))
            const(pool.memset(pick[:, :, GROUPS:], 1.0))
            for g in range(GROUPS):
                const(pool.memset(pick[:, g, g:g + 1], 1.0))
            const(pool.memset(back_to[:], 0.0))
            for q in range(PAIRS_A):
                const(pool.affine_select(out=back_to[:, q], in_=back_to[:, q], compare_op=ALU.not_equal, fill=1.0,
                                         base=-(2 * AUG * (q % 2) + q // 2), pattern=[[-AUG, 2], [0, DV]],
                                         channel_multiplier=1))
            const(pool.memset(mask_f[:], 0.0))
            const(pool.affine_select(out=mask_f[:], in_=mask_f[:], compare_op=ALU.is_ge, fill=MASKED, base=0,
                                     pattern=[[1, P]], channel_multiplier=-1))
            const(pool.tensor_copy(mask_b[:], mask_f[:]))
            pool.wait_ge(s["w"], 96)
            const(pool.tensor_tensor(bond[:], bond[:], bon0[:], ALU.subtract))
            const(pool.tensor_scalar(back_to_r[:], back_to[:], 1.0, 0.0, ALU.mult, ALU.add))
            const(pool.tensor_scalar(wv_part[0][:], wv[:], 1.0, 0.0, ALU.mult, ALU.add))
            const(pool.tensor_tensor(wv_part[1][:], wv[:], wv_part[0][:].bitcast(F32), ALU.subtract))

            def split(value, part, name, n):
                v = value[:].rearrange("p i h c -> p (i h c)")
                parts = [part[:, k].rearrange("p r c -> p (r c)") for k in range(3)]
                c = 0
                for k in range(3):
                    pool.tensor_scalar(parts[k], v, 1.0, 0.0, ALU.mult, ALU.add).then_inc(s[name], 1)
                    c += 1
                    if k < 2:
                        wait_apart(pool, s[name], STEPS_K * n + c, s["const"])
                        pool.tensor_tensor(rest[k + (2 if name == "qsplit" else 0)][:], v, parts[k],
                                           ALU.subtract).then_inc(s[name], 1)
                        c += 1
                        wait_apart(pool, s[name], STEPS_K * n + c, s["const"])
                        v = rest[k + (2 if name == "qsplit" else 0)][:]

            def rstd(mv, ve, out, name, n):
                wait_apart(pool, s["mv_" + name], TT * (n + 1), s["const"])
                pool.tensor_scalar(ve[:], mv[:, :, 1], 1.0, EPS, ALU.mult, ALU.add).then_inc(s["ve_" + name], 1)
                wait_apart(pool, s["ve_" + name], n + 1, s["const"])
                pool.tensor_tensor(out[:], ve[:], pow_half[:], ALU.pow).then_inc(s["rstd_" + name], 1)

            def bonus(n):
                wait_apart(pool, s["sg"], n + 1, s["const"])
                wait_apart(pool, s["p_bonT"], n, s["const"])
                def did(ins):
                    did.c += 1
                    ins.then_inc(s["bon"], 1)
                    wait_apart(pool, s["bon"], BON * n + did.c, s["const"])
                did.c = 0
                def sig(r, w):
                    return sg[:, :, :, r:r + 1].to_broadcast([P, TT, HEADS, w])
                step_b = bond[:].rearrange("p (o h) c -> p o h c", o=1).to_broadcast([P, TT, HEADS, 8])
                base_b = bon0[:].rearrange("p (o h) c -> p o h c", o=1).to_broadcast([P, TT, HEADS, 8])
                did(pool.tensor_tensor(bt[0][:], sig(0, 8), step_b, ALU.mult))
                did(pool.tensor_tensor(bv[0][:], bt[0][:], base_b, ALU.add))
                for r in range(1, 4):
                    pair = bv[r - 1][:].rearrange("p i h (c two) -> p (i h) c two", two=2)
                    w = 8 >> r
                    t = bt[r][:].rearrange("p i h c -> p (i h) c")
                    sr = sg[:].rearrange("p i h r -> p (i h) r")[:, :, r:r + 1].to_broadcast([P, TT * HEADS, w])
                    did(pool.tensor_tensor(t, pair[:, :, :, 1], pair[:, :, :, 0], ALU.subtract))
                    did(pool.tensor_tensor(t, t, sr, ALU.mult))
                    out = bv[r][:].rearrange("p i h c -> p (i h) c") if r < 3 \
                        else k5[:].rearrange("p i h c -> p (i h) c")[:, :, DH:DH + 1]
                    did(pool.tensor_tensor(out, t, pair[:, :, :, 0], ALU.add))

            def step(b, f, n, m, z, y, par):
                if f is not None:
                    wait_apart(pool, s["qkn"], f + 1, s["const"])
                    pool.tensor_scalar(k5[:, :, :, 0:DH], qkn[:, :, HEADS:, :], 1.0, 0.0,
                                       ALU.mult, ALU.add).then_inc(s["kcopy"], 1)
                    bonus(f)
                    wait_apart(pool, s["kcopy"], f + 1, s["const"])
                    wait_apart(pool, s["p_kaT"], f, s["const"])
                    split(k5, k_part, "ksplit", f)
                    wait_apart(pool, s["ksplit"], STEPS_K * (f + 1), s["const"])
                    kp = k_part[:].rearrange("p k r c -> p r k c")
                    rows = k_aug[:].rearrange("p r (m c) -> p r m c", c=DH)
                    pool.tensor_scalar(rows[:, :, 0:3, :], kp[:, :, :, 0:DH], 1.0, 0.0, ALU.mult, ALU.add)
                    pool.tensor_scalar(rows[:, :, 3:5, :], kp[:, :, 0:2, 0:DH], 1.0, 0.0, ALU.mult, ALU.add)
                    pool.tensor_scalar(rows[:, :, 5, :], kp[:, :, 0, 0:DH], 1.0, 0.0, ALU.mult, ALU.add)
                    pool.tensor_scalar(k_aug[:, :, 27:30], kp[:, :, :, DH], 1.0, 0.0,
                                       ALU.mult, ALU.add).then_inc(s["kaug"], 1)
                if y is not None:
                    rstd(mv_y, ve_y, rstd_y, "y", y)
                if m is not None:
                    rstd(mv_a, ve_a, rstd_a, "a", m)
                if f is not None:
                    wait_apart(pool, s["q5"], f + 1, s["const"])
                    wait_apart(pool, s["p_qaT"], f, s["const"])
                    split(q5, q_part, "qsplit", f)
                    wait_apart(pool, s["qsplit"], STEPS_K * (f + 1), s["const"])
                    qp = q_part[:].rearrange("p k r c -> p r k c")
                    rows = q_aug[:].rearrange("p r (m c) -> p r m c", c=DH)
                    for lo, hi, k in ((0, 3, 0), (3, 5, 1), (5, 6, 2)):
                        pool.tensor_scalar(rows[:, :, lo:hi, :],
                                           qp[:, :, k:k + 1, 0:DH].to_broadcast([P, TT * HEADS, hi - lo, DH]),
                                           1.0, 0.0, ALU.mult, ALU.add)
                    pool.tensor_scalar(q_aug[:, :, 24:27], qp[:, :, :, DH], 1.0, 0.0,
                                       ALU.mult, ALU.add).then_inc(s["qaug"], 1)

            rounds(pool, step)

        @block.tensor
        def _(pe):
            pe.wait_ge(s["const"], N_CONST)
            pe.wait_ge(s["w"], 96)

            def scores(b, par, *heads):
                if b is None:
                    return
                for h in heads:
                    g, j = h // GH, h % GH
                    if h == 0:
                        wait(pe, s["qaT"], b + 1)
                        wait(pe, s["kaT"], b + 1)
                    wait(pe, s["prob"], HEADS * b + max(h - BANKS + 1, 0))
                    bank = score[h % BANKS]
                    r = slice(AUG * j, AUG * (j + 1))
                    pe.matmul(bank[:, 0:T], k_augT[par][r, g, 0:P], q_augT[par][r, g, :], start=True, stop=True,
                              tile_position=(AUG * j, 0))
                    pe.matmul(bank[:, T:SC], k_augT[par][r, g, P:T], q_augT[par][r, g, P:T], start=False,
                              stop=True, tile_position=(AUG * j, 0), skip_group_check=True)
                    for o in (0, T):
                        m = pe.matmul(bank[:, o:o + P], ident_b[:], mask_b[:], start=False, stop=True,
                                      skip_group_check=True)
                    m.then_inc(s["p_score"], 1)

            def weighted(b, par, p):
                if b is None:
                    return
                if p == 0:
                    wait(pe, s["val"], 4 * (b + 1))
                wait(pe, s["prob"], HEADS * b + 2 * p + 2)
                wait(pe, s["raw"], GROUPS * b + p // 2)
                for k, (q, w) in enumerate(((slice(0, T), slice(0, T)), (slice(P, T), slice(T, SC)))):
                    for i in range(2):
                        h = 2 * p + i
                        m = pe.matmul(outp[DV * i:DV * (i + 1), p % 2, q], val[par][:, k, h, :],
                                      prob[:, h % RING, w], start=(k == 0), stop=(k == 1),
                                      tile_position=(0, DV * i), skip_group_check=True)
                m.then_inc(s["p_out"], 1)

            def sums(b, g):
                if b is None:
                    return
                if g == 0:
                    wait(pe, s["rec"], b)
                for k, (q, w) in enumerate(((slice(0, T), slice(0, T)), (slice(P, T), slice(T, SC)))):
                    for j in range(GH):
                        m = pe.matmul(total[AUG * j:AUG * (j + 1), q], pick[:, g, :],
                                      prob[:, (GH * g + j) % RING, w], start=(g == 0 and k == 0),
                                      stop=(g == GROUPS - 1 and k == 1), tile_position=(0, AUG * j),
                                      skip_group_check=True)
                m.then_inc(s["p_sum"], 1)

            def spread_out(z, g):
                if z is None:
                    return
                if g == 0:
                    wait(pe, s["rec_low"], z + 1)
                    wait(pe, s["q5"], min(z + 2, B) if isinstance(z, int) else z + 2)
                if g == 2:
                    wait(pe, s["q5"], min(z + 3, B) if isinstance(z, int) else z + 3)
                wait(pe, s["onT"], GROUPS * z + g)
                for i in range(2):
                    left = back_to_r[:, 2 * g + i].rearrange("p i d -> p (i d)")
                    pe.matmul(spread[:, i, :], left, rec_part[0][:], start=True, stop=False)
                    m = pe.matmul(spread[:, i, :], left, rec_part[1][:], start=False, stop=True)
                m.then_inc(s["p_bc"], 1)

            def output(z, par, pieces):
                if z is None:
                    return
                for c in pieces:
                    if c == 0:
                        wait(pe, s["y"], z)
                        wait(pe, s["val"], 4 * min(z + 3, B) if isinstance(z, int) else 4 * (z + 3))
                    wait(pe, s["onT"], GROUPS * z + c // 2 + 1)
                    for i in range(TT):
                        m = pe.matmul(back[:, i * P:(i + 1) * P], onT[1 - par][:, c, i * P:(i + 1) * P],
                                      wout[:, c, :], start=(c == 0 and i == 0), stop=(c == PAIRS_A - 1),
                                      skip_group_check=True)
                if c == PAIRS_A - 1:
                    m.then_inc(s["p_y"], 1)

            def values(f, par, k):
                if f is None:
                    return
                if k == 0:
                    wait(pe, s["y"], f - 2)
                wait(pe, s["val"], 4 * f + k)
                wait(pe, s["xnT_low"], f + 1)
                for n, (x_part, w_part) in enumerate(((0, 0), (0, 1), (1, 0))):
                    m = pe.matmul(back[:, :], xnT_part[1 - par][x_part][:, (k // 2) * P:(k // 2 + 1) * P],
                                  wv_part[w_part][:, (k % 2) * 512:(k % 2 + 1) * 512], start=(n == 0), stop=(n == 2))
                m.then_inc(s["p_v"], 1)

            def step(b, f, n, m, z, y, par):
                values(f, par, 0)
                scores(b, par, 0, 1)
                if n is not None:
                    wait(pe, s["xn"], n + 1)
                    wait(pe, s["qraw"], n)
                    for i in range(TT):
                        mm = pe.transpose(front[:, i * P:(i + 1) * P], xn[:, i, :], ident[:])
                    mm.then_inc(s["p_xnT"], 1)
                values(f, par, 1)
                scores(b, par, 2, 3)
                if n is not None:
                    wait(pe, s["xnT"], n + 1)
                    for i in range(TT):
                        mm = pe.matmul(front[:, T + i * P:T + (i + 1) * P], xnT[par][:, i * P:(i + 1) * P], wqk[:],
                                       start=True, stop=True)
                    mm.then_inc(s["p_qk"], 1)
                spread_out(z, 0)
                weighted(b, par, 0)
                scores(b, par, 4, 5)
                weighted(b, par, 1)
                sums(b, 0)
                values(f, par, 2)
                scores(b, par, 6, 7)
                spread_out(z, 1)
                scores(b, par, 8, 9)
                weighted(b, par, 2)
                values(f, par, 3)
                weighted(b, par, 3)
                sums(b, 1)
                if f is not None:
                    wait(pe, s["bon"], BON * (f + 1))
                    wait(pe, s["q5"], f)
                    if z is not None:
                        wait(pe, s["onT"], GROUPS * z + 2)
                    for i in range(TT):
                        mm = pe.matmul(spread[0:HEADS, 0, i * P:(i + 1) * P], k5[:, i, :, DH], ident[:],
                                       start=True, stop=True)
                    mm.then_inc(s["p_bonT"], 1)
                scores(b, par, 10, 11)
                if n is not None:
                    wait(pe, s["qkn"], n + 1)
                    for i in range(TT):
                        mm = pe.transpose(front[:, i * P:(i + 1) * P], qkn[:, i].rearrange("p h c -> p (h c)"),
                                          ident[:])
                    mm.then_inc(s["p_qkT"], 1)
                weighted(b, par, 4)
                output(z, par, range(0, 4))
                if f is not None:
                    wait(pe, s["cmax"], f + 1)
                    for i in range(TT):
                        mm = pe.matmul(spread[:, 1, i * HEADS:(i + 1) * HEADS], cmax[:, i * P:(i + 1) * P],
                                       ident[0:HEADS, 0:HEADS], start=True, stop=True)
                    mm.then_inc(s["p_cmax"], 1)
                weighted(b, par, 5)
                sums(b, 2)
                spread_out(z, 2)
                scores(b, par, 12, 13)
                if n is not None:
                    wait(pe, s["qkT"], n + 1)
                    for i in range(TT):
                        mm = pe.matmul(front[:, T + i * P:T + (i + 1) * P], qkT[:, i * P:(i + 1) * P], wrot[:],
                                       start=True, stop=True)
                    mm.then_inc(s["p_rot"], 1)

                def turn_operands(aug, name, last, count):
                    wait(pe, s[name + "aug"], f + 1)
                    wait(pe, s[last], count)
                    for g in range(GROUPS):
                        for i in range(TT):
                            o = (g * TT + i) * P
                            mm = pe.transpose(turned_b[:, o:o + P],
                                              aug[:, i * HEADS + GH * g:i * HEADS + GH * (g + 1), :]
                                              .rearrange("p h c -> p (h c)"), ident_b[:])
                    mm.then_inc(s[f"p_{name}aT"], 1)
                if f is not None:
                    turn_operands(k_aug, "k", "qaT", f)
                spread_out(z, 3)
                weighted(b, par, 6)
                scores(b, par, 14, 15)
                output(z, par, range(4, 6))
                weighted(b, par, 7)
                sums(b, 3)
                output(z, par, range(6, 8))
                if f is not None:
                    turn_operands(q_aug, "q", "kaT", f + 1)

            rounds(pe, step)

        @block.scalar
        def _(act):
            act.wait_ge(s["const"], N_CONST)

            def weights(b, *heads):
                if b is None:
                    return
                for h in heads:
                    wait(act, s["p_sum"], GROUPS * b + (h - RING) // GH + 1)
                    wait(act, s["p_score"], HEADS * b + h + 1)
                    act.activation(prob[:, h % RING, :], score[h % BANKS][:, 0:SC], ACT.Exp).then_inc(s["prob"], 1)

            def copy_out(b, par, g):
                if b is None:
                    return
                wait(act, s["p_out"], PAIRS_A * b + 2 * g + 2)
                if g == 0:
                    wait(act, s["p_y"], b - 1)
                act.activation(onT[par][:, 2 * g:2 * g + 2, :], outp[:], ACT.Copy).then_inc(s["raw"], 1)

            def copy_values(f, par, k):
                if f is None:
                    return
                if k == 0:
                    wait(act, s["p_out"], PAIRS_A * (f - 1))
                wait(act, s["p_v"], 4 * f + k + 1)
                act.activation(val[1 - par][:, k // 2, (k % 2) * 8:(k % 2) * 8 + 8, :],
                               back[:, :].rearrange("p (h v) -> p h v", h=8), ACT.Copy).then_inc(s["val"], 1)

            def step(b, f, n, m, z, y, par):
                copy_values(f, par, 0)
                weights(b, 0, 1)
                if n is not None:
                    wait(act, s["p_xnT"], n + 1)
                    wait(act, s["p_v"], 4 * (n - 1))
                    act.activation(xnT[par][:], front[:, 0:T], ACT.Copy).then_inc(s["xnT"], 1)
                copy_values(f, par, 1)
                weights(b, 2, 3)
                if n is not None:
                    wait(act, s["p_qk"], n + 1)
                    wait(act, s["ss1"], n)
                    act.activation(sq1[:].rearrange("p r c -> p (r c)"), front[:, T:2 * T],
                                   ACT.Square).then_inc(s["sq1"], 1)
                if n is not None:
                    act.wait_ge(s["xnT"], n + 1)
                    act.activation(xnT_part[par][0][:], xnT[par][:], ACT.Copy).then_inc(s["xnT_high"], 1)
                weights(b, 4, 5)
                copy_out(b, par, 0)
                copy_values(f, par, 2)
                weights(b, 6, 7)
                weights(b, 8, 9)
                copy_values(f, par, 3)
                copy_out(b, par, 1)
                weights(b, 10, 11)
                if n is not None:
                    wait(act, s["p_qkT"], n + 1)
                    act.activation(qkT[:], front[:, 0:T], ACT.Copy).then_inc(s["qkT"], 1)
                copy_out(b, par, 2)
                weights(b, 12, 13)
                if n is not None:
                    wait(act, s["p_rot"], n + 1)
                    wait(act, s["q4"], n)
                    fr = front[:, T:2 * T].rearrange("p (i k h c) -> p i k h c", i=TT, k=2, c=DH)
                    act.activation(ek[:], fr[:, :, 1], ACT.Exp, scale=-3.0).then_inc(s["ek"], 1)
                    act.activation(sq2[:], fr[:, :, 0], ACT.Square).then_inc(s["sq2"], 1)
                    act.activation(qraw[:], fr[:, :, 0], ACT.Copy).then_inc(s["qraw"], 1)
                weights(b, 14, 15)
                copy_out(b, par, 3)
                if z is not None:
                    wait(act, s["p_y"], z + 1)
                    wait(act, s["yn"], z)
                    act.activation(y_sb[:], back[:, 0:TT * D], ACT.Copy).then_inc(s["y"], 1)
                if f is not None:
                    wait(act, s["p_qaT"], f + 1)
                    wait(act, s["p_score"], HEADS * (f - 1))
                    act.activation(q_augT[1 - par][:].rearrange("p g t -> p (g t)"), turned_b[:, :],
                                   ACT.Copy).then_inc(s["qaT"], 1)

            rounds(act, step)

        @block.vector
        def _(dve):
            def stats(src, stat, mv, name, n):
                for i in range(TT):
                    m = dve.bn_stats(stat[:, i, :], src[:, i * D:(i + 1) * D])
                m.then_inc(s["stat_" + name], 1)
                wait_apart(dve, s["stat_" + name], n + 1, s["const"])
                for i in range(TT):
                    dve.bn_aggr(mv[:, i, :], stat[:, i, :]).then_inc(s["mv_" + name], 1)

            def rsqrt(ssg, r, nt, nu, name, n, half):
                def did(ins):
                    did.c += 1
                    ins.then_inc(s[name], 1)
                    dve.wait_ge(s[name], RSQ * n + did.c)
                did.c = 0
                did(dve.tensor_scalar(r[0][:].bitcast(I32), ssg[:].bitcast(I32), -0.5, float(MAGIC),
                                      ALU.mult, ALU.add))
                for k in range(3):
                    w = half if k == 2 else 0.5
                    did(dve.tensor_tensor(nt[:], ssg[:], r[k][:], ALU.mult))
                    did(dve.scalar_tensor_tensor(out=nu[:], in0=nt[:], scalar=-w, in1=r[k][:], op0=ALU.mult,
                                                 op1=ALU.mult))
                    did(dve.scalar_tensor_tensor(out=r[k + 1][:], in0=nu[:], scalar=3 * w, in1=r[k][:],
                                                 op0=ALU.add, op1=ALU.mult))

            dve.wait_ge(s["const"], N_CONST)

            def reciprocal(z):
                if z is None:
                    return
                wait(dve, s["p_sum"], GROUPS * (z + 1))
                wait(dve, s["p_bc"], GROUPS * z)
                dve.reciprocal(rec[:], total[:, 0:T]).then_inc(s["rec"], 1)
                dve.wait_ge(s["rec"], z + 1)
                dve.tensor_copy(rec_part[0][:], rec[:]).then_inc(s["rec_high"], 1)
                dve.wait_ge(s["rec_high"], z + 1)
                dve.tensor_tensor(rec_part[1][:], rec[:], rec_part[0][:].bitcast(F32),
                                  ALU.subtract).then_inc(s["rec_low"], 1)

            def normalise(z, par, g):
                if z is None:
                    return
                wait(dve, s["p_bc"], GROUPS * z + g + 1)
                wait(dve, s["raw"], GROUPS * z + g + 1)
                o = onT[1 - par][:, 2 * g:2 * g + 2, :]
                dve.tensor_tensor(o, spread[:], o, ALU.mult).then_inc(s["onT"], 1)

            def step(b, f, n, m, z, y, par):
                if f is not None:
                    wait(dve, s["ek"], f + 1)
                    wait(dve, s["bon"], BON * f)
                    dve.tensor_scalar(ek1[:], ek[:], 1.0, None, ALU.add).then_inc(s["ek1"], 1)
                    wait(dve, s["sq2"], f + 1)
                    dve.tensor_reduce(ss2[:], sq2[:], AX.X, ALU.add).then_inc(s["ss2"], 1)
                    dve.wait_ge(s["ek1"], f + 1)
                    dve.reciprocal(sg[:], ek1[:]).then_inc(s["sg"], 1)
                    dve.wait_ge(s["ss2"], f + 1)
                    dve.tensor_scalar(ssg2[:], ss2[:], NORM_MIN2, None, ALU.max).then_inc(s["ssg2"], 1)
                    dve.wait_ge(s["ssg2"], f + 1)
                reciprocal(z)
                if f is not None:
                    rsqrt(ssg2, r2, nt2, nu2, "rsq2", f, 0.25)
                    wait(dve, s["qsplit"], STEPS_K * f)
                    wait(dve, s["qraw"], f + 1)
                    dve.tensor_tensor(q5[:, :, :, 0:DH], qraw[:],
                                      r2[3][:].rearrange("p i (h o) -> p i h o", o=1)
                                      .to_broadcast([P, TT, HEADS, DH]), ALU.mult).then_inc(s["q4"], 1)
                if n is not None:
                    wait(dve, s["sq1"], n + 1)
                    dve.tensor_reduce(ss1[:], sq1[:], AX.X, ALU.add).then_inc(s["ss1"], 1)
                    dve.wait_ge(s["ss1"], n + 1)
                    dve.tensor_scalar(ssg1[:], ss1[:], NORM_MIN2, None, ALU.max).then_inc(s["ssg1"], 1)
                    dve.wait_ge(s["ssg1"], n + 1)
                normalise(z, par, 0)
                if n is not None:
                    rsqrt(ssg1, r1, nt1, nu1, "rsq1", n, 0.5)
                    wait(dve, s["kcopy"], n)
                    dve.tensor_tensor(qkn[:].rearrange("p i h c -> p (i h) c"),
                                      front[:, T:2 * T].rearrange("p (r c) -> p r c", c=DH),
                                      r1[3][:].rearrange("p (r o) -> p r o", o=1)
                                      .to_broadcast([P, TT * 2 * HEADS, DH]), ALU.mult).then_inc(s["qkn"], 1)
                if n is not None:
                    wait(dve, s["xnT_high"], n + 1)
                    wait(dve, s["p_v"], 4 * (n - 1))
                    dve.tensor_tensor(xnT_part[par][1][:], xnT[par][:], xnT_part[par][0][:].bitcast(F32),
                                      ALU.subtract).then_inc(s["xnT_low"], 1)
                normalise(z, par, 1)
                if f is not None:
                    wait(dve, s["p_bonT"], f + 1)
                    dve.tensor_copy(bonT[:], spread[0:HEADS, 0, :]).then_inc(s["bonT"], 1)
                    dve.wait_ge(s["bonT"], f + 1)
                    wait(dve, s["p_cmax"], f)
                    dve.tensor_tensor_scan(out=cmax[:], data0=bonT[:], data1=bonT[:], initial=bonT[:, 0:1],
                                           op0=ALU.max, op1=ALU.max).then_inc(s["cmax"], 1)
                if f is not None:
                    wait(dve, s["p_cmax"], f + 1)
                    dve.tensor_scalar(q5[:, :, :, DH], spread[:, 1, 0:TT * HEADS].rearrange("p (i h) -> p i h", i=TT),
                                      -1.0, None, ALU.mult).then_inc(s["q5"], 1)
                normalise(z, par, 2)
                if y is not None:
                    wait(dve, s["y"], y + 1)
                    stats(y_sb, stat_y, mv_y, "y", y)
                if m is not None:
                    wait(dve, s["xa"], 16 * (m + 1))
                    stats(xa[:].rearrange("p i d -> p (i d)"), stat_a, mv_a, "a", m)
                normalise(z, par, 3)
                if y is not None:
                    wait(dve, s["rstd_y"], y + 1)
                    for i in range(TT):
                        mm = dve.tensor_scalar(yn[:, i, :], y_sb[:, i * D:(i + 1) * D], mv_y[:, i, 0:1],
                                               rstd_y[:, i:i + 1], ALU.subtract, ALU.mult)
                    mm.then_inc(s["yn"], 1)
                    dve.wait_ge(s["yn"], y + 1)
                    wait(dve, s["xr"], 16 * (y + 1))
                    wait(dve, s["x1_out"], 16 * y)
                    dve.tensor_tensor(x1[:], yn[:], xr[:], ALU.add).then_inc(s["x1"], 1)
                if m is not None:
                    wait(dve, s["rstd_a"], m + 1)
                    wait(dve, s["p_xnT"], m)
                    for i in range(TT):
                        mm = dve.tensor_scalar(xn[:, i, :], xa[:, i, :], mv_a[:, i, 0:1], rstd_a[:, i:i + 1],
                                               ALU.subtract, ALU.mult)
                    mm.then_inc(s["xn"], 1)
                if f is not None:
                    wait(dve, s["p_kaT"], f + 1)
                    wait(dve, s["p_score"], HEADS * (f - 1))
                    dve.tensor_copy(k_augT[1 - par][:].rearrange("p g t -> p (g t)"), turned_b[:, :])\
                       .then_inc(s["kaT"], 1)

            rounds(dve, step)


CHUNK = 512
CT = CHUNK // P
NC = B * T // CHUNK
STEPS = CHUNK // B
HID = 512
HC = HID // P
E = 32
NT = B * T // P


def part(t, i, n):
    return t[:, i * n:(i + 1) * n] if isinstance(i, int) else t[:, bass.ds(i * n, n)]


def mixing_layers(nc, x1_d, x3_d, w1, w2, h1, h2, w3, scales, w3_scale, wi, wh, rnn_bias, gate, sorted_d, keep):
    with ExitStack() as ctx:
        def sb(name, shape, dt=F32):
            return ctx.enter_context(nc.sbuf_tensor(name, shape, dt))

        def ps(name, shape, dt=F32):
            return ctx.enter_context(nc.psum_tensor(name, shape, dt))

        def sem(name):
            return ctx.enter_context(nc.semaphore(name))

        ident = sb("ident2", [P, P])
        before = sb("before", [P, P], BF16)
        ones = sb("ones", [P, P], BF16)
        pow_half = sb("pow_half2", [P, CT])
        rev = sb("rev", [P, E])
        w3_sb = sb("w3_sb", [P, HC, D])
        w1_part = [sb(f"w1_{n}", [P, HID], F32R) for n in ("high", "low")]
        w2_part = [sb(f"w2_{n}", [P, HID], F32R) for n in ("high", "low")]
        h1_part = [sb(f"h1_{n}", [P, HC, HID], F32R) for n in ("high", "low")]
        h2_part = [sb(f"h2_{n}", [P, HC, HID], F32R) for n in ("high", "low")]
        sc = sb("sc", [P, 4, HC])
        sc_half = sb("sc_half", [P, HC])
        sc_prod = sb("sc_prod", [P, HC])
        w3s = sb("w3s", [P, D])
        wi_sb = sb("wi_sb", [P, D])
        wh_sb = sb("wh_sb", [P, D])
        rb = sb("rb", [P, 2])
        bias = sb("bias", [P, 1])
        gate_sb = sb("gate_sb", [P, E])

        x1c = sb("x1c", [P, CT, D])
        xn2 = sb("xn2", [P, CT, D])
        xn2T_part = [sb(f"xn2T_{n}", [P, CHUNK], F32R) for n in ("high", "low")]
        th = [sb(f"th{i}", [P, CHUNK]) for i in range(2)]
        hT = [sb(f"hT{i}", [P, HC, CHUNK]) for i in range(3)]
        hT_part = [[sb(f"hT{i}_{n}", [P, HC, CHUNK], F32R) for n in ("high", "low")] for i in range(2)]
        x1v = sb("x1v", [P, CT, D])
        hs = sb("hs", [P, CT, D])
        w1_sb, w2_sb, h1_sb, h2_sb = th[0], th[1], hT[0], hT[1]
        y = sb("y", [P, CT, D])
        x2 = [sb(f"x2{i}", [P, CT, D]) for i in range(2)]
        xn3 = sb("xn3", [P, CT, D])
        xn3T = sb("xn3T", [P, CHUNK])
        state = sb("state", [P, CHUNK])
        x3 = sb("x3", [P, CT, D])
        xn4 = sb("xn4", [P, CT, D])
        stat = {n: sb("bstat_" + n, [P, CT, 6]) for n in "fyxhe"}
        mv = {n: sb("bmv_" + n, [P, CT, 2]) for n in "fyxhe"}
        ve = {n: sb("bve_" + n, [P, CT]) for n in "fyxhe"}
        rs = {n: sb("brs_" + n, [P, CT]) for n in "fyxhe"}
        top = sb("top", [P, CT])
        is_top = sb("is_top", [P, CT, E])
        rtop = sb("rtop", [P, CT, E])
        first = sb("first", [P, CT])
        tanh_top = sb("tanh_top", [P, CT])
        gate_val = sb("gate_val", [P, CT])
        pre = sb("pre", [P, CT, E])
        pre_oh = sb("pre_oh", [P, CT, E])
        xn4T = sb("xn4T", [P, CHUNK])
        onehot = sb("onehot", [P, CT, E], BF16)
        xn4T_all, xs_all, oh_all, rank_all, counts = keep

        main = [ps(f"main{i}", [P, CHUNK]) for i in range(4)]
        yp = ps("yp", [P, CHUNK])
        turn = ps("turn", [P, CHUNK])
        xi = ps("xi", [P, CHUNK])
        route = ps("route", [P, CHUNK])

        names = ("w", "const", "xc0", "xc1", "p_xn2T", "xn2", "xn2T", "xn2T_low",
                 "h1_high", "h1_low", "h2_low", "split", "p_a", "p_g", "tanh", "ag", "h1", "p_h1", "p_h2", "h2", "h3",
                 "p_y", "y", "yn", "x2", "xn3", "p_xn3T", "xn3T", "p_xi", "p_step", "step", "p_state",
                 "hs", "xv", "hn", "x3",
                 "x3_out", "xn4", "p_xn4T", "xn4T", "p_logit", "top", "is_top", "rtop", "first", "onehot",
                 "tanh_top", "gate_val", "xs", "p_rank", "pre", "pre_oh", "rank", "counts", "zeros", "zero", "kept")
        s = {name: sem("b_" + name) for name in names}
        for n in "fyxhe":
            for k in ("stat", "mv", "ve", "rs"):
                s[k + n] = sem(f"b_{k}_{n}")
        N_CONST = 11

        ctx.callback(clear, nc, list(s.values()))
        block = ctx.enter_context(nc.Block())

        def rounds(eng, step):
            def row(k, par):
                return [v if not isinstance(v, int) or 0 <= v < NC else None for v in
                        (k, k - 1, k - 2, k - 3, k - 4, k - 5, k - 6)] + [par]
            for k in range(8):
                step(*row(k, k % 2))
            with eng.Fori(0, (NC - 8) // 2) as i:
                for par in range(2):
                    step(*row(2 * i + (8 + par), par))
            for k in range(NC, NC + 6):
                step(*row(k, k % 2))

        x1_rows = x1_d.rearrange("(c k u) b d -> c (u b) k d", k=CT, u=P // B)
        x3_rows = x3_d.rearrange("(c k p) d -> c p k d", k=CT, p=P)

        def chunk_of(ap, c):
            return ap[c] if isinstance(c, int) else ap[bass.ds(c, 1)].rearrange("o p k d -> p (o k) d")

        @block.sync
        def _(sp):
            for dst, src in ((w1_sb[:], w1), (w2_sb[:], w2), (wi_sb[:], wi), (wh_sb[:], wh), (gate_sb[:], gate),
                             (sc[:], scales), (rb[:], rnn_bias), (w3s[:], w3_scale.to_broadcast([P, D])),
                             (h1_sb[:], h1.rearrange("(c p) n -> p c n", p=P)),
                             (h2_sb[:], h2.rearrange("(c p) n -> p c n", p=P)),
                             (w3_sb[:], w3.rearrange("(c p) n -> p c n", p=P))):
                sp.dma_start(dst, src).then_inc(s["w"], 16)

            def step(p, a, c, v, r, h, q, par):
                if p is not None:
                    wait(sp, s["xn2"], p)
                    sp.dma_start(x1c[:], chunk_of(x1_rows, p)).then_inc(s[f"xc{par}"], 16)
                if v is not None:
                    wait(sp, s["x2"], v)
                    sp.dma_start(x1v[:], chunk_of(x1_rows, v)).then_inc(s["xv"], 16)
                if h is not None:
                    wait(sp, s["x3"], h + 1)
                    sp.dma_start(chunk_of(x3_rows, h), x3[:]).then_inc(s["x3_out"], 16)

            rounds(sp, step)
            sp.wait_ge(s["zeros"], 1)
            slots = sorted_d.rearrange("(g p k) d -> g p (k d)", p=P, k=16)
            for g in range(slots.shape[0]):
                sp.dma_start(slots[g], hT[2][:].rearrange("p k t -> p (k t)")).then_inc(s["zero"], 16)
            sp.wait_ge(s["zero"], 16 * slots.shape[0])
            sp.wait_ge(s["x3_out"], 16 * NC)

        @block.gpsimd
        def _(pool):
            def const(ins):
                const.n += 1
                ins.then_inc(s["const"], 1)
                pool.wait_ge(s["const"], const.n)
            const.n = 0
            const(pool.memset(ident[:], 0.0))
            const(pool.affine_select(out=ident[:], in_=ident[:], compare_op=ALU.not_equal, fill=1.0, base=0,
                                     pattern=[[-1, P]], channel_multiplier=1))
            const(pool.memset(ones[:], 1.0))
            const(pool.affine_select(out=before[:], in_=ones[:], compare_op=ALU.is_gt, fill=0.0, base=0,
                                     pattern=[[1, P]], channel_multiplier=-1))
            const(pool.memset(pow_half[:], -0.5))
            const(pool.iota(rev[:], pattern=[[-1, E]], base=E, channel_multiplier=0,
                            allow_small_or_imprecise_dtypes=True))
            const(pool.memset(state[:], 0.0))
            const(pool.memset(counts[:], 0.0))
            pool.wait_ge(s["w"], 176)
            const(pool.tensor_scalar(sc_half[:], sc[:, 0, :], 0.5, 0.0, ALU.mult, ALU.add))
            const(pool.tensor_tensor(sc_prod[:], sc_half[:], sc[:, 1, :], ALU.mult))
            const(pool.tensor_tensor(bias[:], rb[:, 0:1], rb[:, 1:2], ALU.add))

            def low_part(c, m):
                if c is not None:
                    wait_apart(pool, s["h2"], HC * c + m + 1, s["const"])
                    if m == 0:
                        wait_apart(pool, s["p_h2"], HC * c, s["const"])
                    pool.tensor_tensor(hT_part[1][1][:, m, :], hT[1][:, m, :],
                                       hT_part[1][0][:, m, :].bitcast(F32), ALU.subtract).then_inc(s["h2_low"], 1)

            def rstd(n, c):
                wait_apart(pool, s["mv" + n], CT * (c + 1), s["const"])
                pool.tensor_scalar(ve[n][:], mv[n][:, :, 1], 1.0, EPS, ALU.mult, ALU.add).then_inc(s["ve" + n], 1)
                wait_apart(pool, s["ve" + n], c + 1, s["const"])
                pool.tensor_tensor(rs[n][:], ve[n][:], pow_half[:], ALU.pow).then_inc(s["rs" + n], 1)

            def step(p, a, c, v, r, h, q, par):
                low_part(c, 0)
                if h is not None:
                    rstd("h", h)
                low_part(c, 1)
                if h is not None:
                    rstd("e", h)
                low_part(c, 2)
                low_part(c, 3)
                if p is not None:
                    rstd("f", p)
                if v is not None:
                    rstd("y", v)
                    rstd("x", v)

            rounds(pool, step)
            pool.wait_ge(s["p_y"], NC)
            pool.memset(hT[2][:], 0.0).then_inc(s["zeros"], 1)

        @block.tensor
        def _(pe):
            def turn4(src, name):
                for k in range(CT):
                    m = pe.transpose(turn[:, k * P:(k + 1) * P], src[:, k], ident[:])
                m.then_inc(s[name], 1)

            def rnn_step(r, t):
                wait(pe, s["step"], STEPS * r + t)
                o = t * B
                prev = (t - 1) % STEPS * B
                pe.matmul(xi[:, o:o + B], wh_sb[:], state[:, prev:prev + B], start=False, stop=(t == STEPS - 1),
                          skip_group_check=True).then_inc(s["p_step"], 1)

            pe.wait_ge(s["w"], 176)
            pe.wait_ge(s["const"], N_CONST)
            pe.wait_ge(s["split"], 20)

            def step(p, a, c, v, r, h, q, par):
                if q is not None:
                    wait(pe, s["xn4"], q + 1)
                    wait(pe, s["hs"], min(q + 2, NC) if isinstance(q, int) else q + 2)
                    turn4(xn4[:], "p_xn4T")
                    wait(pe, s["rank"], q)
                    wait(pe, s["counts"], q)
                    wait(pe, s["xn4T"], q + 1)
                    for k in range(CT):
                        m_ = pe.matmul(route[:, k * E:(k + 1) * E], xn4T[:, k * P:(k + 1) * P], gate_sb[:],
                                       start=True, stop=True)
                    m_.then_inc(s["p_logit"], 1)
                if r is not None:
                    wait(pe, s["xn3"], r + 1)
                    if q is not None:
                        wait(pe, s["xn4T"], q + 1)
                    elif h is not None:
                        wait(pe, s["hs"], h + 1)
                    else:
                        wait(pe, s["xn2T_low"], c + 1)
                    turn4(xn3[:], "p_xn3T")
                slots = iter(range(STEPS))

                def rnn(n=1):
                    if r is not None:
                        for _ in range(n):
                            t = next(slots, None)
                            if t is not None:
                                rnn_step(r, t)

                def recurrence_input():
                    if r is not None:
                        wait(pe, s["xn3T"], r + 1)
                        wait(pe, s["step"], STEPS * r)
                        pe.matmul(xi[:, :], wi_sb[:], xn3T[:], start=True, stop=False,
                                  skip_group_check=True).then_inc(s["p_xi"], 1)

                def ranks():
                    if q is not None:
                        wait(pe, s["onehot"], q + 1)
                        for k in range(CT):
                            for j in range(k):
                                pe.matmul(route[:, 128 + k * E:128 + (k + 1) * E], ones[:], onehot[:, j, :],
                                          start=(j == 0), stop=False)
                            pe.matmul(route[:, 128 + k * E:128 + (k + 1) * E], before[:], onehot[:, k, :],
                                      start=(k == 0), stop=True)
                        for j in range(CT):
                            m_ = pe.matmul(route[:, 256:256 + E], ones[:], onehot[:, j, :], start=(j == 0),
                                           stop=(j == CT - 1))
                        m_.then_inc(s["p_rank"], 1)

                def layer(w, src, first, m):
                    if m == 0:
                        wait(pe, s["h3"], HC * c) if first else wait(pe, s["h2"], HC * (c + 1))
                    elif m >= 2:
                        wait(pe, s["h2" if first else "h3"], HC * c + m - 1)
                    for k in range(HC):
                        if m == 0:
                            wait(pe, s["h1_high" if first else "h2"], HC * c + k + 1)
                        pe.matmul(main[m % 2][:, :], w[0][:, k, m * P:(m + 1) * P], src[0][:, k, :],
                                  start=(k == 0), stop=False)
                        pe.matmul(main[m % 2][:, :], w[1][:, k, m * P:(m + 1) * P], src[0][:, k, :],
                                  start=False, stop=False)
                        if k == 2 and not (first and m == 0):
                            rnn()
                    for k in range(HC):
                        if m == 0:
                            wait(pe, s["h1_low" if first else "h2_low"], HC * c + k + 1)
                        mm = pe.matmul(main[m % 2][:, :], w[0][:, k, m * P:(m + 1) * P], src[1][:, k, :],
                                       start=False, stop=(k == HC - 1))
                    mm.then_inc(s["p_h1" if first else "p_h2"], 1)

                if c is not None:
                    for m in range(HC):
                        layer(h1_part, hT_part[0], True, m)
                        if m == 0:
                            ranks()
                            recurrence_input()
                        else:
                            rnn()
                else:
                    ranks()
                    recurrence_input()
                    rnn(6)
                if a is not None:
                    wait(pe, s["xn2"], a + 1)
                    if r is not None:
                        wait(pe, s["xn3T"], r + 1)
                    else:
                        wait(pe, s["xn2T_low"], a)
                    turn4(xn2[:], "p_xn2T")
                    wait(pe, s["xn2T"], a + 1)
                for m in range(HC):
                    if a is not None:
                        wait(pe, s["h1"], HC * a + m)
                        for w, bank, done in ((w1_part, main[2], "p_a"), (w2_part, main[3], "p_g")):
                            pe.matmul(bank[:, :], w[0][:, m * P:(m + 1) * P], xn2T_part[0][:], start=True, stop=False)
                            pe.matmul(bank[:, :], w[1][:, m * P:(m + 1) * P], xn2T_part[0][:], start=False, stop=False)
                            wait(pe, s["xn2T_low"], a + 1)
                            pe.matmul(bank[:, :], w[0][:, m * P:(m + 1) * P], xn2T_part[1][:],
                                      start=False, stop=True).then_inc(s[done], 1)
                    if c is not None:
                        layer(h2_part, hT_part[1], False, m)
                        rnn()

                def output(k):
                    if c is not None:
                        for m in range(HC):
                            mm = pe.matmul(yp[:, k * P:(k + 1) * P], hT[2][:, m, k * P:(k + 1) * P],
                                           w3_sb[:, m, :], start=(m == 0), stop=(m == HC - 1))
                        if k == CT - 1:
                            mm.then_inc(s["p_y"], 1)

                rnn()
                if c is not None:
                    wait(pe, s["h3"], HC * (c + 1))
                    wait(pe, s["y"], c)
                output(0)
                rnn(STEPS)
                output(1)
                if r is not None:
                    wait(pe, s["step"], STEPS * (r + 1))
                    if a is not None:
                        wait(pe, s["xn2T_low"], a + 1)
                    else:
                        wait(pe, s["xn3T"], r + 1)
                    for k in range(CT):
                        m_ = pe.transpose(turn[:, k * P:(k + 1) * P], state[:, k * P:(k + 1) * P], ident[:])
                    m_.then_inc(s["p_state"], 1)
                output(2)
                output(3)

            rounds(pe, step)

        @block.scalar
        def _(act):
            act.wait_ge(s["const"], N_CONST)

            def step(p, a, c, v, r, h, q, par):
                slots = iter(range(STEPS))

                def rnn(n=1):
                    if r is not None:
                        for _ in range(n):
                            t = next(slots, None)
                            if t is not None:
                                wait(act, s["p_step"], STEPS * r + t + 1)
                                if t == 0:
                                    wait(act, s["p_state"], r)
                                act.activation(state[:, t * B:(t + 1) * B], xi[:, t * B:(t + 1) * B], ACT.Tanh,
                                               bias=bias[:]).then_inc(s["step"], 1)

                if q is not None:
                    wait(act, s["p_xn4T"], q + 1)
                    wait(act, s["p_logit"], q)
                    wait(act, s["kept"], q)
                    act.activation(xn4T[:], turn[:, :], ACT.Copy).then_inc(s["xn4T"], 1)
                if r is not None:
                    wait(act, s["p_xn3T"], r + 1)
                    act.activation(xn3T[:], turn[:, :], ACT.Copy).then_inc(s["xn3T"], 1)

                def turned_top():
                    if q is not None:
                        wait(act, s["top"], q + 1)
                        act.activation(tanh_top[:], top[:], ACT.Tanh, scale=0.5).then_inc(s["tanh_top"], 1)

                if c is not None:
                    for m in range(HC):
                        wait(act, s["p_h1"], HC * c + m + 1)
                        if m == 0:
                            wait(act, s["p_h2"], HC * c)
                            wait(act, s["h2_low"], HC * c)
                        act.activation(hT_part[1][0][:, m, :], main[m % 2][:, :], ACT.Gelu, scale=sc[:, 2, m:m + 1])
                        act.activation(hT[1][:, m, :], main[m % 2][:, :], ACT.Gelu,
                                       scale=sc[:, 2, m:m + 1]).then_inc(s["h2"], 1)
                        if m == 0:
                            turned_top()
                        if m < HC - 1:
                            rnn(2)
                else:
                    rnn(6)
                    turned_top()
                if a is not None:
                    wait(act, s["p_xn2T"], a + 1)
                    wait(act, s["p_g"], HC * a)
                    act.activation(xn2T_part[0][:], turn[:, :], ACT.Copy).then_inc(s["xn2T"], 1)
                for m in range(HC):
                    if a is not None:
                        wait(act, s["p_a"], HC * a + m + 1)
                        wait(act, s["h1"], HC * a + m - 1)
                        act.activation(th[m % 2][:], main[2][:, :], ACT.Tanh,
                                       scale=sc_half[:, m:m + 1]).then_inc(s["tanh"], 1)
                    if c is not None:
                        rnn(2)
                        wait(act, s["p_h2"], HC * c + m + 1)
                        if m == 0:
                            wait(act, s["p_y"], c)
                        act.activation(hT[2][:, m, :], main[m % 2][:, :], ACT.Gelu,
                                       scale=sc[:, 3, m:m + 1]).then_inc(s["h3"], 1)
                    if a is not None:
                        wait(act, s["h1"], HC * a + m + 1)
                        if m == 0:
                            wait(act, s["p_h1"], HC * a)
                        act.activation(hT_part[0][0][:, m, :], hT[0][:, m, :], ACT.Copy).then_inc(s["h1_high"], 1)
                rnn(STEPS)
                if r is not None:
                    wait(act, s["p_state"], r + 1)
                    wait(act, s["x3"], r)
                    act.activation(hs[:].rearrange("p k d -> p (k d)"), turn[:, :], ACT.Copy).then_inc(s["hs"], 1)

            rounds(act, step)

        @block.vector
        def _(dve):
            dve.wait_ge(s["w"], 176)
            pieces = []
            for whole, (high, low) in ((w1_sb, w1_part), (w2_sb, w2_part), (h1_sb, h1_part), (h2_sb, h2_part)):
                if len(whole.shape) == 2:
                    pieces.append((whole[:], high[:], low[:]))
                else:
                    pieces += [(whole[:, k], high[:, k], low[:, k]) for k in range(HC)]
            for k, (whole, high, low) in enumerate(pieces):
                dve.tensor_copy(high, whole).then_inc(s["split"], 1)
                dve.wait_ge(s["split"], 2 * k + 1)
                dve.tensor_tensor(low, whole, high.bitcast(F32), ALU.subtract).then_inc(s["split"], 1)
            dve.wait_ge(s["const"], N_CONST)

            def stats(n, tiles, c):
                for k in range(CT):
                    m = dve.bn_stats(stat[n][:, k, :], tiles(k))
                m.then_inc(s["stat" + n], 1)
                wait_apart(dve, s["stat" + n], c + 1, s["const"])
                for k in range(CT):
                    dve.bn_aggr(mv[n][:, k, :], stat[n][:, k, :]).then_inc(s["mv" + n], 1)

            def apply(n, out, tiles, done, c):
                wait(dve, s["rs" + n], c + 1)
                for k in range(CT):
                    m = dve.tensor_scalar(out[:, k, :], tiles(k), mv[n][:, k, 0:1], rs[n][:, k:k + 1],
                                          ALU.subtract, ALU.mult)
                m.then_inc(s[done], 1)
                dve.wait_ge(s[done], c + 1)

            def step(p, a, c, v, r, h, q, par):
                if q is not None:
                    lg = route[:, 0:CT * E].rearrange("p (k e) -> p k e", e=E)

                    def wide(col):
                        return col[:].rearrange("p (k o) -> p k o", o=1).to_broadcast([P, CT, E])
                    wait(dve, s["p_logit"], q + 1)
                    wait(dve, s["tanh_top"], q)
                    dve.tensor_reduce(top[:], lg, AX.X, ALU.max).then_inc(s["top"], 1)
                    dve.wait_ge(s["top"], q + 1)
                    dve.tensor_tensor(is_top[:], lg, wide(top), ALU.is_ge).then_inc(s["is_top"], 1)
                    dve.wait_ge(s["is_top"], q + 1)
                    dve.tensor_tensor(rtop[:], is_top[:], rev[:].rearrange("p (o e) -> p o e", o=1)
                                      .to_broadcast([P, CT, E]), ALU.mult).then_inc(s["rtop"], 1)
                    dve.wait_ge(s["rtop"], q + 1)
                    dve.tensor_reduce(first[:], rtop[:], AX.X, ALU.max).then_inc(s["first"], 1)
                    dve.wait_ge(s["first"], q + 1)
                    wait(dve, s["p_rank"], q)
                    wait(dve, s["pre_oh"], q)
                    dve.tensor_tensor(onehot[:], rtop[:], wide(first), ALU.is_equal).then_inc(s["onehot"], 1)
                    dve.wait_ge(s["onehot"], q + 1)
                    dve.tensor_copy(part(oh_all, q, CT), onehot[:])
                    dve.tensor_copy(part(xn4T_all, q, CHUNK), xn4T[:]).then_inc(s["kept"], 1)
                    dve.wait_ge(s["tanh_top"], q + 1)
                    dve.tensor_scalar(gate_val[:], tanh_top[:], 0.5, 0.5, ALU.mult, ALU.add)\
                       .then_inc(s["gate_val"], 1)
                    dve.wait_ge(s["gate_val"], q + 1)
                    dve.tensor_tensor(part(xs_all, q, CT), xn4[:], gate_val[:].rearrange("p (k o) -> p k o", o=1)
                                      .to_broadcast([P, CT, D]), ALU.mult).then_inc(s["xs"], 1)
                if h is not None:
                    wait(dve, s["hs"], h + 1)
                    stats("h", lambda k: hs[:, k, :], h)
                    apply("h", hs, lambda k: hs[:, k, :], "hn", h)
                    wait(dve, s["x3_out"], 16 * h)
                    dve.tensor_tensor(x3[:], hs[:], x2[1 - par][:], ALU.add).then_inc(s["x3"], 1)
                    dve.wait_ge(s["x3"], h + 1)
                    stats("e", lambda k: x3[:, k, :], h)
                    wait(dve, s["xs"], h)
                    wait(dve, s["p_xn4T"], h)
                    apply("e", xn4, lambda k: x3[:, k, :], "xn4", h)
                if q is not None:
                    wait(dve, s["p_rank"], q + 1)
                    cnt = counts[:].rearrange("p (o e) -> p o e", o=1).to_broadcast([P, CT, E])
                    dve.wait_ge(s["onehot"], q + 1)
                    wait(dve, s["counts"], q)
                    dve.tensor_tensor(pre[:], route[:, 128:128 + CT * E].rearrange("p (k e) -> p k e", e=E), cnt,
                                      ALU.add).then_inc(s["pre"], 1)
                    dve.wait_ge(s["pre"], q + 1)
                    dve.tensor_tensor(counts[:], counts[:], route[:, 256:256 + E], ALU.add)\
                       .then_inc(s["counts"], 1)
                    dve.tensor_tensor(pre_oh[:], pre[:], onehot[:], ALU.mult).then_inc(s["pre_oh"], 1)
                    dve.wait_ge(s["pre_oh"], q + 1)
                    dve.tensor_reduce(part(rank_all, q, CT), pre_oh[:], AX.X, ALU.add).then_inc(s["rank"], 1)
                def low_part(m):
                    wait(dve, s["h1_high"], HC * a + m + 1)
                    wait(dve, s["p_h1"], HC * a)
                    dve.tensor_tensor(hT_part[0][1][:, m, :], hT[0][:, m, :], hT_part[0][0][:, m, :].bitcast(F32),
                                      ALU.subtract).then_inc(s["h1_low"], 1)

                def ffn_output():
                    if v is not None:
                        wait(dve, s["p_y"], v + 1)
                        dve.tensor_tensor(y[:], yp[:, :].rearrange("p (k d) -> p k d", d=D),
                                          w3s[:].rearrange("p (o d) -> p o d", o=1).to_broadcast([P, CT, D]),
                                          ALU.mult).then_inc(s["y"], 1)
                        dve.wait_ge(s["y"], v + 1)
                        stats("y", lambda k: y[:, k, :], v)

                def second_sum():
                    if v is not None:
                        apply("y", y, lambda k: y[:, k, :], "yn", v)
                        wait(dve, s["xv"], 16 * (v + 1))
                        wait(dve, s["x3"], v - 1)
                        dve.tensor_tensor(x2[1 - par][:], y[:], x1v[:], ALU.add).then_inc(s["x2"], 1)
                        dve.wait_ge(s["x2"], v + 1)
                        stats("x", lambda k: x2[1 - par][:, k, :], v)

                def recurrence_norm():
                    if v is not None:
                        wait(dve, s["p_xn3T"], v)
                        apply("x", xn3, lambda k: x2[1 - par][:, k, :], "xn3", v)

                if a is not None:
                    wait(dve, s["xn2T"], a + 1)
                    wait(dve, s["p_g"], HC * a)
                    dve.tensor_tensor(xn2T_part[1][:], turn[:, :], xn2T_part[0][:].bitcast(F32),
                                      ALU.subtract).then_inc(s["xn2T_low"], 1)
                if p is not None:
                    wait(dve, s[f"xc{par}"], 8 * (p - par) + 16)
                    stats("f", lambda k: x1c[:, k, :], p)
                for m, between in enumerate((ffn_output, second_sum, recurrence_norm, None)):
                    if a is not None:
                        wait(dve, s["tanh"], HC * a + m + 1)
                        dve.scalar_tensor_tensor(out=th[m % 2][:], in0=th[m % 2][:], scalar=1.0,
                                                 in1=main[2][:, :], op0=ALU.add,
                                                 op1=ALU.mult).then_inc(s["ag"], 1)
                        wait(dve, s["p_g"], HC * a + m + 1)
                        wait(dve, s["h1_high"], HC * a)
                        dve.wait_ge(s["ag"], HC * a + m + 1)
                        dve.scalar_tensor_tensor(out=hT[0][:, m, :], in0=main[3][:, :],
                                                 scalar=sc_prod[:, m:m + 1], in1=th[m % 2][:], op0=ALU.mult,
                                                 op1=ALU.mult).then_inc(s["h1"], 1)
                        if m > 0:
                            low_part(m - 1)
                    if between is not None:
                        between()
                if a is not None:
                    low_part(HC - 1)
                if p is not None:
                    wait(dve, s["p_xn2T"], p)
                    apply("f", xn2, lambda k: x1c[:, k, :], "xn2", p)

            rounds(dve, step)


I = 256
IC = I // P
SLOTS = NT + E
OFF = P.bit_length() - 1


def experts_layer(nc, x3_d, sorted_d, routed_d, gate_up, down, sh_gate_up, sh_down, out, keep):
    with ExitStack() as ctx:
        def sb(name, shape, dt=F32):
            return ctx.enter_context(nc.sbuf_tensor(name, shape, dt))

        def ps(name, shape, dt=F32):
            return ctx.enter_context(nc.psum_tensor(name, shape, dt))

        def sem(name):
            return ctx.enter_context(nc.semaphore(name))

        xn4T_all, xs_all, oh_all, rank_all, counts = keep
        position = sb("position", [P, NT], I32)
        ident = sb("ident3", [P, P])
        col = sb("col", [P, 1])
        expert = sb("expert", [1, SLOTS], I32)
        wgu = sb("wgu", [P, E, 2 * I])
        wd = sb("wd", [P, E, IC, D])
        sgu = sb("sgu", [P, 2 * I])
        sd = sb("sd", [P, IC, D])
        full = sb("full", [P, E])
        full_i = sb("full_i", [P, E], I32)
        tiles_i = sb("tiles_i", [P, E], I32)
        tiles = sb("tiles", [P, E])
        upto = sb("upto", [P, E])
        start0 = sb("start0", [P, E])
        start = sb("start", [P, E])
        own = sb("own", [P, 16, E])
        own_start = sb("own_start", [P, NT])
        behind = sb("behind", [P, E])
        owner0 = sb("owner0", [P, 1])
        ones_e = sb("ones_e", [P, E])
        owner = sb("owner", [P, 1])
        silu = [sb(f"silu{i}", [P, CHUNK]) for i in range(2)]
        hid = [sb(f"hid{i}", [P, IC, CHUNK]) for i in range(2)]
        xg = [sb(f"xg{i}", [P, 2, D]) for i in range(2)]
        xgT = [sb(f"xgT{i}", [P, 2 * P]) for i in range(2)]
        act_g = [sb(f"act_g{i}", [P, I]) for i in range(2)]
        hid_g = [sb(f"hid_g{i}", [P, I]) for i in range(2)]
        hid_gT = [sb(f"hid_gT{i}", [P, I]) for i in range(2)]
        yg = [sb(f"yg{i}", [P, 2, D]) for i in range(2)]
        stat = sb("cstat", [P, CT, 6])
        mv = sb("cmv", [P, CT, 2])
        eps = sb("eps", [P, 1])
        sd_y = sb("sd_y", [P, CT])
        rs = sb("crs", [P, CT])
        shared_all = xn4T_all
        x3_all = xs_all
        rows = wgu[:].rearrange("p e i -> p (e i)")
        rt_all = rows[:, 0:NT * D]
        res_all = rows[:, NT * D:2 * NT * D]

        bank = [ps(f"bank{i}", [P, 512]) for i in range(8)]

        names = ("wsh", "wex", "const", "full", "full_i", "tiles_i", "tiles", "upto", "start0", "start",
                 "own", "own_start",
                 "position", "behind", "owner0", "owner", "p_owner", "expert", "p_g", "p_u", "silu", "hid", "p_sh",
                 "sh", "placed", "x3l", "xg0", "xg1", "p_xgT", "xgT", "p_gu", "act_g", "hid_g", "p_hT",
                 "hid_gT", "p_yg", "yg", "yg_out0", "yg_out1", "rt0", "rt1", "rt2", "rt3", "ysum", "stat",
                 "mv", "sd_y", "rs", "yn", "res", "out")
        s = {name: sem("c_" + name) for name in names}
        N_CONST = 5
        ctx.callback(clear, nc, list(s.values()))
        block = ctx.enter_context(nc.Block())

        sorted_t = sorted_d.rearrange("(j k p) d -> j p k d", k=2, p=P)
        routed_t = routed_d.rearrange("(j k p) d -> j p k d", k=2, p=P)
        out_v = out.rearrange("b (c k u) d -> c u b k d", k=CT, u=P // B)
        PAIRS = SLOTS // 2

        def chunk_of(ap, c):
            return ap[c] if isinstance(c, int) else ap[bass.ds(c, 1)].rearrange("o p k d -> p (o k) d")

        def chunk_rounds(eng, step):
            step(0, None, 0)
            step(1, 0, 1)
            with eng.Fori(0, (NC - 2) // 2) as i:
                for par in range(2):
                    step(2 * i + (2 + par), 2 * i + (1 + par), par)
            step(None, NC - 1, 0)

        def slot_rounds(eng, step):
            step(-1, 0, 1)
            step(0, 1, 0)
            step(1, 2, 1)
            with eng.Fori(0, (PAIRS - 4) // 2) as i:
                for par in range(2):
                    step(2 * i + (2 + par), 2 * i + (3 + par), par)
            step(PAIRS - 2, PAIRS - 1, 0)
            step(PAIRS - 1, None, 1)
            step(PAIRS, None, 0)

        def tiles_of(m):
            for i in range(2):
                t = 2 * m + i
                if isinstance(t, int):
                    yield t, i, 0 <= t < SLOTS, 1 <= t <= SLOTS, 2 <= t <= SLOTS + 1
                else:
                    yield t, i, True, True, True

        @block.sync
        def _(sp):
            sp.dma_start(sgu[:], sh_gate_up).then_inc(s["wsh"], 16)
            sp.dma_start(sd[:], sh_down.rearrange("(c p) d -> p c d", p=P)).then_inc(s["wsh"], 16)
            for e in range(0, E, 8):
                sp.dma_start(wgu[:, e:e + 8, :], gate_up[e:e + 8].rearrange("e d i -> d e i")).then_inc(s["wex"], 16)
                sp.dma_start(wd[:, e:e + 8], down[e:e + 8].rearrange("e (c p) d -> p e c d", p=P))\
                  .then_inc(s["wex"], 16)
            sp.wait_ge(s["placed"], 16 * NT)
            sp.dma_start(xg[0][:], sorted_t[0]).then_inc(s["xg0"], 16)
            sp.dma_start(xg[1][:], sorted_t[1]).then_inc(s["xg1"], 16)
            sp.dma_start(x3_all[:], x3_d.rearrange("(j p) d -> p j d", p=P)).then_inc(s["x3l"], 16)

            def step(m, a, par):
                if not isinstance(m, int) or 0 <= m < PAIRS - 2:
                    wait(sp, s["p_xgT"], m + 1)
                    sp.dma_start(xg[par][:], chunk_of(sorted_t, m + 2)).then_inc(s[f"xg{par}"], 16)
                if not isinstance(m, int) or m >= 2:
                    wait(sp, s["yg"], 2 * (m - 1))
                    sp.dma_start(chunk_of(routed_t, m - 2), yg[par][:]).then_inc(s[f"yg_out{par}"], 16)

            slot_rounds(sp, step)
            sp.wait_ge(s["yg"], SLOTS)
            sp.dma_start(routed_t[PAIRS - 1], yg[1][:]).then_inc(s["yg_out1"], 16)

            def last(c):
                wait(sp, s["res"], c + 1)
                for u in range(P // B):
                    dst = out_v[c, u] if isinstance(c, int) else out_v[bass.ds(c, 1), u]\
                        .rearrange("o b k d -> (o b) k d")
                    sp.dma_start(dst, part(res_all, c, CHUNK)[u * B:(u + 1) * B]
                                 .rearrange("b (k d) -> b k d", d=D)).then_inc(s["out"], 16)
            last(0)
            with sp.Fori(0, NC - 1) as c:
                last(c + 1)
            sp.wait_ge(s["out"], 16 * NC * (P // B))

        @block.gpsimd
        def _(pool):
            def const(ins):
                const.n += 1
                ins.then_inc(s["const"], 1)
                pool.wait_ge(s["const"], const.n)
            const.n = 0
            const(pool.memset(ident[:], 0.0))
            const(pool.affine_select(out=ident[:], in_=ident[:], compare_op=ALU.not_equal, fill=1.0, base=0,
                                     pattern=[[-1, P]], channel_multiplier=1))
            const(pool.memset(eps[:], EPS))
            const(pool.memset(ones_e[:], 1.0))
            const(pool.iota(col[:], pattern=[[0, 1]], base=0, channel_multiplier=1,
                            allow_small_or_imprecise_dtypes=True))
            pool.wait_ge(s["position"], 1)
            for k in range(NT):
                pool.indirect_dma_start(out=sorted_d[:, :], out_offset=bass.IndirectOffsetOnAxis(
                    ap=position[:, k:k + 1], axis=0), in_=xs_all[:, k, :], in_offset=None)\
                    .then_inc(s["placed"], 16)
            pool.wait_ge(s["placed"], 16 * NT)
            for par in range(2):
                pool.wait_ge(s[f"yg_out{par}"], 8 * PAIRS)

            for c in range(NC):
                wait(pool, s["ysum"], c - 3)
                for k in range(c * CT, (c + 1) * CT):
                    pool.indirect_dma_start(out=rt_all[:, k * D:(k + 1) * D], out_offset=None, in_=routed_d[:, :],
                                            in_offset=bass.IndirectOffsetOnAxis(ap=position[:, k:k + 1], axis=0))\
                        .then_inc(s[f"rt{c % 4}"], 16)

        @block.tensor
        def _(pe):
            pe.wait_ge(s["wsh"], 32)
            pe.wait_ge(s["const"], N_CONST)
            pe.wait_ge(s["owner"], 1)
            pe.matmul(bank[7][0:1, 0:SLOTS], owner[:], ident[:, 0:SLOTS], start=True, stop=True)\
              .then_inc(s["p_owner"], 1)

            def shared(c, d, par):
                if c is not None:
                    for m in range(IC):
                        wait(pe, s["hid"], IC * (c - 1) + m + 1)
                        pe.matmul(bank[2 * m][:, :], sgu[:, m * P:(m + 1) * P], part(xn4T_all, c, CHUNK),
                                  start=True, stop=True).then_inc(s["p_g"], 1)
                        pe.matmul(bank[2 * m + 1][:, :], sgu[:, I + m * P:I + (m + 1) * P],
                                  part(xn4T_all, c, CHUNK), start=True, stop=True).then_inc(s["p_u"], 1)
                if d is not None:
                    wait(pe, s["hid"], IC * (d + 1))
                    wait(pe, s["sh"], d)
                    for k in range(CT):
                        for m in range(IC):
                            mm = pe.matmul(bank[4][:, k * P:(k + 1) * P], hid[1 - par][:, m, k * P:(k + 1) * P],
                                           sd[:, m, :], start=(m == 0), stop=(m == IC - 1))
                    mm.then_inc(s["p_sh"], 1)
            chunk_rounds(pe, shared)

            pe.wait_ge(s["wex"], 16 * (E // 4))
            pe.wait_ge(s["expert"], 1)
            pe.wait_ge(s["sh"], NC)

            def owner_of(t):
                return pe.value_load(expert[0:1, t:t + 1] if isinstance(t, int) else expert[0:1, bass.ds(t, 1)],
                                     min_val=0, max_val=E - 1)

            owners = {}

            def step(m, a, par):
                for t, i, now, one, two in tiles_of(m):
                    if now:
                        last = owners.get(i)
                        e = owners[i] = owner_of(t)
                        wait(pe, s["xgT"], m + 1)
                        wait(pe, s["hid_g"], t - 3)
                        pe.matmul(bank[2 * par + i][:, :], xgT[par][:, i * P:(i + 1) * P],
                                  wgu[:, bass.ds(e, 1), :].rearrange("p o i -> p (o i)"),
                                  start=True, stop=True).then_inc(s["p_gu"], 1)
                    if two:
                        e = last if par and now else owner_of(t - 2)
                        wait(pe, s["hid_gT"], t - 1)
                        wait(pe, s["yg"], t - 3)
                        for k in range(IC):
                            mm = pe.matmul(bank[6 + i][:, 0:D], hid_gT[i][:, k * P:(k + 1) * P],
                                           wd[:, bass.ds(e, 1), k, :].rearrange("p o d -> p (o d)"),
                                           start=(k == 0), stop=(k == IC - 1))
                        mm.then_inc(s["p_yg"], 1)
                    if one:
                        wait(pe, s["hid_g"], t)
                        wait(pe, s["hid_gT"], t - 1)
                        for k in range(IC):
                            mm = pe.transpose(bank[4][:, k * P:(k + 1) * P], hid_g[1 - i][:, k * P:(k + 1) * P],
                                              ident[:])
                        mm.then_inc(s["p_hT"], 1)
                    if a is not None and i == 0:
                        wait(pe, s[f"xg{1 - par}"], 8 * (m + par) + 16)
                        wait(pe, s["xgT"], m + 1)
                        for k in range(2):
                            mm = pe.transpose(bank[5][:, k * P:(k + 1) * P], xg[1 - par][:, k, :], ident[:])
                        mm.then_inc(s["p_xgT"], 1)

            slot_rounds(pe, step)

        @block.scalar
        def _(act):
            def shared(c, d, par):
                if d is not None:
                    wait(act, s["p_sh"], d + 1)
                    wait(act, s["p_u"], IC * (d + 1))
                    act.activation(part(shared_all, d, CHUNK), bank[4][:, :], ACT.Copy).then_inc(s["sh"], 1)
                if c is not None:
                    for m in range(IC):
                        wait(act, s["p_g"], IC * c + m + 1)
                        wait(act, s["hid"], IC * (c - 1) + m + 1)
                        act.activation(silu[m][:], bank[2 * m][:, :], ACT.Silu).then_inc(s["silu"], 1)
            chunk_rounds(act, shared)

            def step(m, a, par):
                for t, i, now, one, two in tiles_of(m):
                    if now:
                        wait(act, s["p_gu"], t + 1)
                        wait(act, s["hid_g"], t - 1)
                        act.activation(act_g[i][:], bank[2 * par + i][:, 0:I], ACT.Silu).then_inc(s["act_g"], 1)
                    if one:
                        wait(act, s["p_hT"], t)
                        wait(act, s["p_yg"], t - 2)
                        act.activation(hid_gT[1 - i][:], bank[4][:, 0:I], ACT.Copy).then_inc(s["hid_gT"], 1)

            slot_rounds(act, step)

            def last(c):
                wait(act, s["mv"], CT * (c + 1))
                wait(act, s["rs"], c)
                act.activation(sd_y[:], mv[:, :, 1], ACT.Sqrt, bias=eps[:]).then_inc(s["sd_y"], 1)
            last(0)
            with act.Fori(0, NC - 1) as c:
                last(c + 1)

        @block.vector
        def _(dve):
            dve.wait_ge(s["const"], N_CONST)

            def did(ins, name):
                ins.then_inc(s[name], 1)
                dve.wait_ge(s[name], 1)
            did(dve.tensor_scalar(full[:], counts[:], float(P - 1), None, ALU.add), "full")
            did(dve.tensor_copy(full_i[:], full[:]), "full_i")
            did(dve.tensor_single_scalar(tiles_i[:], full_i[:], OFF, ALU.arith_shift_right), "tiles_i")
            did(dve.tensor_copy(tiles[:], tiles_i[:]), "tiles")
            did(dve.tensor_tensor_scan(out=upto[:], data0=ones_e[:], data1=tiles[:], initial=0.0, op0=ALU.mult,
                                       op1=ALU.add), "upto")
            did(dve.tensor_tensor(start0[:], upto[:], tiles[:], ALU.subtract), "start0")
            did(dve.tensor_scalar(start[:], start0[:], float(P), None, ALU.mult), "start")
            did(dve.tensor_scalar(behind[:], upto[:], col[:, 0:1], None, ALU.is_le), "behind")
            did(dve.tensor_reduce(owner0[:], behind[:], AX.X, ALU.add), "owner0")
            did(dve.tensor_scalar(owner[:], owner0[:], float(E - 1), None, ALU.min), "owner")
            for k in range(0, NT, 16):
                dve.tensor_tensor(own[:], oh_all[:, k:k + 16, :], start[:].rearrange("p (o e) -> p o e", o=1)
                                  .to_broadcast([P, 16, E]), ALU.mult).then_inc(s["own"], 1)
                dve.wait_ge(s["own"], k // 16 + 1)
                dve.tensor_reduce(own_start[:, k:k + 16], own[:], AX.X, ALU.add).then_inc(s["own_start"], 1)
                dve.wait_ge(s["own_start"], k // 16 + 1)
            did(dve.tensor_tensor(position[:], own_start[:], rank_all[:], ALU.add), "position")
            dve.wait_ge(s["p_owner"], 1)
            did(dve.tensor_copy(expert[:], bank[7][0:1, 0:SLOTS]), "expert")

            def shared(c, d, par):
                if c is not None:
                    for m in range(IC):
                        wait(dve, s["silu"], IC * c + m + 1)
                        wait(dve, s["p_u"], IC * c + m + 1)
                        wait(dve, s["p_sh"], c - 1)
                        dve.tensor_tensor(hid[par][:, m, :], bank[2 * m + 1][:, :], silu[m][:], ALU.mult)\
                           .then_inc(s["hid"], 1)
            chunk_rounds(dve, shared)

            def step(m, a, par):
                for t, i, now, one, two in tiles_of(m):
                    if two:
                        wait(dve, s["p_yg"], t - 1)
                        if i == 0:
                            wait(dve, s[f"yg_out{1 - par}"], 8 * (m - 1 - (1 - par)))
                        dve.tensor_copy(yg[1 - par][:, i, :], bank[6 + i][:, 0:D]).then_inc(s["yg"], 1)
                    if now:
                        wait(dve, s["act_g"], t + 1)
                        wait(dve, s["p_hT"], t - 1)
                        dve.tensor_tensor(hid_g[i][:], bank[2 * par + i][:, I:2 * I], act_g[i][:], ALU.mult)\
                           .then_inc(s["hid_g"], 1)
                    if a is not None and i == 0:
                        wait(dve, s["p_xgT"], m + 2)
                        wait(dve, s["p_gu"], 2 * m)
                        dve.tensor_copy(xgT[1 - par][:], bank[5][:, 0:2 * P]).then_inc(s["xgT"], 1)

            slot_rounds(dve, step)

            dve.wait_ge(s["x3l"], 16)
            dve.wait_ge(s["sh"], NC)

            def last(c, i, turn):
                def tile(ap, k):
                    return part(ap, c * CT + k, D)
                wait(dve, s[f"rt{i}"], 16 * CT * (turn + 1))
                dve.tensor_tensor(part(rt_all, c, CHUNK), part(rt_all, c, CHUNK), part(shared_all, c, CHUNK),
                                  ALU.add).then_inc(s["ysum"], 1)
                dve.wait_ge(s["ysum"], c + 1)
                for k in range(CT):
                    m = dve.bn_stats(stat[:, k, :], tile(rt_all, k))
                m.then_inc(s["stat"], 1)
                wait_apart(dve, s["stat"], c + 1, s["const"])
                for k in range(CT):
                    dve.bn_aggr(mv[:, k, :], stat[:, k, :]).then_inc(s["mv"], 1)
                wait(dve, s["sd_y"], c + 1)
                dve.reciprocal(rs[:], sd_y[:]).then_inc(s["rs"], 1)
                dve.wait_ge(s["rs"], c + 1)
                for k in range(CT):
                    m = dve.tensor_scalar(tile(res_all, k), tile(rt_all, k), mv[:, k, 0:1], rs[:, k:k + 1],
                                          ALU.subtract, ALU.mult)
                m.then_inc(s["yn"], 1)
                dve.wait_ge(s["yn"], c + 1)
                dve.tensor_tensor(part(res_all, c, CHUNK), part(res_all, c, CHUNK),
                                  part(x3_all[:].rearrange("p k d -> p (k d)"), c, CHUNK),
                                  ALU.add).then_inc(s["res"], 1)
            for c in range(4):
                last(c, c, 0)
            with dve.Fori(0, NC // 4 - 1) as j:
                for i in range(4):
                    last(4 * j + (4 + i), i, j + 1)


def build(nc, t, out):
    def dram(name, shape):
        return nc.dram_tensor(name, shape, F32).ap()

    x1_d = dram("x1_d", (T, B, D))
    x3_d = dram("x3_d", (T * B, D))
    sorted_d = dram("sorted_d", (SLOTS * P, D))
    routed_d = dram("routed_d", (SLOTS * P, D))
    attention_layer(nc, t["x"], t["w_qk"], t["w_v"], t["w_rot"], t["w_out"], t["bonus0"], t["bonus1"], x1_d)
    with ExitStack() as ctx:
        def sb(name, shape, dt=F32):
            return ctx.enter_context(nc.sbuf_tensor(name, shape, dt))
        keep = (sb("xn4T_all", [P, NT * P]), sb("xs_all", [P, NT, D]), sb("oh_all", [P, NT, E], BF16),
                sb("rank_all", [P, NT]), sb("counts", [P, E]))
        mixing_layers(nc, x1_d, x3_d, t["w1"], t["w2"], t["h1"], t["h2"], t["w3"], t["scales"], t["w3_s"],
                      t["wi"], t["wh"], t["rnn_bias"], t["gate"], sorted_d, keep)
        experts_layer(nc, x3_d, sorted_d, routed_d, t["gate_up"], t["down"], t["sh_gate_up"],
                      t["sh_down"], out, keep)


def host_layout(np, i):
    w_rot = np.zeros((P, P), np.float32)
    for h in range(HEADS):
        q = slice(DH * h, DH * (h + 1))
        k = slice(DH * (HEADS + h), DH * (HEADS + h + 1))
        w_rot[q, q] = i["L0_attn_W_nudge"][h]
        w_rot[k, k] = i["L0_attn_simple_roots"].T
    bonus = i["L0_attn_chamber_bonus"].reshape(1, HEADS, 8, 2)
    return {
        "x": i["L0_attn_x"],
        "w_qk": np.concatenate([i["L0_attn_W_q"].T, i["L0_attn_W_k"].T], 1),
        "w_v": i["L0_attn_W_v"].T,
        "w_rot": w_rot,
        "w_out": i["L0_attn_W_out"].T,
        "bonus0": bonus[..., 0],
        "bonus1": bonus[..., 1],
        "w1": i["L0_ffn_w1_w"].T,
        "w2": i["L0_ffn_w2_w"].T,
        "h1": i["L0_ffn_h1_w"].T,
        "h2": i["L0_ffn_h2_w"].T,
        "w3": i["L0_ffn_w3_w"].T,
        "scales": np.stack([i[f"L0_ffn_{k}_s"].reshape(HC, P) for k in ("w1", "w2", "h1", "h2")]).transpose(2, 0, 1),
        "w3_s": i["L0_ffn_w3_s"].reshape(1, D),
        "wi": i["L1_attn_Wi"].T,
        "wh": i["L1_attn_Wh"].T,
        "rnn_bias": np.stack([i["L1_attn_bi"], i["L1_attn_bh"]], 1),
        "gate": i["L1_ffn_gate_w"],
        "sh_gate_up": np.concatenate([i["L1_ffn_shared_gate_w"], i["L1_ffn_shared_up_w"]], 1),
        "sh_down": i["L1_ffn_shared_down_w"],
        "gate_up": np.concatenate([i["L1_ffn_routed_gate_w"], i["L1_ffn_routed_up_w"]], 2),
        "down": i["L1_ffn_routed_down_w"],
    }


def kernel(**inputs):
    import numpy as np
    import concourse.bacc as bacc
    from concourse.bass_utils import run_bass_kernel_spmd

    nc = bacc.Bacc("TRN2", target_bir_lowering=False, num_devices=1)
    arrays, tensors = {}, {}
    for name, a in host_layout(np, {k: np.asarray(v) for k, v in inputs.items()}).items():
        a = np.ascontiguousarray(a)
        arrays[f"in_{name}"] = a
        tensors[name] = nc.dram_tensor(f"in_{name}", a.shape, mybir.dt.from_np(a.dtype), kind="ExternalInput").ap()
    out = nc.dram_tensor("out_0", (B, T, D), F32, kind="ExternalOutput").ap()
    build(nc, tensors, out)
    r = run_bass_kernel_spmd(nc, [arrays], core_ids=[0])
    return r.results[0]["out_0"]
```
